# Optimizing a Trainium2 kernel written in Bass

```python
import numpy as np
import jax
import jax.numpy as jnp

def _softmax(x, axis=-1):
    return jax.nn.softmax(x, axis=axis)

def _gelu(x):
    return jax.nn.gelu(x, approximate=True)

def _silu(x):
    return jax.nn.silu(x)

def _sigmoid(x):
    return jax.nn.sigmoid(x)

def _layernorm(x, axis=-1, eps=1e-05):
    m = jnp.mean(x, axis=axis, keepdims=True)
    v = jnp.var(x, axis=axis, keepdims=True)
    return (x - m) / jnp.sqrt(v + eps)

def _scatter_add(tgt, idx, src, axis=0):
    return tgt.at[idx].add(src)

def _segment_sum(src, seg, n):
    return jax.ops.segment_sum(src, seg, n)
kernel_name = 'mk_adj_resnorm_d4_adj_r2_50ebd6'

def setup_inputs(seed: int=0):
    np.random.seed(seed)
    _w = jnp.asarray

    def _rec_inputs():
        import jax
        import jax.numpy as jnp
        _gk = jax.random.key(seed)
        x = -8.776e-05 + 1 * jax.random.normal(jax.random.fold_in(_gk, 1), (2048, 256), jnp.float32)
        _w = (1.0 + jnp.arange(2048, dtype=jnp.float32)) ** (-0.5)
        _w = _w / _w.mean()
        _pij = jnp.clip(0.000976562 * _w[:, None] * _w[None, :], 0.0, 1.0)
        _a = jax.random.uniform(jax.random.fold_in(_gk, 2), (2048, 2048)) < _pij
        _a = jnp.logical_or(_a, jnp.eye(2048, dtype=bool))
        _af = _a.astype(jnp.float32)
        _af = _af * jax.random.uniform(jax.random.fold_in(_gk, 3), (2048, 2048), jnp.float32, 0.05, 1)
        adj = _af
        return (x, adj)
    x, adj = _rec_inputs()

    def _L0_gnn_setup():
        import jax, jax.numpy as jnp
        import numpy as np
        N = 5000
        IN_F = 256
        OUT_F = 256
        key = jax.random.key(seed)
        k1, k2, k3 = jax.random.split(key, 3)
        x = jax.random.normal(k1, (N, IN_F), dtype=jnp.float32)
        adj = jax.random.uniform(k2, (N, N), dtype=jnp.float32)
        stdv = 1.0 / np.sqrt(OUT_F)
        weight = jax.random.uniform(k3, (IN_F, OUT_F), dtype=jnp.float32, minval=-stdv, maxval=stdv)
        t = jnp.ones((1,), dtype=jnp.float32)
        return {'x': x, 'adj': adj, 't': t, 'weight': weight}
    _L0_gnn_all = _L0_gnn_setup()
    _L0_gnn_in = {k: v for k, v in _L0_gnn_all.items() if k in ('t', 'weight')}
    del _L0_gnn_all

    def _L1_gnn_setup():
        import jax, jax.numpy as jnp
        import numpy as np
        N = 4096
        D = 256
        EPS = 1e-12
        key = jax.random.key(seed)
        k1, k2 = jax.random.split(key)
        cur = jax.random.normal(k1, (N, D), dtype=jnp.float32)
        incidence_m = jax.random.normal(k2, (N, N), dtype=jnp.float32)
        return {'cur': cur, 'incidence_m': incidence_m}
    _L1_gnn_all = _L1_gnn_setup()
    _L1_gnn_in = {k: v for k, v in _L1_gnn_all.items() if k in ()}
    del _L1_gnn_all

    def _L2_gnn_setup():
        import jax, jax.numpy as jnp
        import numpy as np
        N = 1024
        HID = 256
        H = 8
        key = jax.random.key(seed)
        ks = jax.random.split(key, 8)
        x = jax.random.normal(ks[0], (N, HID), dtype=jnp.float32)
        sp = jax.random.normal(ks[1], (N, N), dtype=jnp.float32)
        zero_mask = jax.random.uniform(ks[2], (N, N)) < 0.2
        spatial_encoding = jnp.where(zero_mask, 0.0, sp)
        edge_encoding = jax.random.normal(ks[3], (N, N), dtype=jnp.float32)
        s = 1.0 / np.sqrt(HID)
        Wq = jax.random.normal(ks[4], (HID, HID * H), dtype=jnp.float32) * s
        Wk = jax.random.normal(ks[5], (HID, HID * H), dtype=jnp.float32) * s
        Wv = jax.random.normal(ks[6], (HID, HID * H), dtype=jnp.float32) * s
        Wout = jax.random.normal(ks[7], (HID * H, HID), dtype=jnp.float32) * (1.0 / np.sqrt(HID * H))
        return {'x': x, 'spatial_encoding': spatial_encoding, 'edge_encoding': edge_encoding, 'Wq': Wq, 'Wk': Wk, 'Wv': Wv, 'Wout': Wout}
    _L2_gnn_all = _L2_gnn_setup()
    _L2_gnn_in = {k: v for k, v in _L2_gnn_all.items() if k in ('Wq', 'Wk', 'Wv', 'Wout')}
    del _L2_gnn_all

    def _L3_gnn_setup():
        import jax, jax.numpy as jnp
        import numpy as np
        IN_F = 256
        OUT_F = 256
        N = 4096
        key = jax.random.key(seed)
        k1, k2, k3 = jax.random.split(key, 3)
        x = jax.random.normal(k1, (N, IN_F), dtype=jnp.float32)
        graph = jax.random.uniform(k2, (N, N), dtype=jnp.float32)
        std = float(np.sqrt(2.0 / (IN_F + OUT_F)))
        weight = jax.random.normal(k3, (IN_F, OUT_F), dtype=jnp.float32) * std
        bias = jnp.zeros((OUT_F,), dtype=jnp.float32)
        return {'x': x, 'graph': graph, 'weight': weight, 'bias': bias}
    _L3_gnn_all = _L3_gnn_setup()
    _L3_gnn_in = {k: v for k, v in _L3_gnn_all.items() if k in ('weight', 'bias')}
    del _L3_gnn_all
    return {'x': x, 'adj': adj, 'L0_gnn_t': _L0_gnn_in['t'], 'L0_gnn_weight': _L0_gnn_in['weight'], 'L2_gnn_Wq': _L2_gnn_in['Wq'], 'L2_gnn_Wk': _L2_gnn_in['Wk'], 'L2_gnn_Wv': _L2_gnn_in['Wv'], 'L2_gnn_Wout': _L2_gnn_in['Wout'], 'L3_gnn_weight': _L3_gnn_in['weight'], 'L3_gnn_bias': _L3_gnn_in['bias']}

def reference(x, adj, L0_gnn_t, L0_gnn_weight, L2_gnn_Wq, L2_gnn_Wk, L2_gnn_Wv, L2_gnn_Wout, L3_gnn_weight, L3_gnn_bias):
    import jax
    import jax.numpy as jnp

    def _L0_gnn_ref(x, adj, t, weight):
        import jax, jax.numpy as jnp
        import numpy as np
        N = 5000
        IN_F = 256
        OUT_F = 256
        ts = t[0]
        support = x @ weight
        return (1.0 - ts) * support + ts * (adj @ support)

    def _L1_gnn_ref(cur, incidence_m):
        import jax, jax.numpy as jnp
        import numpy as np
        N = 4096
        D = 256
        EPS = 1e-12
        mask = incidence_m > 0
        head = jax.lax.stop_gradient(mask.astype(incidence_m.dtype))
        head = head / jnp.maximum(jnp.sqrt(jnp.sum(head * head, axis=-1, keepdims=True)), EPS)
        inc = incidence_m + head
        edge_fea = inc @ cur
        edge_degree = jnp.sum(inc, axis=-1, keepdims=True)
        return edge_fea / edge_degree

    def _L2_gnn_ref(x, spatial_encoding, edge_encoding, Wq, Wk, Wv, Wout):
        import jax, jax.numpy as jnp
        import numpy as np
        N = 1024
        HID = 256
        H = 8
        n, d = x.shape
        h = Wq.shape[1] // d
        scale = d ** (-0.5)
        q = (x @ Wq).reshape(h, n, d)
        k = (x @ Wk).reshape(h, n, d)
        v = (x @ Wv).reshape(h, n, d)
        a = jnp.einsum('hnd,hmd->hnm', q, k) * scale
        a = a + spatial_encoding + edge_encoding
        mask = spatial_encoding == 0.0
        a = jnp.where(mask, -1000000.0, a)
        a = jax.nn.softmax(a, axis=-1)
        a = jnp.where(mask, 0.0, a)
        out = jnp.einsum('hnm,hmd->hnd', a, v)
        out = out.transpose(1, 0, 2).reshape(n, h * d)
        return out @ Wout

    def _L3_gnn_ref(x, graph, weight, bias):
        import jax, jax.numpy as jnp
        import numpy as np
        IN_F = 256
        OUT_F = 256
        N = 4096
        gt = graph.T
        deg = jnp.sum(gt, axis=1)
        d_inv_sqrt = deg ** (-0.5)
        norm = d_inv_sqrt[:, None] * gt * d_inv_sqrt[None, :]
        h = x @ weight
        y = norm @ h + bias
        return y
    x = _layernorm(x + _L0_gnn_ref(x, adj, L0_gnn_t, L0_gnn_weight), axis=-1)
    x = _layernorm(x + _L1_gnn_ref(x, adj), axis=-1)
    x = _layernorm(x + _L2_gnn_ref(x, adj, adj, L2_gnn_Wq, L2_gnn_Wk, L2_gnn_Wv, L2_gnn_Wout), axis=-1)
    x = _layernorm(x + _L3_gnn_ref(x, adj, L3_gnn_weight, L3_gnn_bias), axis=-1)
    return x

_drawn_inputs = setup_inputs


def setup_inputs(seed=0):
    import zlib

    import numpy as np

    out = dict(_drawn_inputs(seed))
    spreads = {'L3_gnn_bias': (0.0, 0.1)}
    factors = {}
    for name, (base, spread) in spreads.items():
        noise = np.random.default_rng([zlib.crc32(name.encode()), seed]).standard_normal(out[name].shape)
        drawn = base * np.exp(spread * noise) if base else spread * noise
        out[name] = jnp.asarray(drawn.astype(out[name].dtype))
    for name, factor in factors.items():
        out[name] = (out[name] * factor).astype(out[name].dtype)
    return out
```

```python
from contextlib import ExitStack

import concourse.bass as bass
from concourse import mybir

ALU = mybir.AluOpType
ACT = mybir.ActivationFunctionType
AX_X = mybir.AxisListType.X
F32 = mybir.dt.float32
F32R = mybir.dt.float32r
BF16 = mybir.dt.bfloat16
U8 = mybir.dt.uint8

P = 128
BANK = 512
LN_EPS = 1e-5
NORM_EPS = 1e-12
MASKED = -1.0e6
NEVER = -1.0e30
DMA = 16
START = 1


def plain(ap):
    return ap.bitcast(F32)


def graph_layers(nc, x, adj, mix, w0, wq, wk, wv, wout, w3, bias, out):
    N, D = x.shape
    T = N // P
    K = D // P
    H = wq.shape[1] // D
    C = H
    R = N // H
    PAIRS = T // 2
    HALF = N // 2
    GROUPS = N // BANK
    TPB = BANK // P
    assert K == 2 and R == 2 * P and C * R == N and C == PAIRS and 2 * D == BANK

    bias_scratch = nc.dram_tensor("bias_scratch", (N, N), F32, kind="Internal").ap()
    wvt_scratch = nc.dram_tensor("wvt_scratch", (C, P, K, D), F32, kind="Internal").ap()
    x1_scratch = nc.dram_tensor("x1_scratch", (N, D), F32, kind="Internal").ap()
    x2_scratch = nc.dram_tensor("x2_scratch", (N, D), F32, kind="Internal").ap()
    zeros_scratch = nc.dram_tensor("zeros_scratch", (N, 1), F32, kind="Internal").ap()

    whole = ExitStack()

    def sb(scope, name, shape, dtype=F32):
        return scope.enter_context(nc.sbuf_tensor(name, shape, dtype))

    spent, fresh, of_block = [], [], []

    def sem(scope, name):
        made = scope.enter_context(nc.semaphore(name))
        spent.append(made)
        fresh.append(made)
        return made

    def next_block():
        of_block[:] = fresh
        fresh.clear()
        return nc.Block()

    def start(engine, n, of):
        for s in of_block[n::of]:
            engine.sem_inc(s, START)

    def clear_spent():
        numbers = sorted(s.num for s in spent)
        with nc.Block() as block:
            @block.gpsimd
            def _(pool):
                start = numbers[0]
                for n, after in zip(numbers, numbers[1:] + [None]):
                    if after != n + 1:
                        pool.sem_clear(range(start, n + 1))
                        start = after
        spent.clear()

    def sems(scope, name, n=2):
        return [sem(scope, f"{name}{i}") for i in range(n)]

    def first_apart(engine, count):
        yield 0, True
        with engine.Fori(1, count) as i:
            yield i, False

    with whole:
        ident = sb(whole, "ident", [P, P])
        ones = sb(whole, "ones", [P, P])
        eps_col = sb(whole, "eps_col", [P, 1])
        masked_col = sb(whole, "masked_col", [P, 1])
        positives = sb(whole, "positives", [P, T])
        zeros = sb(whole, "zeros", [P, T])
        row_sum = sb(whole, "row_sum", [P, T])
        col_sum = sb(whole, "col_sum", [P, T, 2])
        stats = sb(whole, "stats", [P, 2, TPB, 6])
        mean_var = sb(whole, "mean_var", [P, 2, TPB, 2])
        deviation = sb(whole, "deviation", [P, 2, TPB])
        inv_dev = sb(whole, "inv_dev", [P, 2, TPB])

        class Projection:
            def __init__(self, scope, tag, banks, w_dram, y):
                self.xs = [sb(scope, f"{tag}_xs{k}", [P, D]) for k in range(2)]
                self.xT_high = [sb(scope, f"{tag}_xT_high{k}", [P, K, P], F32R) for k in range(2)]
                self.xT_low = [sb(scope, f"{tag}_xT_low{k}", [P, K, P], F32R) for k in range(2)]
                self.w = sb(scope, f"{tag}_w", [P, K, D])
                self.w_high = sb(scope, f"{tag}_w_high", [P, K, D], F32R)
                self.w_low = sb(scope, f"{tag}_w_low", [P, K, D], F32R)
                self.xT_bank, self.y_bank = banks
                self.w_dram, self.y = w_dram, y
                self.w_in = sem(scope, f"{tag}_w_in")
                self.w_high_done = sem(scope, f"{tag}_w_high_done")
                self.w_low_done = sem(scope, f"{tag}_w_low_done")
                self.xs_in = sems(scope, f"{tag}_xs_in")
                self.xT_full = sems(scope, f"{tag}_xT_full")
                self.high_done = sems(scope, f"{tag}_high_done")
                self.low_done = sems(scope, f"{tag}_low_done")
                self.y_full = sems(scope, f"{tag}_y_full")
                self.y_done = sems(scope, f"{tag}_y_done")

            def load_weight(self, sp):
                sp.dma_start(self.w[:], self.w_dram.rearrange("(k p) n -> p k n", p=P)).then_inc(self.w_in, DMA)

            def split_weight_high(self, act):
                act.wait_ge(self.w_in, START + DMA)
                act.activation(self.w_high[:], self.w[:], ACT.Copy).then_inc(self.w_high_done, 1)

            def split_weight_low(self, dve):
                dve.wait_ge(self.w_high_done, START + 1)
                dve.tensor_tensor(self.w_low[:], self.w[:], plain(self.w_high[:]), ALU.subtract).then_inc(
                    self.w_low_done, 1)

            def load(self, sp, i, k, rows):
                sp.wait_ge(self.xT_full[k], START + i)
                sp.dma_start(self.xs[k][:], rows).then_inc(self.xs_in[k], DMA)

            def transposes(self, pe, i, k):
                pe.wait_ge(self.xs_in[k], START + DMA * (i + 1))
                pe.wait_ge(self.low_done[1 - k], START + i + k)
                for kk in range(K):
                    mm = pe.transpose(self.xT_bank[:, kk * P:(kk + 1) * P], self.xs[k][:, kk * P:(kk + 1) * P],
                                      ident[:])
                mm.then_inc(self.xT_full[k], 1)

            def high(self, act, i, k):
                act.wait_ge(self.xT_full[k], START + i + 1)
                act.wait_ge(self.y_full[k], START + i)
                act.activation(self.xT_high[k][:], self.xT_bank[:, 0:D].rearrange("p (k n) -> p k n", k=K),
                               ACT.Copy).then_inc(self.high_done[k], 1)

            def low(self, dve, i, k):
                dve.wait_ge(self.high_done[k], START + i + 1)
                dve.tensor_tensor(self.xT_low[k][:], self.xT_bank[:, 0:D].rearrange("p (k n) -> p k n", k=K),
                                  plain(self.xT_high[k][:]), ALU.subtract).then_inc(self.low_done[k], 1)

            def products(self, pe, i, k):
                pe.wait_ge(self.low_done[k], START + i + 1)
                pe.wait_ge(self.y_done[1 - k], START + i + k)
                for kk in range(K):
                    for n, (a, b) in enumerate(((self.xT_high[k], self.w_high), (self.xT_high[k], self.w_low),
                                                (self.xT_low[k], self.w_high))):
                        mm = pe.matmul(self.y_bank[:, 0:D], a[:, kk, :], b[:, kk, :], start=(kk == 0 and n == 0),
                                       stop=(kk == K - 1 and n == 2))
                mm.then_inc(self.y_full[k], 1)

            def evacuate(self, act, i, k, scale=None):
                act.wait_ge(self.y_full[k], START + i + 1)
                t = 2 * i + k
                dst = self.y[:, bass.ds(t, 1), :].rearrange("p o d -> p (o d)")
                by = 1.0 if scale is None else scale[:, bass.ds(t, 1)]
                act.activation(dst, self.y_bank[:, 0:D], ACT.Copy, scale=by).then_inc(self.y_done[k], 1)

        class Propagation:
            def __init__(self, scope, tag, acc):
                self.acc = acc
                self.left_high = [sb(scope, f"{tag}_left_high{k}", [P, D], F32R) for k in range(2)]
                self.left_low = [sb(scope, f"{tag}_left_low{k}", [P, D], F32R) for k in range(2)]
                with ExitStack() as front_half:
                    self.mov_high, self.mov_low = (
                        [sb(front_half, f"{tag}_{part}{u}", [P, HALF], F32R) for u in range(2)]
                        for part in ("mov_high", "mov_low"))
                self.turn = [sb(scope, f"{tag}_turn{q}", [P, K, BANK]) for q in range(2)]
                self.z = [sb(scope, f"{tag}_z{q}", [P, TPB, D]) for q in range(2)]
                self.left_high_done = sems(scope, f"{tag}_left_high_done")
                self.left_low_done = sems(scope, f"{tag}_left_low_done")
                self.mov_high_done = sems(scope, f"{tag}_mov_high_done")
                self.mov_low_done = sems(scope, f"{tag}_mov_low_done")
                self.summed = [sems(scope, f"{tag}_summed{k}_") for k in range(2)]
                self.turn_full = sems(scope, f"{tag}_turn_full")
                self.turned = sems(scope, f"{tag}_turned")
                self.norm = NormSems(scope, tag)
                self.stored = sems(scope, f"{tag}_stored")

            def left_high_part(self, act, i, k, left):
                act.wait_ge(self.summed[k][1], START + i)
                act.activation(self.left_high[k][:], left, ACT.Copy).then_inc(self.left_high_done[k], 1)

            def left_low_part(self, dve, i, k, left):
                dve.wait_ge(self.left_high_done[k], START + i + 1)
                dve.tensor_tensor(self.left_low[k][:], left, plain(self.left_high[k][:]), ALU.subtract).then_inc(
                    self.left_low_done[k], 1)

            def high_part(self, act, i, k, u, source, **more):
                act.wait_ge(self.summed[1 - k][u], START + i + k)
                act.activation(self.mov_high[u][:], source, ACT.Copy, **more).then_inc(self.mov_high_done[u], 1)

            def low_part(self, dve, i, k, u, source):
                dve.wait_ge(self.mov_high_done[u], START + 2 * i + k + 1)
                dve.tensor_tensor(self.mov_low[u][:], source, plain(self.mov_high[u][:]), ALU.subtract).then_inc(
                    self.mov_low_done[u], 1)

            def products(self, pe):
                for i, first in first_apart(pe, PAIRS):
                    for k in range(2):
                        pe.wait_ge(self.left_low_done[k], START + i + 1)
                        for u in range(2):
                            pe.wait_ge(self.mov_low_done[u], START + 2 * i + k + 1)
                            for dh in range(K):
                                cols = slice(dh * P, (dh + 1) * P)
                                for n, (a, b) in enumerate(((self.left_high[k], self.mov_high[u]),
                                                            (self.left_high[k], self.mov_low[u]),
                                                            (self.left_low[k], self.mov_high[u]))):
                                    for j in range(HALF // BANK):
                                        mm = pe.matmul(self.acc[:, u * HALF // BANK + j, dh, :], a[:, cols],
                                                       b[:, j * BANK:(j + 1) * BANK],
                                                       start=(first and k == 0 and n == 0), stop=(n == 2),
                                                       skip_group_check=True)
                            mm.then_inc(self.summed[k][u], 1)

            def bank_pair(self, j):
                return self.acc[:, bass.ds(j, 1), :, :].rearrange("p o k n -> p (o k) n")

            def turn_in(self, act, i, q):
                if q == 0:
                    act.wait_ge(self.summed[1][0], START + PAIRS)
                    act.wait_ge(self.summed[1][1], START + PAIRS)
                act.wait_ge(self.turned[q], START + i)
                act.activation(self.turn[q][:], self.bank_pair(2 * i + q), ACT.Copy).then_inc(self.turn_full[q], 1)

            def turn_back(self, pe, j):
                q = j % 2
                pe.wait_ge(self.turn_full[q], START + j // 2 + 1)
                for dh in range(K):
                    for a in range(TPB):
                        mm = pe.transpose(self.acc[:, j, dh, a * P:(a + 1) * P],
                                          self.turn[q][:, dh, a * P:(a + 1) * P], ident[:])
                mm.then_inc(self.turned[q], 1)

            def residual(self, dve, i, q, scale_of, residual_of):
                dve.wait_ge(self.turned[q], START + i + 1)
                for a in range(TPB):
                    t = (2 * i + q) * TPB + a
                    agg = self.bank_pair(2 * i + q)[:, :, a * P:(a + 1) * P]
                    dve.scalar_tensor_tensor(
                        out=self.z[q][:, a, :].rearrange("p (k n) -> p k n", k=K), in0=agg, scalar=scale_of(t),
                        in1=residual_of(t).rearrange("p (k n) -> p k n", k=K), op0=ALU.mult, op1=ALU.add,
                    ).then_inc(self.norm.z_done[q], 1)
                dve.wait_ge(self.norm.z_done[q], START + TPB * (i + 1))

        class NormSems:
            def __init__(self, scope, tag):
                self.z_done = sems(scope, f"{tag}_z_done")
                self.stats_done = sems(scope, f"{tag}_stats_done")
                self.var_done = sems(scope, f"{tag}_var_done")
                self.dev_done = sems(scope, f"{tag}_dev_done")
                self.inv_done = sems(scope, f"{tag}_inv_done")
                self.normed = sems(scope, f"{tag}_normed")

        def norm_stats(dve, s, i, q, tile):
            for a in range(TPB):
                dve.bn_stats(stats[:, q, a, :], tile(a)).then_inc(s.stats_done[q], 1)
            dve.wait_ge(s.stats_done[q], START + TPB * (i + 1))
            for a in range(TPB):
                dve.bn_aggr(mean_var[:, q, a, :], stats[:, q, a, :]).then_inc(s.var_done[q], 1)

        def norm_root(act, s, i, q):
            act.wait_ge(s.var_done[q], START + TPB * (i + 1))
            act.activation(deviation[:, q, :], mean_var[:, q, :, 1], ACT.Sqrt, bias=eps_col[:, 0:1]).then_inc(
                s.dev_done[q], 1)

        def norm_apply(dve, s, i, q, tile, dst):
            dve.wait_ge(s.dev_done[q], START + i + 1)
            dve.reciprocal(inv_dev[:, q, :], deviation[:, q, :]).then_inc(s.inv_done[q], 1)
            dve.wait_ge(s.inv_done[q], START + i + 1)
            for a in range(TPB):
                dve.tensor_scalar(dst(a), tile(a), mean_var[:, q, a, 0:1], inv_dev[:, q, a:a + 1], ALU.subtract,
                                  ALU.mult).then_inc(s.normed[q], 1)

        front = ExitStack()
        with front:
            adjT = sb(front, "adjT", [P, T, N])
            xa = sb(front, "xa", [P, T, D])

            with ExitStack() as early:
                support = sb(early, "support", [P, T, D])
                mix_col = sb(early, "mix_col", [P, 1])
                one_less_mix = sb(early, "one_less_mix", [P, 1])
                with ExitStack() as s1:
                    rows = [sb(s1, f"rows{k}", [P, N]) for k in range(2)]
                    act_junk = sb(s1, "act_junk", [P, N], BF16)
                    dve_junk = [sb(s1, f"dve_junk{n}", [P, N], U8) for n in range(2)]
                    wv_in_sb = sb(s1, "wv_in_sb", [P, K, D])
                    wvt = sb(s1, "wvt", [P, K, D])
                    turn_bank = [s1.enter_context(nc.psum_tensor(f"turn_bank{g}", [P, TPB, P], F32))
                                 for g in range(GROUPS)]
                    spare_bank = [s1.enter_context(nc.psum_tensor(f"spare_bank{g}", [P, BANK], F32))
                                  for g in range(3)]
                    proj = Projection(s1, "sup", spare_bank[0:2], w0, support)
                    ident_zeroed = sem(s1, "ident_zeroed")
                    consts_done = sem(s1, "consts_done")
                    mix_in = sem(s1, "mix_in")
                    xa_in = sem(s1, "xa_in")
                    rows_in = sems(s1, "rows_in")
                    turn_full = sems(s1, "turn_full", GROUPS)
                    turn_free = sems(s1, "turn_free", GROUPS)
                    summed_rows = sems(s1, "summed_rows")
                    counted = [sems(s1, f"counted{n}_") for n in range(2)]
                    wv_in = sem(s1, "wv_in")
                    wvt_full = sem(s1, "wvt_full")
                    wvt_ready = sem(s1, "wvt_ready")
                    wvt_stored = sem(s1, "wvt_stored")
                    zeros_stored = sem(s1, "zeros_stored")

                    with next_block() as block:
                        @block.sync
                        def _(sp):
                            start(sp, 0, 5)
                            sp.dma_start(mix_col[:], mix.rearrange("(a b) -> a b", a=1).broadcast_to([P, 1])).then_inc(
                                mix_in, DMA)
                            proj.load_weight(sp)
                            with sp.Fori(0, PAIRS) as i:
                                for k in range(2):
                                    t = 2 * i + k
                                    sp.wait_ge(counted[0][k], START + i)
                                    sp.wait_ge(counted[1][k], START + i)
                                    sp.wait_ge(summed_rows[k], START + i)
                                    sp.dma_start(rows[k][:], adj[bass.ds(t * P, P), :]).then_inc(rows_in[k], DMA)
                                    proj.load(sp, i, k, x[bass.ds(t * P, P), :])
                                sp.wait_ge(wvt_full, START + i)
                                sp.dma_start(wv_in_sb[:], wv[:, bass.ds(i * D, D)].rearrange(
                                    "(k p) d -> p k d", p=P)).then_inc(wv_in, DMA)
                            sp.dma_start(xa[:], x.rearrange("(t p) d -> p t d", p=P)).then_inc(xa_in, DMA)
                            for k in range(2):
                                sp.wait_ge(counted[1][k], START + PAIRS)
                            sp.dma_start(zeros_scratch.rearrange("(t p) o -> p t o", p=P), zeros[:].rearrange(
                                "p (t o) -> p t o", o=1), allow_slow_non_contiguous=True).then_inc(zeros_stored, DMA)
                            sp.wait_ge(zeros_stored, START + DMA)
                            sp.wait_ge(xa_in, START + DMA)

                        @block.gpsimd
                        def _(pool):
                            start(pool, 1, 5)
                            pool.memset(ident[:], 0.0).then_inc(ident_zeroed, 1)
                            pool.memset(ones[:], 1.0).then_inc(consts_done, 1)
                            pool.memset(eps_col[:], LN_EPS).then_inc(consts_done, 1)
                            pool.memset(masked_col[:], MASKED).then_inc(consts_done, 1)
                            pool.wait_ge(ident_zeroed, START + 1)
                            pool.affine_select(out=ident[:], in_=ident[:], compare_op=ALU.not_equal, fill=1.0, base=0,
                                               pattern=[[-1, P]], channel_multiplier=1).then_inc(consts_done, 1)

                        @block.tensor
                        def _(pe):
                            start(pe, 2, 5)
                            pe.wait_ge(consts_done, START + 4)
                            pe.wait_ge(proj.w_low_done, START + 1)
                            with pe.Fori(0, PAIRS) as i:
                                for k in range(2):
                                    proj.transposes(pe, i, k)
                                    pe.wait_ge(rows_in[k], START + DMA * (i + 1))
                                    for g in range(GROUPS):
                                        pe.wait_ge(turn_free[g], START + 2 * i + k)
                                        for a in range(TPB):
                                            at = (g * TPB + a) * P
                                            mm = pe.transpose(turn_bank[g][:, a, :], rows[k][:, at:at + P], ident[:])
                                        mm.then_inc(turn_full[g], 1)
                                    proj.products(pe, i, k)
                                pe.wait_ge(wv_in, START + DMA * (i + 1))
                                pe.wait_ge(wvt_ready, START + i)
                                for dk in range(K):
                                    for kk in range(K):
                                        mm = pe.transpose(spare_bank[2][:, dk * D + kk * P:dk * D + (kk + 1) * P],
                                                          wv_in_sb[:, kk, dk * P:(dk + 1) * P], ident[:])
                                mm.then_inc(wvt_full, 1)

                        @block.scalar
                        def _(act):
                            start(act, 3, 5)
                            act.wait_ge(consts_done, START + 4)
                            proj.split_weight_high(act)
                            with act.Fori(0, PAIRS) as i:
                                for k in range(2):
                                    t = 2 * i + k
                                    proj.high(act, i, k)
                                    for g in range(GROUPS):
                                        act.wait_ge(turn_full[g], START + t + 1)
                                        act.activation(adjT[:, g * TPB:(g + 1) * TPB, bass.ds(t * P, P)],
                                                       turn_bank[g][:], ACT.Copy).then_inc(turn_free[g], 1)
                                    act.wait_ge(summed_rows[1 - k], START + i + k)
                                    act.activation(act_junk[:], rows[k][:], ACT.Copy,
                                                   accum_out=row_sum[:, bass.ds(t, 1)]).then_inc(summed_rows[k], 1)
                                    proj.evacuate(act, i, k)
                                act.wait_ge(wvt_full, START + i + 1)
                                act.wait_ge(wvt_stored, START + DMA * i)
                                act.activation(wvt[:], spare_bank[2][:].rearrange("p (k d) -> p k d", k=K),
                                               ACT.Copy).then_inc(wvt_ready, 1)
                                act.wait_ge(wvt_ready, START + i + 1)
                                act.dma_start(wvt_scratch[bass.ds(i, 1)].rearrange("o p k d -> (o p) k d"),
                                              wvt[:]).then_inc(wvt_stored, DMA)
                            act.wait_ge(wvt_stored, START + DMA * C)

                        @block.vector
                        def _(dve):
                            start(dve, 4, 5)
                            proj.split_weight_low(dve)
                            dve.wait_ge(mix_in, START + DMA)
                            dve.tensor_scalar(one_less_mix[:], mix_col[:], -1.0, 1.0, ALU.mult, ALU.add)
                            with dve.Fori(0, PAIRS) as i:
                                for k in range(2):
                                    t = 2 * i + k
                                    proj.low(dve, i, k)
                                    dve.wait_ge(rows_in[k], START + DMA * (i + 1))
                                    for n in range(2):
                                        dve.wait_ge(counted[n][1 - k], START + i + k)
                                    dve.tensor_scalar(dve_junk[0][:], rows[k][:], 0.0, 0.0, ALU.is_gt, ALU.add,
                                                      accum_out=positives[:, bass.ds(t, 1)]).then_inc(counted[0][k], 1)
                                    dve.tensor_scalar(dve_junk[1][:], rows[k][:], 0.0, 0.0, ALU.is_equal, ALU.add,
                                                      accum_out=zeros[:, bass.ds(t, 1)]).then_inc(counted[1][k], 1)

                with ExitStack() as s2:
                    acc = s2.enter_context(nc.psum_tensor("acc0", [P, GROUPS, K, BANK], F32))
                    prop = Propagation(s2, "l0", acc)
                    raw = [sb(s2, f"raw{u}", [P, HALF]) for u in range(2)]
                    masked = [sb(s2, f"masked{u}", [P, HALF]) for u in range(2)]
                    raw_in = sems(s2, "raw_in")
                    floor_done = sems(s2, "floor_done")
                    masked_done = sems(s2, "masked_done")
                    masked_stored = sems(s2, "masked_stored")
                    mixed = sems(s2, "mixed")
                    by_c = lambda ap: ap.rearrange("p (r c) -> p c r", c=C)
                    grouped = lambda ap: ap.rearrange("p (c r) -> p c r", c=C)

                    with next_block() as block:
                        @block.sync
                        def _(sp):
                            start(sp, 0, 5)
                            def load(t, u):
                                sp.dma_start(raw[u][:], adj[bass.ds(t * P, P), u * HALF:(u + 1) * HALF]).then_inc(
                                    raw_in[u], DMA)

                            def store(t, u):
                                dst = bias_scratch[bass.ds(t * P, P), :].rearrange("n (c r) -> n c r", c=C)
                                sp.dma_start(dst[:, :, u * P:(u + 1) * P], grouped(masked[u][:])).then_inc(
                                    masked_stored[u], DMA)

                            for u in range(2):
                                load(0, u)
                            with sp.Fori(1, T) as t:
                                for u in range(2):
                                    sp.wait_ge(masked_done[u], START + t)
                                    load(t, u)
                                    store(t - 1, u)
                            for u in range(2):
                                sp.wait_ge(masked_done[u], START + T)
                                store(T - 1, u)
                            for u in range(2):
                                sp.wait_ge(masked_stored[u], START + DMA * T)

                        @block.gpsimd
                        def _(pool):
                            start(pool, 1, 5)
                            with pool.Fori(0, T) as t:
                                for u in range(2):
                                    pool.wait_ge(floor_done[u], START + t + 1)
                                    pool.tensor_tensor(grouped(masked[u][:]), grouped(masked[u][:]), by_c(raw[u][:]),
                                                       ALU.add).then_inc(masked_done[u], 1)

                        @block.tensor
                        def _(pe):
                            start(pe, 2, 5)
                            prop.products(pe)
                            for j in range(GROUPS):
                                prop.turn_back(pe, j)

                        @block.scalar
                        def _(act):
                            start(act, 3, 5)
                            act.activation(deviation[:, 0, 0:1], eps_col[:], ACT.Sqrt)
                            with act.Fori(0, PAIRS) as i:
                                for k in range(2):
                                    t = 2 * i + k
                                    prop.left_high_part(act, i, k, support[:, bass.ds(t, 1), :].rearrange(
                                        "p o d -> p (o d)"))
                                    for u in range(2):
                                        source = adjT[:, bass.ds(t, 1), u * HALF:(u + 1) * HALF].rearrange(
                                            "p o n -> p (o n)")
                                        total = col_sum[:, bass.ds(t, 1), u:u + 1].rearrange("p o n -> p (o n)")
                                        prop.high_part(act, i, k, u, source, accum_out=total)
                            with act.Fori(0, GROUPS // 2) as i:
                                for q in range(2):
                                    prop.turn_in(act, i, q)
                                for q in range(2):
                                    norm_root(act, prop.norm, i, q)

                        @block.vector
                        def _(dve):
                            start(dve, 4, 5)
                            with dve.Fori(0, PAIRS) as i:
                                for k in range(2):
                                    t = 2 * i + k
                                    prop.left_low_part(dve, i, k, support[:, bass.ds(t, 1), :].rearrange(
                                        "p o d -> p (o d)"))
                                    for u in range(2):
                                        prop.low_part(dve, i, k, u, adjT[:, bass.ds(t, 1), u * HALF:(u + 1) * HALF]
                                                      .rearrange("p o n -> p (o n)"))
                                        dve.wait_ge(raw_in[u], START + DMA * (t + 1))
                                        dve.wait_ge(masked_stored[u], START + DMA * t)
                                        dve.tensor_scalar(grouped(masked[u][:]), by_c(raw[u][:]), 0.0, NEVER,
                                                          ALU.is_equal, ALU.mult).then_inc(floor_done[u], 1)
                            for j in range(GROUPS):
                                tiles = slice(j * TPB, (j + 1) * TPB)
                                dve.scalar_tensor_tensor(out=xa[:, tiles, :], in0=support[:, tiles, :],
                                                         scalar=one_less_mix[:, 0:1], in1=xa[:, tiles, :],
                                                         op0=ALU.mult, op1=ALU.add).then_inc(mixed[0], 1)
                            dve.wait_ge(mixed[0], START + GROUPS)
                            for i in range(GROUPS // 2):
                                for q in range(2):
                                    prop.residual(dve, i, q, lambda t: mix_col[:, 0:1],
                                                  lambda t: xa[:, bass.ds(t, 1), :].rearrange("p o d -> p (o d)"))
                                    norm_stats(dve, prop.norm, i, q, lambda a: prop.z[q][:, a, :])
                                for q in range(2):
                                    norm_apply(dve, prop.norm, i, q, lambda a: prop.z[q][:, a, :],
                                               lambda a: xa[:, bass.ds((2 * i + q) * TPB + a, 1), :].rearrange(
                                                   "p o d -> p (o d)"))

            with ExitStack() as s3:
                acc = s3.enter_context(nc.psum_tensor("acc1", [P, GROUPS, K, BANK], F32))
                prop = Propagation(s3, "l1", acc)
                inc = [sb(s3, f"inc{n}", [P, HALF]) for n in range(4)]
                head_row = sb(s3, "head_row", [P, N])
                head_diag = sb(s3, "head_diag", [P, TPB, P])
                head = sb(s3, "head", [P, T])
                length = sb(s3, "length", [P, T])
                inv_degree = sb(s3, "inv_degree", [P, T])
                length_done = sem(s3, "length_done")
                small = sem(s3, "small")
                diag_done = sem(s3, "diag_done")
                head_full = sem(s3, "head_full")
                head_out = sem(s3, "head_out")
                head_part = sems(s3, "head_part", 4)
                inc_done = sems(s3, "inc_done", 4)

                with next_block() as block:
                    @block.tensor
                    def _(pe):
                        start(pe, 0, 5)
                        for g in range(GROUPS):
                            pe.wait_ge(diag_done, START + TPB * (g + 1))
                            pe.matmul(acc[:, g, 0, :], ones[:],
                                      head_diag[:].rearrange("p a n -> p (a n)"), start=True,
                                      stop=True).then_inc(head_full, 1)
                        pe.wait_ge(head_out, START + GROUPS)
                        prop.products(pe)
                        for j in range(GROUPS):
                            prop.turn_back(pe, j)

                    @block.scalar
                    def _(act):
                        start(act, 1, 5)
                        act.activation(length[:], positives[:], ACT.Sqrt).then_inc(length_done, 1)
                        for g in range(GROUPS):
                            act.wait_ge(head_full, START + g + 1)
                            act.activation(head_row[:, g * BANK:(g + 1) * BANK], acc[:, g, 0, :],
                                           ACT.Copy).then_inc(head_out, 1)
                        with act.Fori(0, PAIRS) as i:
                            for k in range(2):
                                t = 2 * i + k
                                prop.left_high_part(act, i, k, xa[:, bass.ds(t, 1), :].rearrange("p o d -> p (o d)"))
                                for u in range(2):
                                    n = 2 * k + u
                                    act.wait_ge(inc_done[n], START + i + 1)
                                    prop.high_part(act, i, k, u, inc[n][:])
                        with act.Fori(0, GROUPS // 2) as i:
                            for q in range(2):
                                prop.turn_in(act, i, q)
                            for q in range(2):
                                norm_root(act, prop.norm, i, q)

                    @block.gpsimd
                    def _(pool):
                        start(pool, 2, 5)
                        with pool.Fori(0, PAIRS) as i:
                            for k in range(2):
                                for u in range(2):
                                    n = 2 * k + u
                                    pool.wait_ge(head_part[n], START + i + 1)
                                    pool.tensor_tensor(inc[n][:], inc[n][:],
                                                       adjT[:, bass.ds(2 * i + k, 1), u * HALF:(u + 1) * HALF]
                                                       .rearrange("p o n -> p (o n)"), ALU.add).then_inc(inc_done[n], 1)

                    @block.vector
                    def _(dve):
                        start(dve, 3, 5)
                        dve.wait_ge(length_done, START + 1)
                        dve.tensor_scalar(length[:], length[:], NORM_EPS, None, ALU.max).then_inc(small, 1)
                        dve.wait_ge(small, START + 1)
                        dve.reciprocal(head[:], length[:]).then_inc(small, 1)
                        dve.wait_ge(small, START + 2)
                        dve.tensor_tensor(length[:], positives[:], head[:], ALU.mult).then_inc(small, 1)
                        dve.wait_ge(small, START + 3)
                        dve.tensor_tensor(length[:], length[:], row_sum[:], ALU.add).then_inc(small, 1)
                        dve.wait_ge(small, START + 4)
                        dve.reciprocal(inv_degree[:], length[:]).then_inc(small, 1)
                        for g in range(GROUPS):
                            if g:
                                dve.wait_ge(head_full, START + g)
                            for a in range(TPB):
                                dve.tensor_scalar(head_diag[:, a, :], ident[:], head[:, g * TPB + a:g * TPB + a + 1],
                                                  None, ALU.mult).then_inc(diag_done, 1)
                        dve.wait_ge(head_out, START + GROUPS)

                        for n in range(4):
                            dve.scalar_tensor_tensor(
                                out=inc[n][:], in0=adjT[:, n // 2, (n % 2) * HALF:(n % 2 + 1) * HALF], scalar=0.0,
                                in1=head_row[:, (n % 2) * HALF:(n % 2 + 1) * HALF], op0=ALU.is_gt,
                                op1=ALU.mult).then_inc(head_part[n], 1)

                        def pair(i, more):
                            for k in range(2):
                                prop.left_low_part(dve, i, k, xa[:, bass.ds(2 * i + k, 1), :].rearrange(
                                    "p o d -> p (o d)"))
                                for u in range(2):
                                    n = 2 * k + u
                                    dve.wait_ge(prop.mov_high_done[u], START + 2 * i + k + 1)
                                    dve.tensor_tensor(prop.mov_low[u][:], inc[n][:], plain(prop.mov_high[u][:]),
                                                      ALU.subtract).then_inc(prop.mov_low_done[u], 1)
                                    if more:
                                        dve.wait_ge(prop.mov_low_done[u], START + 2 * i + k + 1)
                                        dve.scalar_tensor_tensor(
                                            out=inc[n][:],
                                            in0=adjT[:, bass.ds(2 * (i + 1) + k, 1), u * HALF:(u + 1) * HALF]
                                            .rearrange("p o n -> p (o n)"), scalar=0.0,
                                            in1=head_row[:, u * HALF:(u + 1) * HALF], op0=ALU.is_gt,
                                            op1=ALU.mult).then_inc(head_part[n], 1)

                        with dve.Fori(0, PAIRS - 1) as i:
                            pair(i, True)
                        pair(PAIRS - 1, False)
                        for i in range(GROUPS // 2):
                            for q in range(2):
                                dve.wait_ge(prop.stored[q], START + DMA * i)
                                prop.residual(dve, i, q, lambda t: inv_degree[:, bass.ds(t, 1)],
                                              lambda t: xa[:, bass.ds(t, 1), :].rearrange("p o d -> p (o d)"))
                                norm_stats(dve, prop.norm, i, q, lambda a: prop.z[q][:, a, :])
                            for q in range(2):
                                norm_apply(dve, prop.norm, i, q, lambda a: prop.z[q][:, a, :],
                                           lambda a: prop.z[q][:, a, :])

                    @block.sync
                    def _(sp):
                        start(sp, 4, 5)
                        x1_tiles = x1_scratch.rearrange("(t p) d -> p t d", p=P)
                        with sp.Fori(0, GROUPS // 2) as i:
                            for q in range(2):
                                sp.wait_ge(prop.norm.normed[q], START + TPB * (i + 1))
                                sp.dma_start(x1_tiles[:, bass.ds((2 * i + q) * TPB, TPB), :], prop.z[q][:]).then_inc(
                                    prop.stored[q], DMA)
                        for q in range(2):
                            sp.wait_ge(prop.stored[q], START + DMA * (GROUPS // 2))
        clear_spent()

        with ExitStack() as s4:
            x1_head = sb(s4, "x1_head", [P, 2, D])
            xT_high = sb(s4, "xT_high", [P, K, R], F32R)
            xT_low = sb(s4, "xT_low", [P, K, R], F32R)
            wo_raw = sb(s4, "wo_raw", [P, K, D])
            wo_high = sb(s4, "wo_high", [P, K, D], F32R)
            wo_low = sb(s4, "wo_low", [P, K, D], F32R)
            wk_raw, wvt_raw = ([sb(s4, f"{w}_raw{k}", [P, K, D]) for k in range(2)] for w in ("wk", "wvt"))
            wk_high, wk_low, wvt_high, wvt_low, fold_high, fold_low = (
                [sb(s4, f"{w}{k}", [P, K, D], F32R) for k in range(2)]
                for w in ("wk_high", "wk_low", "wvt_high", "wvt_low", "fold_high", "fold_low"))
            wq_raw = sb(s4, "wq_raw", [P, K, D])
            wq_high = sb(s4, "wq_high", [P, K, D], F32R)
            wq_low = sb(s4, "wq_low", [P, K, D], F32R)
            qT_high = sb(s4, "qT_high", [P, K, R], F32R)
            qT_low = sb(s4, "qT_low", [P, K, R], F32R)
            kT_high = sb(s4, "kT_high", [P, K, N], F32R)
            kT_low = sb(s4, "kT_low", [P, K, N], F32R)
            vals = sb(s4, "vals", [P, T, 2, D], F32R)
            masked_in = [sb(s4, f"masked_in{b}", [P, N]) for b in range(2)]
            probs = [sb(s4, f"probs{b}", [P, N]) for b in range(2)]
            pT_high = sb(s4, "pT_high", [P, T, P], F32R)
            pT_low = sb(s4, "pT_low", [P, T, P], F32R)
            total = sb(s4, "total", [P, T, D])
            zero_count = sb(s4, "zero_count", [P, T])
            least = sb(s4, "least", [P, T])
            least_tmp = sb(s4, "least_tmp", [P, T])
            chunk_max = [sb(s4, f"chunk_max{b}", [P, GROUPS]) for b in range(2)]
            row_max = [sb(s4, f"row_max{b}", [P, 1]) for b in range(2)]
            neg_max = [sb(s4, f"neg_max{b}", [P, 1]) for b in range(2)]
            masked_exp = [sb(s4, f"masked_exp{b}", [P, 1]) for b in range(2)]
            chunk_sum = [sb(s4, f"chunk_sum{b}", [P, GROUPS]) for b in range(2)]
            row_total = [sb(s4, f"row_total{b}", [P, 1]) for b in range(2)]
            denom = [sb(s4, f"denom{b}", [P, 1]) for b in range(2)]
            inv_denom = [sb(s4, f"inv_denom{b}", [P, 1]) for b in range(2)]
            s_bank, t_bank, o_bank, m_bank = (
                [s4.enter_context(nc.psum_tensor(f"{n}_bank{b}", [P, BANK], F32)) for b in range(2)]
                for n in ("s", "t", "o", "m"))

            total_in = sem(s4, "total_in")
            count_in = sem(s4, "count_in")
            least_done = sem(s4, "least_done")
            x1_in = sem(s4, "x1_in")
            xT_full = sem(s4, "xT_full")
            xT_high_done = sem(s4, "xT_high_done")
            xT_low_done = sem(s4, "xT_low_done")
            wo_in = sem(s4, "wo_in")
            wo_high_done = sem(s4, "wo_high_done")
            wo_low_done = sem(s4, "wo_low_done")
            wk_in, wvt_in, wk_high_done, wk_low_done, wvt_high_done, wvt_low_done = (
                sems(s4, f"{n}_") for n in
                ("wk_in", "wvt_in", "wk_high_done", "wk_low_done", "wvt_high_done", "wvt_low_done"))
            fold_full, fold_high_done, fold_low_done = (
                sems(s4, f"{n}_") for n in ("fold_full", "fold_high_done", "fold_low_done"))
            k_full, k_high_done, k_low_done = (sems(s4, f"{n}_") for n in ("k_full", "k_high_done", "k_low_done"))
            v_full, v_high_done, v_low_done = (sems(s4, f"{n}_") for n in ("v_full", "v_high_done", "v_low_done"))
            wq_in = sem(s4, "wq_in")
            wq_high_done = sem(s4, "wq_high_done")
            wq_low_done = sem(s4, "wq_low_done")
            q_full = sem(s4, "q_full")
            q_high_done = sem(s4, "q_high_done")
            q_low_done = sem(s4, "q_low_done")
            bias_in = sems(s4, "bias_in")
            s_full = sems(s4, "s_full")
            s_done = sems(s4, "s_done")
            first_max_done = sem(s4, "first_max_done")
            max_done = sems(s4, "max_done")
            neg_done = sems(s4, "neg_done")
            masked_exp_done = sems(s4, "masked_exp_done")
            exp_done = sems(s4, "exp_done")
            t_full = sems(s4, "t_full")
            pT_high_done = sems(s4, "pT_high_done")
            pT_low_done = sems(s4, "pT_low_done")
            sum_done = sems(s4, "sum_done")
            denom_done = sems(s4, "denom_done")
            inv_done = sems(s4, "inv_done")
            o_full = sems(s4, "o_full")
            o_half = sems(s4, "o_half")
            o_done = sems(s4, "o_done")
            norm2 = NormSems(s4, "l2")
            x2_stored = sem(s4, "x2_stored")

            half_scale = 0.5 * float(D) ** -0.5
            halves = lambda bank: bank[:].rearrange("p (k n) -> p k n", k=K)

            def three_products(pe, dst, left, right, kk_range, cols, last_sem):
                for kk in kk_range:
                    for n, (a, b) in enumerate(((left[0], right[0]), (left[0], right[1]), (left[1], right[0]))):
                        mm = pe.matmul(dst, a[:, kk, cols], b[:, kk, :], start=(kk == 0 and n == 0),
                                       stop=(kk == K - 1 and n == 2))
                return mm

            with next_block() as block:
                @block.sync
                def _(sp):
                    start(sp, 0, 4)
                    sp.dma_start(total[:].rearrange("p (a c) d -> p a (c d)", a=2),
                                 x1_scratch.rearrange("(a r c) d -> r a (c d)", a=2, c=C)).then_inc(total_in, DMA)
                    sp.dma_start(zero_count[:].rearrange("p (a c) -> p a c", a=2),
                                 zeros_scratch.rearrange("(a r c) o -> r a (c o)", a=2, c=C)).then_inc(count_in, DMA)
                    bias_rows = bias_scratch.rearrange("(b r c) m -> b c r m", b=2, c=C)

                    def load_keys_weights(h, jj, k):
                        c, n = 2 * jj + k, 4 * h + jj
                        sp.wait_ge(wk_low_done[k], START + n)
                        sp.dma_start(wk_raw[k][:], wk[:, bass.ds(c * D, D)].rearrange("(k p) n -> p k n", p=P)
                                     ).then_inc(wk_in[k], DMA)
                        sp.wait_ge(wvt_low_done[k], START + n)
                        sp.dma_start(wvt_raw[k][:], wvt_scratch[bass.ds(c, 1)].rearrange("o p k n -> (o p) k n")
                                     ).then_inc(wvt_in[k], DMA)

                    def load_tile_inputs(c, use):
                        sp.wait_ge(wq_low_done, START + use)
                        sp.dma_start(wq_raw[:], wq[:, bass.ds(c * D, D)].rearrange("(k p) n -> p k n", p=P)
                                     ).then_inc(wq_in, DMA)
                        for b in range(2):
                            sp.wait_ge(neg_done[b], START + use)
                            sp.dma_start(masked_in[b][:], bias_rows[b, bass.ds(c, 1)].rearrange("o r m -> (o r) m")
                                         ).then_inc(bias_in[b], DMA)

                    with sp.Fori(0, H) as h:
                        sp.wait_ge(xT_full, START + h)
                        sp.dma_start(x1_head[:], x1_scratch[bass.ds(h * R, R), :].rearrange("(a p) d -> p a d", p=P)
                                     ).then_inc(x1_in, DMA)
                        sp.wait_ge(wo_low_done, START + h)
                        sp.dma_start(wo_raw[:], wout[bass.ds(h * D, D), :].rearrange("(k p) n -> p k n", p=P)
                                     ).then_inc(wo_in, DMA)
                        for k in range(2):
                            load_keys_weights(h, 0, k)
                        with sp.Fori(1, C // 2) as jj:
                            for k in range(2):
                                load_keys_weights(h, jj, k)
                        load_tile_inputs(0, h * C)
                        with sp.Fori(1, C) as c:
                            load_tile_inputs(c, h * C + c)
                    sp.wait_ge(norm2.normed[0], START + T // 2)
                    sp.wait_ge(norm2.normed[1], START + T // 2)
                    sp.dma_start(x2_scratch.rearrange("(a r c) d -> r a (c d)", a=2, c=C),
                                 total[:].rearrange("p (a c) d -> p a (c d)", a=2)).then_inc(x2_stored, DMA)
                    sp.wait_ge(x2_stored, START + DMA)

                @block.tensor
                def _(pe):
                    start(pe, 1, 4)
                    def turn_x(h):
                        pe.wait_ge(x1_in, START + DMA * (h + 1))
                        for kk in range(K):
                            for a in range(2):
                                mm = pe.transpose(m_bank[0][:, kk * R + a * P:kk * R + (a + 1) * P],
                                                  x1_head[:, a, kk * P:(kk + 1) * P], ident[:])
                        mm.then_inc(xT_full, 1)

                    def keys_and_values(h, jj, k):
                        n = 4 * h + jj
                        if k == 0:
                            pe.wait_ge(xT_low_done, START + h + 1)
                            pe.wait_ge(wo_low_done, START + h + 1)
                        pe.wait_ge(wvt_low_done[k], START + n + 1)
                        pe.wait_ge(fold_low_done[1 - k], START + n + k)
                        for a in range(2):
                            mm = three_products(pe, m_bank[0][:, a * D:(a + 1) * D], (wvt_high[k], wvt_low[k]),
                                                (wo_high, wo_low), range(K), slice(a * P, (a + 1) * P), None)
                        mm.then_inc(fold_full[k], 1)
                        pe.wait_ge(wk_low_done[k], START + n + 1)
                        pe.wait_ge(k_low_done[1 - k], START + n + k)
                        if k == 0:
                            pe.wait_ge(q_low_done, START + h * C)
                        for dh in range(K):
                            mm = three_products(pe, m_bank[1][:, dh * R:(dh + 1) * R], (wk_high[k], wk_low[k]),
                                                (xT_high, xT_low), range(K), slice(dh * P, (dh + 1) * P), None)
                        mm.then_inc(k_full[k], 1)
                        pe.wait_ge(fold_low_done[k], START + n + 1)
                        pe.wait_ge(v_low_done[k], START + n)
                        pe.wait_ge(o_done[k], START + h * C)
                        for a in range(2):
                            mm = three_products(pe, o_bank[k][:, a * D:(a + 1) * D], (xT_high, xT_low),
                                                (fold_high[k], fold_low[k]), range(K), slice(a * P, (a + 1) * P), None)
                        mm.then_inc(v_full[k], 1)

                    def queries(use):
                        pe.wait_ge(wq_low_done, START + use + 1)
                        for dh in range(K):
                            mm = three_products(pe, m_bank[1][:, dh * R:(dh + 1) * R], (wq_high, wq_low),
                                                (xT_high, xT_low), range(K), slice(dh * P, (dh + 1) * P), None)
                        mm.then_inc(q_full, 1)

                    def scores(b, use, j):
                        bank = j % 2
                        if j == 0:
                            pe.wait_ge(q_low_done, START + use + 1)
                        pe.wait_ge(s_done[bank], START + 2 * (2 * use + b) + j // 2)
                        for dh in range(K):
                            for n, (a, kT) in enumerate(((qT_high, kT_high), (qT_high, kT_low), (qT_low, kT_high))):
                                mm = pe.matmul(s_bank[bank][:], a[:, dh, b * P:(b + 1) * P],
                                               kT[:, dh, j * BANK:(j + 1) * BANK], start=(dh == 0 and n == 0),
                                               stop=(dh == K - 1 and n == 2))
                        mm.then_inc(s_full[bank], 1)

                    def turns(b, use, g):
                        pe.wait_ge(exp_done[b], START + GROUPS * use + g + 1)
                        pe.wait_ge(pT_low_done[g % 2], START + 2 * (2 * use + b) + g // 2)
                        for a in range(TPB):
                            at = (g * TPB + a) * P
                            mm = pe.transpose(t_bank[g % 2][:, a * P:(a + 1) * P], probs[b][:, at:at + P], ident[:])
                        mm.then_inc(t_full[g % 2], 1)

                    def weigh(b, use, g):
                        if g == 0:
                            pe.wait_ge(o_done[b], START + use)
                        pe.wait_ge(pT_low_done[g % 2], START + 2 * (2 * use + b) + g // 2 + 1)
                        for t in range(g * TPB, (g + 1) * TPB):
                            pe.matmul(o_bank[b][:], pT_high[:, t, :], vals[:, t, :, :].rearrange("p s d -> p (s d)"),
                                      start=(t == 0), stop=False)
                            mm = pe.matmul(o_bank[b][:, 0:D], pT_low[:, t, :], vals[:, t, 0, :], start=False,
                                           stop=(t == T - 1))
                        if g == GROUPS - 1:
                            mm.then_inc(o_full[b], 1)

                    def step(b, use, next_scores, next_queries):
                        score = (lambda j: scores(1 - b, use + b, j)) if next_scores else (lambda j: None)
                        turns(b, use, 0)
                        turns(b, use, 1)
                        score(0)
                        turns(b, use, 2)
                        score(1)
                        turns(b, use, 3)
                        score(2)
                        weigh(b, use, 0)
                        score(3)
                        if next_queries:
                            queries(use + 1)
                        for g in range(1, GROUPS):
                            weigh(b, use, g)

                    with pe.Fori(0, H) as h:
                        turn_x(h)
                        with pe.Fori(0, C // 2) as jj:
                            for k in range(2):
                                keys_and_values(h, jj, k)
                        for k in range(2):
                            pe.wait_ge(k_low_done[k], START + (h + 1) * (C // 2))
                            pe.wait_ge(v_low_done[k], START + (h + 1) * (C // 2))
                        queries(h * C)
                        for j in range(GROUPS):
                            scores(0, h * C, j)
                        with pe.Fori(0, C - 1) as c:
                            step(0, h * C + c, True, True)
                            step(1, h * C + c, True, False)
                        step(0, h * C + C - 1, True, False)
                        step(1, h * C + C - 1, False, False)

                @block.scalar
                def _(act):
                    start(act, 2, 4)
                    def split_keys_weights(h, jj, k):
                        n = 4 * h + jj
                        act.wait_ge(k_full[k], START + n)
                        act.wait_ge(wvt_in[k], START + DMA * (n + 1))
                        act.activation(wvt_high[k][:], wvt_raw[k][:], ACT.Copy).then_inc(wvt_high_done[k], 1)
                        act.wait_ge(wk_in[k], START + DMA * (n + 1))
                        act.activation(wk_high[k][:], wk_raw[k][:], ACT.Copy).then_inc(wk_high_done[k], 1)

                    def evacuate_keys(h, jj, k):
                        n, c = 4 * h + jj, 2 * jj + k
                        act.wait_ge(fold_full[k], START + n + 1)
                        act.wait_ge(v_full[k], START + n)
                        act.activation(fold_high[k][:], halves(m_bank[0]), ACT.Copy).then_inc(fold_high_done[k], 1)
                        act.wait_ge(k_full[k], START + n + 1)
                        act.activation(kT_high[:, :, bass.ds(c * R, R)], halves(m_bank[1]), ACT.Copy).then_inc(
                            k_high_done[k], 1)
                        act.wait_ge(v_full[k], START + n + 1)
                        act.activation(vals[:, bass.ds(2 * c, 2), 0, :], halves(o_bank[k]), ACT.Copy).then_inc(
                            v_high_done[k], 1)

                    def split_query_weights(use):
                        act.wait_ge(wq_in, START + DMA * (use + 1))
                        act.wait_ge(q_full, START + use)
                        act.activation(wq_high[:], wq_raw[:], ACT.Copy).then_inc(wq_high_done, 1)

                    def evacuate_queries(use):
                        act.wait_ge(q_full, START + use + 1)
                        act.activation(qT_high[:], halves(m_bank[1]), ACT.Copy, scale=half_scale).then_inc(
                            q_high_done, 1)

                    def exps(b, use, j):
                        if j == 0:
                            act.wait_ge(neg_done[b], START + use + 1)
                            act.wait_ge(inv_done[b], START + use)
                            act.activation(masked_exp[b][:], neg_max[b][:], ACT.Exp, bias=masked_col[:, 0:1]).then_inc(
                                masked_exp_done[b], 1)
                        part = probs[b][:, j * BANK:(j + 1) * BANK]
                        act.activation(part, part, ACT.Exp, bias=neg_max[b][:, 0:1], scale=2.0,
                                       accum_out=chunk_sum[b][:, j:j + 1]).then_inc(exp_done[b], 1)

                    def prob_high(b, use, g):
                        act.wait_ge(t_full[g % 2], START + 2 * (2 * use + b) + g // 2 + 1)
                        act.activation(pT_high[:, g * TPB:(g + 1) * TPB, :], t_bank[g % 2][:].rearrange(
                            "p (a n) -> p a n", a=TPB), ACT.Copy).then_inc(pT_high_done[g % 2], 1)

                    def step(b, use, next_queries):
                        exps(b, use, 0)
                        exps(b, use, 1)
                        prob_high(b, use, 0)
                        exps(b, use, 2)
                        prob_high(b, use, 1)
                        exps(b, use, 3)
                        prob_high(b, use, 2)
                        if next_queries:
                            split_query_weights(use + 1)
                        prob_high(b, use, 3)
                        if next_queries:
                            evacuate_queries(use + 1)

                    act.activation(masked_exp[0][:], masked_col[:], ACT.Exp).then_inc(masked_exp_done[0], 1)
                    with act.Fori(0, H) as h:
                        act.wait_ge(xT_full, START + h + 1)
                        act.activation(xT_high[:], halves(m_bank[0]), ACT.Copy).then_inc(xT_high_done, 1)
                        act.wait_ge(wo_in, START + DMA * (h + 1))
                        act.activation(wo_high[:], wo_raw[:], ACT.Copy).then_inc(wo_high_done, 1)
                        split_keys_weights(h, 0, 0)
                        with act.Fori(0, C // 2 - 1) as jj:
                            split_keys_weights(h, jj, 1)
                            evacuate_keys(h, jj, 0)
                            split_keys_weights(h, jj + 1, 0)
                            evacuate_keys(h, jj, 1)
                        split_keys_weights(h, C // 2 - 1, 1)
                        evacuate_keys(h, C // 2 - 1, 0)
                        evacuate_keys(h, C // 2 - 1, 1)
                        split_query_weights(h * C)
                        evacuate_queries(h * C)
                        with act.Fori(0, C - 1) as c:
                            step(0, h * C + c, True)
                            step(1, h * C + c, False)
                        step(0, h * C + C - 1, False)
                        step(1, h * C + C - 1, False)
                    with act.Fori(0, T // TPB // 2) as i:
                        for q in range(2):
                            norm_root(act, norm2, i, q)

                @block.vector
                def _(dve):
                    start(dve, 3, 4)
                    def low(dst, source, high):
                        return dve.tensor_tensor(dst, source, plain(high), ALU.subtract)

                    def split_keys_weights(h, jj, k):
                        n = 4 * h + jj
                        dve.wait_ge(wvt_high_done[k], START + n + 1)
                        low(wvt_low[k][:], wvt_raw[k][:], wvt_high[k][:]).then_inc(wvt_low_done[k], 1)
                        dve.wait_ge(wk_high_done[k], START + n + 1)
                        low(wk_low[k][:], wk_raw[k][:], wk_high[k][:]).then_inc(wk_low_done[k], 1)

                    def evacuate_keys(h, jj, k):
                        n, c = 4 * h + jj, 2 * jj + k
                        dve.wait_ge(fold_high_done[k], START + n + 1)
                        low(fold_low[k][:], halves(m_bank[0]), fold_high[k][:]).then_inc(fold_low_done[k], 1)
                        dve.wait_ge(k_high_done[k], START + n + 1)
                        low(kT_low[:, :, bass.ds(c * R, R)], halves(m_bank[1]), kT_high[:, :, bass.ds(c * R, R)]
                            ).then_inc(k_low_done[k], 1)
                        dve.wait_ge(v_high_done[k], START + n + 1)
                        low(vals[:, bass.ds(2 * c, 2), 1, :], halves(o_bank[k]), vals[:, bass.ds(2 * c, 2), 0, :]
                            ).then_inc(v_low_done[k], 1)

                    def split_query_weights(use):
                        dve.wait_ge(wq_high_done, START + use + 1)
                        low(wq_low[:], wq_raw[:], wq_high[:]).then_inc(wq_low_done, 1)

                    def evacuate_queries(use):
                        dve.wait_ge(q_high_done, START + use + 1)
                        dve.scalar_tensor_tensor(out=qT_low[:], in0=halves(m_bank[1]), scalar=half_scale,
                                                 in1=plain(qT_high[:]), op0=ALU.mult, op1=ALU.subtract).then_inc(
                            q_low_done, 1)

                    def await_scores(b, use, j):
                        dve.wait_ge(s_full[j % 2], START + 2 * (2 * use + b) + j // 2 + 1)

                    def masked_scores(b, use, j):
                        at = slice(j * BANK, (j + 1) * BANK)
                        dve.tensor_tensor_reduce(probs[b][:, at], s_bank[j % 2][:], masked_in[b][:, at], 1.0, NEVER,
                                                 ALU.add, ALU.max, chunk_max[b][:, j:j + 1]).then_inc(s_done[j % 2], 1)

                    def first_masked_scores(use, j):
                        at = slice(j * BANK, (j + 1) * BANK)
                        if j == 0:
                            dve.wait_ge(bias_in[0], START + DMA * (use + 1))
                        await_scores(0, use, j)
                        dve.tensor_tensor(probs[0][:, at], s_bank[j % 2][:], masked_in[0][:, at], ALU.add).then_inc(
                            s_done[j % 2], 1)
                        dve.wait_ge(s_done[j % 2], START + 2 * (2 * use) + j // 2 + 1)
                        dve.tensor_reduce(chunk_max[0][:, j:j + 1], probs[0][:, at], AX_X, ALU.max).then_inc(
                            first_max_done, 1)

                    def row_maximum(b, use, c, first=None):
                        for bank in range(2):
                            dve.wait_ge(s_done[bank], START + 2 * (2 * use + b) + 2)
                        if first is not None:
                            dve.wait_ge(first_max_done, START + GROUPS * (first + 1))
                        dve.tensor_reduce(row_max[b][:], chunk_max[b][:], AX_X, ALU.max).then_inc(max_done[b], 1)
                        dve.wait_ge(max_done[b], START + use + 1)
                        dve.tensor_scalar(neg_max[b][:], row_max[b][:], least[:, bass.ds(b * C + c, 1)], -2.0,
                                          ALU.max, ALU.mult).then_inc(neg_done[b], 1)

                    def prob_low(b, use, g):
                        dve.wait_ge(pT_high_done[g % 2], START + 2 * (2 * use + b) + g // 2 + 1)
                        low(pT_low[:, g * TPB:(g + 1) * TPB, :], t_bank[g % 2][:].rearrange("p (a n) -> p a n", a=TPB),
                            pT_high[:, g * TPB:(g + 1) * TPB, :]).then_inc(pT_low_done[g % 2], 1)

                    def denominator(b, use, c, ready):
                        dve.wait_ge(exp_done[b], START + GROUPS * (use + 1))
                        dve.tensor_reduce(row_total[b][:], chunk_sum[b][:], AX_X, ALU.add).then_inc(sum_done[b], 1)
                        dve.wait_ge(sum_done[b], START + use + 1)
                        dve.scalar_tensor_tensor(out=denom[b][:], in0=masked_exp[b][:],
                                                 scalar=zero_count[:, bass.ds(b * C + c, 1)], in1=row_total[b][:],
                                                 op0=ALU.mult, op1=ALU.add).then_inc(denom_done[b], 1)
                        ready(3)
                        dve.wait_ge(denom_done[b], START + use + 1)
                        dve.reciprocal(inv_denom[b][:], denom[b][:]).then_inc(inv_done[b], 1)

                    def add_head(b, use, c):
                        dve.wait_ge(o_full[b], START + use + 1)
                        dve.wait_ge(inv_done[b], START + use + 1)
                        mine = total[:, bass.ds(b * C + c, 1), :].rearrange("p o d -> p (o d)")
                        dve.scalar_tensor_tensor(out=mine, in0=o_bank[b][:, 0:D], scalar=inv_denom[b][:, 0:1], in1=mine,
                                                 op0=ALU.mult, op1=ALU.add).then_inc(o_half[b], 1)
                        dve.wait_ge(o_half[b], START + use + 1)
                        dve.scalar_tensor_tensor(out=mine, in0=o_bank[b][:, D:2 * D], scalar=inv_denom[b][:, 0:1],
                                                 in1=mine, op0=ALU.mult, op1=ALU.add).then_inc(o_done[b], 1)

                    def step(b, use, c, next_scores, next_queries):
                        if next_scores:
                            ready = lambda j: await_scores(1 - b, use + b, j)
                            score = lambda j: masked_scores(1 - b, use + b, j)
                        else:
                            ready = score = lambda j: None
                        prob_low(b, use, 0)
                        if next_scores:
                            dve.wait_ge(bias_in[1 - b], START + DMA * (use + b + 1))
                        ready(0)
                        prob_low(b, use, 1)
                        score(0)
                        ready(1)
                        prob_low(b, use, 2)
                        score(1)
                        if next_queries:
                            split_query_weights(use + 1)
                        ready(2)
                        prob_low(b, use, 3)
                        score(2)
                        denominator(b, use, c, ready)
                        score(3)
                        if next_scores:
                            row_maximum(1 - b, use + b, c + b)
                        if next_queries:
                            evacuate_queries(use + 1)
                        add_head(b, use, c)

                    dve.wait_ge(count_in, START + DMA)
                    dve.tensor_scalar(least[:], zero_count[:], 0.0, 0.5 * MASKED, ALU.is_gt, ALU.mult).then_inc(least_done, 1)
                    dve.tensor_scalar(least_tmp[:], zero_count[:], 0.0, NEVER, ALU.is_equal, ALU.mult).then_inc(
                        least_done, 1)
                    dve.wait_ge(least_done, START + 2)
                    dve.tensor_tensor(least[:], least[:], least_tmp[:], ALU.add).then_inc(least_done, 1)
                    dve.wait_ge(least_done, START + 3)
                    dve.wait_ge(total_in, START + DMA)
                    with dve.Fori(0, H) as h:
                        dve.wait_ge(xT_high_done, START + h + 1)
                        low(xT_low[:], halves(m_bank[0]), xT_high[:]).then_inc(xT_low_done, 1)
                        dve.wait_ge(wo_high_done, START + h + 1)
                        low(wo_low[:], wo_raw[:], wo_high[:]).then_inc(wo_low_done, 1)
                        split_keys_weights(h, 0, 0)
                        with dve.Fori(0, C // 2 - 1) as jj:
                            split_keys_weights(h, jj, 1)
                            evacuate_keys(h, jj, 0)
                            split_keys_weights(h, jj + 1, 0)
                            evacuate_keys(h, jj, 1)
                        split_keys_weights(h, C // 2 - 1, 1)
                        evacuate_keys(h, C // 2 - 1, 0)
                        evacuate_keys(h, C // 2 - 1, 1)
                        split_query_weights(h * C)
                        evacuate_queries(h * C)
                        for j in range(GROUPS):
                            first_masked_scores(h * C, j)
                        row_maximum(0, h * C, 0, h)
                        with dve.Fori(0, C - 1) as c:
                            step(0, h * C + c, c, True, True)
                            step(1, h * C + c, c, True, False)
                        step(0, h * C + C - 1, C - 1, True, False)
                        step(1, h * C + C - 1, C - 1, False, False)
                    for b in range(2):
                        dve.wait_ge(o_done[b], START + H * C)
                    for i in range(T // TPB // 2):
                        for q in range(2):
                            norm_stats(dve, norm2, i, q, lambda a: total[:, bass.ds((2 * i + q) * TPB + a, 1), :]
                                       .rearrange("p o d -> p (o d)"))
                        for q in range(2):
                            tile = lambda a: total[:, bass.ds((2 * i + q) * TPB + a, 1), :].rearrange(
                                "p o d -> p (o d)")
                            norm_apply(dve, norm2, i, q, tile, tile)

        clear_spent()

        with ExitStack() as s5:
            xb = sb(s5, "xb", [P, T, D])
            scaled = sb(s5, "scaled", [P, T, D])
            bias_all = sb(s5, "bias_all", [P, D])
            degree = sb(s5, "degree", [P, T])
            root = sb(s5, "root", [P, T])
            inv_root = sb(s5, "inv_root", [P, T])
            rows = [sb(s5, f"adj_rows{k}", [P, N]) for k in range(2)]
            rows_in = sems(s5, "adj_rows_in")
            with ExitStack() as s5a:
                spare = [s5a.enter_context(nc.psum_tensor(f"proj3_bank{g}", [P, BANK], F32)) for g in range(2)]
                proj = Projection(s5a, "p3", spare, w3, scaled)
                xb_in = sem(s5a, "xb_in")
                bias_in3 = sem(s5a, "bias_in3")
                biased = sem(s5a, "biased")
                degree_done = sem(s5a, "degree_done")
                root_done = sem(s5a, "root_done")
                inv_root_done = sem(s5a, "inv_root_done")
                with next_block() as block:
                    @block.sync
                    def _(sp):
                        start(sp, 0, 5)
                        proj.load_weight(sp)
                        with sp.Fori(0, PAIRS) as i:
                            for k in range(2):
                                proj.load(sp, i, k, x2_scratch[bass.ds((2 * i + k) * P, P), :])
                        sp.dma_start(xb[:], x2_scratch.rearrange("(t p) d -> p t d", p=P)).then_inc(xb_in, DMA)
                        sp.dma_start(bias_all[:], bias.partition_broadcast(P)).then_inc(bias_in3, DMA)

                    @block.gpsimd
                    def _(pool):
                        start(pool, 1, 5)
                        pool.wait_ge(xb_in, START + DMA)
                        pool.wait_ge(bias_in3, START + DMA)
                        for t in range(T):
                            pool.tensor_tensor(xb[:, t, :], xb[:, t, :], bias_all[:], ALU.add).then_inc(biased, 1)

                    @block.tensor
                    def _(pe):
                        start(pe, 2, 5)
                        pe.wait_ge(proj.w_low_done, START + 1)
                        proj.transposes(pe, 0, 0)
                        for i, k in ((0, 1),):
                            proj.transposes(pe, i, k)
                            proj.products(pe, 0, 0)
                        with pe.Fori(1, PAIRS) as i:
                            proj.transposes(pe, i, 0)
                            proj.products(pe, i - 1, 1)
                            proj.transposes(pe, i, 1)
                            proj.products(pe, i, 0)
                        proj.products(pe, PAIRS - 1, 1)

                    @block.scalar
                    def _(act):
                        start(act, 3, 5)
                        act.wait_ge(degree_done, START + 1)
                        act.activation(root[:], degree[:], ACT.Sqrt).then_inc(root_done, 1)
                        proj.split_weight_high(act)
                        act.wait_ge(inv_root_done, START + 1)
                        proj.high(act, 0, 0)
                        with act.Fori(0, PAIRS - 1) as i:
                            proj.high(act, i, 1)
                            proj.evacuate(act, i, 0, inv_root)
                            proj.high(act, i + 1, 0)
                            proj.evacuate(act, i, 1, inv_root)
                        proj.high(act, PAIRS - 1, 1)
                        proj.evacuate(act, PAIRS - 1, 0, inv_root)
                        proj.evacuate(act, PAIRS - 1, 1, inv_root)

                    @block.vector
                    def _(dve):
                        start(dve, 4, 5)
                        dve.tensor_tensor(degree[:], col_sum[:, :, 0], col_sum[:, :, 1], ALU.add).then_inc(
                            degree_done, 1)
                        dve.wait_ge(root_done, START + 1)
                        dve.reciprocal(inv_root[:], root[:]).then_inc(inv_root_done, 1)
                        proj.split_weight_low(dve)
                        with dve.Fori(0, PAIRS) as i:
                            for k in range(2):
                                proj.low(dve, i, k)

            with ExitStack() as s5b:
                acc = s5b.enter_context(nc.psum_tensor("acc3", [P, GROUPS, K, BANK], F32))
                prop = Propagation(s5b, "l3", acc)
                with next_block() as block:
                    @block.sync
                    def _(sp):
                        start(sp, 0, 4)
                        with sp.Fori(0, PAIRS) as i:
                            for k in range(2):
                                for u in range(2):
                                    sp.wait_ge(prop.mov_low_done[u], START + 2 * i)
                                sp.dma_start(rows[k][:], adj[bass.ds((2 * i + k) * P, P), :]).then_inc(
                                    rows_in[k], DMA)
                        out_tiles = out.rearrange("(t p) d -> p t d", p=P)
                        with sp.Fori(0, GROUPS // 2) as i:
                            for q in range(2):
                                sp.wait_ge(prop.norm.normed[q], START + TPB * (i + 1))
                                sp.dma_start(out_tiles[:, bass.ds((2 * i + q) * TPB, TPB), :], prop.z[q][:]).then_inc(
                                    prop.stored[q], DMA)
                        for q in range(2):
                            sp.wait_ge(prop.stored[q], START + DMA * (GROUPS // 2))

                    @block.tensor
                    def _(pe):
                        start(pe, 1, 4)
                        prop.products(pe)
                        for j in range(GROUPS):
                            prop.turn_back(pe, j)

                    @block.scalar
                    def _(act):
                        start(act, 2, 4)
                        act.activation(deviation[:, 0, 0:1], eps_col[:], ACT.Sqrt)
                        with act.Fori(0, PAIRS) as i:
                            for k in range(2):
                                prop.left_high_part(act, i, k, scaled[:, bass.ds(2 * i + k, 1), :].rearrange(
                                    "p o d -> p (o d)"))
                                act.wait_ge(rows_in[k], START + DMA * (i + 1))
                                for u in range(2):
                                    prop.high_part(act, i, k, u, rows[k][:, u * HALF:(u + 1) * HALF])
                        with act.Fori(0, GROUPS // 2) as i:
                            for q in range(2):
                                prop.turn_in(act, i, q)
                            for q in range(2):
                                norm_root(act, prop.norm, i, q)

                    @block.vector
                    def _(dve):
                        start(dve, 3, 4)
                        with dve.Fori(0, PAIRS) as i:
                            for k in range(2):
                                prop.left_low_part(dve, i, k, scaled[:, bass.ds(2 * i + k, 1), :].rearrange(
                                    "p o d -> p (o d)"))
                                for u in range(2):
                                    prop.low_part(dve, i, k, u, rows[k][:, u * HALF:(u + 1) * HALF])
                        for i in range(GROUPS // 2):
                            for q in range(2):
                                dve.wait_ge(prop.stored[q], START + DMA * i)
                                prop.residual(dve, i, q, lambda t: inv_root[:, bass.ds(t, 1)],
                                              lambda t: xb[:, bass.ds(t, 1), :].rearrange("p o d -> p (o d)"))
                                norm_stats(dve, prop.norm, i, q, lambda a: prop.z[q][:, a, :])
                            for q in range(2):
                                norm_apply(dve, prop.norm, i, q, lambda a: prop.z[q][:, a, :],
                                           lambda a: prop.z[q][:, a, :])


_INS = ['x', 'adj', 'L0_gnn_t', 'L0_gnn_weight', 'L2_gnn_Wq', 'L2_gnn_Wk', 'L2_gnn_Wv', 'L2_gnn_Wout',
        'L3_gnn_weight', 'L3_gnn_bias']
_OUTS = [((2048, 256), 'float32')]


def kernel(**inputs):
    import numpy as _np
    import concourse.bacc as _bacc
    from concourse import mybir as _mybir
    from concourse.bass_utils import run_bass_kernel_spmd as _run

    nc = _bacc.Bacc("TRN2", target_bir_lowering=False, num_devices=1)
    arrays, args = {}, []
    for name in _INS:
        a = _np.ascontiguousarray(inputs[name])
        arrays[f"in_{name}_dram"] = a
        args.append(nc.dram_tensor(f"in_{name}_dram", a.shape, _mybir.dt.from_np(a.dtype), kind="ExternalInput").ap())
    for i, (shape, dtype) in enumerate(_OUTS):
        dt = _mybir.dt.from_np(_np.dtype(dtype))
        args.append(nc.dram_tensor(f"out_{i}_dram", shape, dt, kind="ExternalOutput").ap())
    graph_layers(nc, *args)
    r = _run(nc, [arrays], core_ids=[0])
    got = tuple(r.results[0][f"out_{i}_dram"] for i in range(len(_OUTS)))
    return got[0]
```

```python
from contextlib import ExitStack

import concourse.bass as bass
from concourse import mybir

ALU = mybir.AluOpType
ACT = mybir.ActivationFunctionType
AX_X = mybir.AxisListType.X
F32 = mybir.dt.float32
F32R = mybir.dt.float32r
BF16 = mybir.dt.bfloat16
U8 = mybir.dt.uint8

P = 128
BANK = 512
LN_EPS = 1e-5
NORM_EPS = 1e-12
MASKED = -1.0e6
NEVER = -2.0 ** 100
DMA = 16
START = 1


def plain(ap):
    return ap.bitcast(F32)


def graph_layers(nc, x, adj, mix, w0, wq, wk, wv, wout, w3, bias, out):
    N, D = x.shape
    T = N // P
    K = D // P
    H = wq.shape[1] // D
    C = H
    R = N // H
    PAIRS = T // 2
    HALF = N // 2
    GROUPS = N // BANK
    TPB = BANK // P
    assert K == 2 and R == 2 * P and C * R == N and C == PAIRS and 2 * D == BANK

    bias_scratch = nc.dram_tensor("bias_scratch", (N, N), F32, kind="Internal").ap()
    wvt_scratch = nc.dram_tensor("wvt_scratch", (C, P, K, D), F32, kind="Internal").ap()
    x1_scratch = nc.dram_tensor("x1_scratch", (N, D), F32, kind="Internal").ap()
    x2_scratch = nc.dram_tensor("x2_scratch", (N, D), F32, kind="Internal").ap()
    zeros_scratch = nc.dram_tensor("zeros_scratch", (N, 1), F32, kind="Internal").ap()

    whole = ExitStack()

    def sb(scope, name, shape, dtype=F32):
        return scope.enter_context(nc.sbuf_tensor(name, shape, dtype))

    spent, fresh, of_block = [], [], []

    def sem(scope, name):
        made = scope.enter_context(nc.semaphore(name))
        spent.append(made)
        fresh.append(made)
        return made

    def next_block():
        of_block[:] = fresh
        fresh.clear()
        return nc.Block()

    def start(engine, n, of):
        for s in of_block[n::of]:
            engine.sem_inc(s, START)

    def clear_spent():
        numbers = sorted(s.num for s in spent)
        with nc.Block() as block:
            @block.gpsimd
            def _(pool):
                start = numbers[0]
                for n, after in zip(numbers, numbers[1:] + [None]):
                    if after != n + 1:
                        pool.sem_clear(range(start, n + 1))
                        start = after
        spent.clear()

    def sems(scope, name, n=2):
        return [sem(scope, f"{name}{i}") for i in range(n)]

    with whole:
        ident = sb(whole, "ident", [P, P])
        eps_col = sb(whole, "eps_col", [P, 1])
        masked_col = sb(whole, "masked_col", [P, 1])

        class Projection:
            def __init__(self, scope, tag, xT_bank, y_bank, w_dram, y_reads):
                self.xT_bank, self.y_bank, self.w_dram = xT_bank, y_bank, w_dram
                self.y_reads = y_reads
                self.w = sb(scope, f"{tag}_w", [P, K, D])
                self.w_high = sb(scope, f"{tag}_w_high", [P, K, D], F32R)
                self.w_low = sb(scope, f"{tag}_w_low", [P, K, D], F32R)
                self.xT_high = [sb(scope, f"{tag}_xT_high{k}", [P, K, P], F32R) for k in range(2)]
                self.xT_low = [sb(scope, f"{tag}_xT_low{k}", [P, K, P], F32R) for k in range(2)]
                self.w_in = sem(scope, f"{tag}_w_in")
                self.w_high_done = sem(scope, f"{tag}_w_high_done")
                self.w_low_done = sem(scope, f"{tag}_w_low_done")
                self.xT_full = sems(scope, f"{tag}_xT_full")
                self.high_done = sems(scope, f"{tag}_high_done")
                self.low_done = sems(scope, f"{tag}_low_done")
                self.y_full = sems(scope, f"{tag}_y_full")
                self.y_high_done = sems(scope, f"{tag}_y_high_done")
                self.y_read = sems(scope, f"{tag}_y_read")

            def load_weight(self, sp):
                sp.dma_start(self.w[:], self.w_dram.rearrange("(k p) n -> p k n", p=P)).then_inc(self.w_in, DMA)

            def split_weight_high(self, act):
                act.wait_ge(self.w_in, START + DMA)
                act.activation(self.w_high[:], self.w[:], ACT.Copy).then_inc(self.w_high_done, 1)

            def split_weight_low(self, dve):
                dve.wait_ge(self.w_high_done, START + 1)
                dve.tensor_tensor(self.w_low[:], self.w[:], plain(self.w_high[:]), ALU.subtract).then_inc(
                    self.w_low_done, 1)

            def transposes(self, pe, i, k, tile):
                pe.wait_ge(self.low_done[k], START + i)
                for kk in range(K):
                    mm = pe.transpose(self.xT_bank[k][:, kk * P:(kk + 1) * P], tile[:, kk * P:(kk + 1) * P], ident[:])
                mm.then_inc(self.xT_full[k], 1)

            def turned(self, k):
                return self.xT_bank[k][:, 0:D].rearrange("p (k n) -> p k n", k=K)

            def high(self, act, i, k):
                act.wait_ge(self.xT_full[k], START + i + 1)
                act.wait_ge(self.y_full[k], START + i)
                act.activation(self.xT_high[k][:], self.turned(k), ACT.Copy).then_inc(self.high_done[k], 1)

            def low(self, dve, i, k):
                dve.wait_ge(self.high_done[k], START + i + 1)
                dve.tensor_tensor(self.xT_low[k][:], self.turned(k), plain(self.xT_high[k][:]),
                                  ALU.subtract).then_inc(self.low_done[k], 1)

            def products(self, pe, i, k):
                pe.wait_ge(self.low_done[k], START + i + 1)
                pe.wait_ge(self.y_read[k], START + self.y_reads * i)
                for kk in range(K):
                    for n, (a, b) in enumerate(((self.xT_high[k], self.w_high), (self.xT_high[k], self.w_low),
                                                (self.xT_low[k], self.w_high))):
                        mm = pe.matmul(self.y_bank[k][:, 0:D], a[:, kk, :], b[:, kk, :], start=(kk == 0 and n == 0),
                                       stop=(kk == K - 1 and n == 2))
                mm.then_inc(self.y_full[k], 1)

            def y_high(self, act, i, k, dst, scale=1.0):
                act.wait_ge(self.y_full[k], START + i + 1)
                act.activation(dst, self.y_bank[k][:, 0:D], ACT.Copy, scale=scale).then_inc(self.y_high_done[k], 1)

            def y_low(self, dve, i, k, dst, high, scale=1.0):
                dve.wait_ge(self.y_high_done[k], START + i + 1)
                dve.scalar_tensor_tensor(out=dst, in0=self.y_bank[k][:, 0:D], scalar=scale, in1=plain(high),
                                         op0=ALU.mult, op1=ALU.subtract).then_inc(self.y_read[k], 1)

        def part_of(right, t, part):
            return right[:, bass.ds(t, 1), part, :].rearrange("p o d -> p (o d)")

        class RowProducts:
            def __init__(self, scope, tag, right, o_read):
                self.right, self.o_read = right, o_read
                self.high_part = [sb(scope, f"{tag}_high{b}", [P, TPB, P], F32R) for b in range(2)]
                self.low_part = [sb(scope, f"{tag}_low{b}", [P, TPB, P], F32R) for b in range(2)]
                self.turn_bank, self.o_bank = (
                    [scope.enter_context(nc.psum_tensor(f"{tag}_{n}_bank{b}", [P, BANK], F32)) for b in range(2)]
                    for n in ("turn", "o"))
                self.turned = sems(scope, f"{tag}_turned")
                self.high_done = sems(scope, f"{tag}_high_done")
                self.low_done = sems(scope, f"{tag}_low_done")
                self.o_full = sems(scope, f"{tag}_o_full")

            def uses(self, i, k, g):
                return 2 * (2 * i + k) + g // 2

            def turns(self, pe, i, k, g, cols):
                b = g % 2
                pe.wait_ge(self.low_done[b], START + self.uses(i, k, g))
                for a in range(TPB):
                    mm = pe.transpose(self.turn_bank[b][:, a * P:(a + 1) * P], cols(a), ident[:])
                mm.then_inc(self.turned[b], 1)

            def bank(self, b):
                return self.turn_bank[b][:].rearrange("p (a n) -> p a n", a=TPB)

            def high(self, act, i, k, g):
                b = g % 2
                act.wait_ge(self.turned[b], START + self.uses(i, k, g) + 1)
                act.activation(self.high_part[b][:], self.bank(b), ACT.Copy).then_inc(self.high_done[b], 1)

            def low(self, dve, i, k, g):
                b = g % 2
                dve.wait_ge(self.high_done[b], START + self.uses(i, k, g) + 1)
                dve.tensor_tensor(self.low_part[b][:], self.bank(b), plain(self.high_part[b][:]),
                                  ALU.subtract).then_inc(self.low_done[b], 1)

            def weigh(self, pe, i, k, g):
                b = g % 2
                pe.wait_ge(self.low_done[b], START + self.uses(i, k, g) + 1)
                if g == 0:
                    pe.wait_ge(self.o_read[k], START + i)
                for a in range(TPB):
                    m = g * TPB + a
                    for n, (left, part) in enumerate(((self.high_part[b], 0), (self.high_part[b], 1),
                                                      (self.low_part[b], 0))):
                        mm = pe.matmul(self.o_bank[k][:, 0:D], left[:, a, :], self.right[:, m, part, :],
                                       start=(m == 0 and n == 0), stop=(m == T - 1 and n == 2))
                if g == GROUPS - 1:
                    mm.then_inc(self.o_full[k], 1)

            def run(self, pe, cols, awaited, before_weigh=None):
                def turns(i, k, g):
                    awaited(i, k, g)
                    self.turns(pe, i, k, g, lambda a: cols(k, (g * TPB + a) * P))

                def tile(i, k, more, start_of=None):
                    for g in range(GROUPS):
                        if start_of is not None:
                            start_of(g)
                        self.weigh(pe, i, k, g)
                        if g < 2:
                            turns(i, k, g + 2)
                        elif more:
                            turns(i + k, 1 - k, g - 2)

                turns(0, 0, 0)
                turns(0, 0, 1)
                tile(0, 0, True, before_weigh)
                tile(0, 1, True)
                with pe.Fori(1, PAIRS - 1) as i:
                    tile(i, 0, True)
                    tile(i, 1, True)
                tile(PAIRS - 1, 0, True)
                tile(PAIRS - 1, 1, False)

        class TileNorm:
            def __init__(self, scope, tag):
                self.z = [sb(scope, f"{tag}_z{k}", [P, D]) for k in range(2)]
                self.stats, self.mean_var, self.deviation, self.inv_dev, self.shift = (
                    [sb(scope, f"{tag}_{n}{k}", [P, w]) for k in range(2)]
                    for n, w in (("stats", 6), ("mean_var", 2), ("deviation", 1), ("inv_dev", 1), ("shift", 1)))
                self.z_done, self.stats_done, self.var_done, self.dev_done, self.inv_done, self.shift_done, \
                    self.normed = (sems(scope, f"{tag}_{n}") for n in (
                        "z_done", "stats_done", "var_done", "dev_done", "inv_done", "shift_done", "normed"))

            def residual(self, dve, i, k, products, scale, x):
                dve.wait_ge(products.o_full[k], START + i + 1)
                dve.wait_ge(self.normed[k], START + i)
                dve.scalar_tensor_tensor(out=self.z[k][:], in0=products.o_bank[k][:, 0:D], scalar=scale, in1=x,
                                         op0=ALU.mult, op1=ALU.add).then_inc(self.z_done[k], 1)
                dve.wait_ge(self.z_done[k], START + i + 1)
                dve.bn_stats(self.stats[k][:], self.z[k][:]).then_inc(self.stats_done[k], 1)

            def await_stats(self, dve, i, k):
                dve.wait_ge(self.stats_done[k], START + i + 1)

            def variance(self, dve, i, k):
                dve.bn_aggr(self.mean_var[k][:], self.stats[k][:]).then_inc(self.var_done[k], 1)

            def root(self, act, i, k):
                act.wait_ge(self.var_done[k], START + i + 1)
                act.activation(self.deviation[k][:], self.mean_var[k][:, 1:2], ACT.Sqrt, bias=eps_col[:, 0:1]
                               ).then_inc(self.dev_done[k], 1)

            def scale_and_shift(self, dve, i, k):
                dve.wait_ge(self.dev_done[k], START + i + 1)
                dve.reciprocal(self.inv_dev[k][:], self.deviation[k][:]).then_inc(self.inv_done[k], 1)
                dve.wait_ge(self.inv_done[k], START + i + 1)
                dve.scalar_tensor_tensor(out=self.shift[k][:], in0=self.mean_var[k][:, 0:1], scalar=-1.0,
                                         in1=self.inv_dev[k][:], op0=ALU.mult, op1=ALU.mult).then_inc(
                    self.shift_done[k], 1)

            def apply(self, act, i, k, dst):
                act.wait_ge(self.shift_done[k], START + i + 1)
                act.activation(dst, self.z[k][:], ACT.Identity, bias=self.shift[k][:, 0:1],
                               scale=self.inv_dev[k][:, 0:1]).then_inc(self.normed[k], 1)

        front = ExitStack()
        with front:
            half_rows = [[sb(front, f"half_rows{k}{u}", [P, HALF]) for u in range(2)] for k in range(2)]
            xa = sb(front, "xa", [P, T, D])
            support, x0_parts = (sb(front, n, [P, T, 2, D], F32R) for n in ("support", "x0_parts"))
            positives = sb(front, "positives", [P, T, 2])
            head = sb(front, "head", [P, T])
            masked = [sb(front, f"masked{n}", [P, HALF]) for n in range(4)]
            zero_sum = sb(front, "zero_sum", [P, T])
            masked_stored = sems(front, "masked_stored", 4)
            zeros_stored = sem(front, "zeros_stored")
            mix_col = sb(front, "mix_col", [P, 1])
            one_less_mix = sb(front, "one_less_mix", [P, 1])
            half_in = [sems(front, f"half_in{k}_") for k in range(2)]
            tile_of = lambda array, t: array[:, bass.ds(t, 1), :].rearrange("p o d -> p (o d)")
            adj_part = lambda k, at, n: half_rows[k][at // HALF][:, at % HALF:at % HALF + n]

            def load_half(sp, i, k, u):
                sp.dma_start(half_rows[k][u][:], adj[bass.ds((2 * i + k) * P, P), u * HALF:(u + 1) * HALF]).then_inc(
                    half_in[k][u], DMA)

            with ExitStack() as s1:
                wv_rows = [sb(s1, f"wv_rows{k}", [P, K, D]) for k in range(2)]
                wvt = [sb(s1, f"wvt{k}", [P, K, D]) for k in range(2)]
                xT_bank, y_bank, wvt_bank = (
                    [s1.enter_context(nc.psum_tensor(f"{n}_bank{k}", [P, BANK], F32)) for k in range(2)]
                    for n in ("xT", "y", "wvt"))
                proj = Projection(s1, "sup", xT_bank, y_bank, w0, 2)
                ident_zeroed = sem(s1, "ident_zeroed")
                consts_done = sem(s1, "consts_done")
                mix_in = sem(s1, "mix_in")
                mix_done = sem(s1, "mix_done")
                xa_in = sems(s1, "xa_in", GROUPS)
                wv_in = sems(s1, "wv_in")
                wvt_full = sems(s1, "wvt_full")
                wvt_ready = sems(s1, "wvt_ready")
                wvt_stored = sems(s1, "wvt_stored")

                with next_block() as block:
                    @block.sync
                    def _(sp):
                        start(sp, 0, 5)
                        proj.load_weight(sp)
                        for g in range(GROUPS):
                            tiles = slice(g * TPB, (g + 1) * TPB)
                            sp.dma_start(xa[:, tiles, :], x[g * BANK:(g + 1) * BANK, :].rearrange(
                                "(t p) d -> p t d", p=P)).then_inc(xa_in[g], DMA)
                        sp.dma_start(mix_col[:], mix.rearrange("(a b) -> a b", a=1).broadcast_to([P, 1])).then_inc(
                            mix_in, DMA)
                        def load_wv(i, k):
                            sp.wait_ge(wvt_full[k], START + i)
                            sp.dma_start(wv_rows[k][:], wv[:, bass.ds((2 * i + k) * D, D)].rearrange(
                                "(k p) d -> p k d", p=P)).then_inc(wv_in[k], DMA)
                        for k in range(2):
                            load_wv(0, k)
                        for k in range(2):
                            for u in range(2):
                                load_half(sp, 0, k, u)
                        with sp.Fori(1, C // 2) as i:
                            for k in range(2):
                                load_wv(i, k)

                    @block.gpsimd
                    def _(pool):
                        start(pool, 1, 5)
                        pool.memset(ident[:], 0.0).then_inc(ident_zeroed, 1)
                        pool.memset(eps_col[:], LN_EPS).then_inc(consts_done, 1)
                        pool.memset(masked_col[:], MASKED).then_inc(consts_done, 1)
                        pool.wait_ge(ident_zeroed, START + 1)
                        pool.affine_select(out=ident[:], in_=ident[:], compare_op=ALU.not_equal, fill=1.0, base=0,
                                           pattern=[[-1, P]], channel_multiplier=1).then_inc(consts_done, 1)

                    @block.tensor
                    def _(pe):
                        start(pe, 2, 5)
                        def turn_values(i, k):
                            pe.wait_ge(wv_in[k], START + DMA * (i + 1))
                            pe.wait_ge(wvt_ready[k], START + i)
                            for dk in range(K):
                                for kk in range(K):
                                    mm = pe.transpose(wvt_bank[k][:, dk * D + kk * P:dk * D + (kk + 1) * P],
                                                      wv_rows[k][:, kk, dk * P:(dk + 1) * P], ident[:])
                            mm.then_inc(wvt_full[k], 1)

                        pe.wait_ge(consts_done, START + 3)
                        pe.wait_ge(xa_in[0], START + DMA)
                        proj.transposes(pe, 0, 0, xa[:, 0, :])
                        proj.transposes(pe, 0, 1, xa[:, 1, :])
                        pe.wait_ge(proj.w_low_done, START + 1)
                        proj.products(pe, 0, 0)
                        for i in range(1, PAIRS):
                            for k in range(2):
                                if (2 * i + k) % TPB == 0:
                                    pe.wait_ge(xa_in[(2 * i + k) // TPB], START + DMA)
                                proj.transposes(pe, i, k, xa[:, 2 * i + k, :])
                                proj.products(pe, i - 1 + k, 1 - k)
                            if i > 1:
                                turn_values((i - 2) // 2, i % 2)
                        proj.products(pe, PAIRS - 1, 1)
                        for k in range(2):
                            turn_values(C // 2 - 1, k)

                    @block.scalar
                    def _(act):
                        start(act, 3, 5)
                        act.wait_ge(consts_done, START + 3)
                        proj.split_weight_high(act)
                        proj.high(act, 0, 0)
                        proj.high(act, 0, 1)
                        proj.y_high(act, 0, 0, support[:, 0, 0, :])
                        def keep_values(i, k):
                            act.wait_ge(wvt_full[k], START + i + 1)
                            act.wait_ge(wvt_stored[k], START + DMA * i)
                            act.activation(wvt[k][:], wvt_bank[k][:].rearrange("p (k d) -> p k d", k=K),
                                           ACT.Copy).then_inc(wvt_ready[k], 1)

                        def store_values(i, k):
                            act.wait_ge(wvt_ready[k], START + i + 1)
                            act.dma_start(wvt_scratch[bass.ds(2 * i + k, 1)].rearrange("o p k d -> (o p) k d"),
                                          wvt[k][:]).then_inc(wvt_stored[k], DMA)

                        for i in range(1, PAIRS):
                            for k in range(2):
                                proj.high(act, i, k)
                                proj.y_high(act, i - 1 + k, 1 - k, part_of(support, 2 * (i - 1 + k) + 1 - k, 0))
                            if i > 1:
                                keep_values((i - 2) // 2, i % 2)
                                store_values((i - 2) // 2, i % 2)
                        proj.y_high(act, PAIRS - 1, 1, support[:, T - 1, 0, :])
                        for k in range(2):
                            keep_values(C // 2 - 1, k)
                            store_values(C // 2 - 1, k)
                        for k in range(2):
                            act.wait_ge(wvt_stored[k], START + DMA * (C // 2))

                    @block.vector
                    def _(dve):
                        start(dve, 4, 5)
                        proj.split_weight_low(dve)
                        dve.wait_ge(mix_in, START + DMA)
                        dve.tensor_scalar(one_less_mix[:], mix_col[:], -1.0, 1.0, ALU.mult, ALU.add).then_inc(
                            mix_done, 1)

                        def split_support(i, k):
                            t = 2 * i + k
                            proj.y_low(dve, i, k, part_of(support, t, 1), part_of(support, t, 0))
                            mine = tile_of(xa, t)
                            dve.scalar_tensor_tensor(out=mine, in0=y_bank[k][:, 0:D], scalar=one_less_mix[:, 0:1],
                                                     in1=mine, op0=ALU.mult, op1=ALU.add).then_inc(proj.y_read[k], 1)

                        proj.low(dve, 0, 0)
                        proj.low(dve, 0, 1)
                        dve.wait_ge(mix_done, START + 1)
                        split_support(0, 0)
                        with dve.Fori(1, PAIRS) as i:
                            for k in range(2):
                                proj.low(dve, i, k)
                                split_support(i - 1 + k, 1 - k)
                        split_support(PAIRS - 1, 1)

            with ExitStack() as s2:
                norm = TileNorm(s2, "l0")
                rows = RowProducts(s2, "l0", support, norm.z_done)
                zeros = sb(s2, "zeros", [P, T, 2])
                positive_sum = sb(s2, "positive_sum", [P, T])
                length = sb(s2, "length", [P, T])
                positive_mark, zero_mark = (
                    [sb(s2, f"{n}_mark{u}", [P, HALF], BF16) for u in range(2)]
                    for n in ("positive", "zero"))
                floor_done = sems(s2, "floor_done", 4)
                zeros_counted = sems(s2, "zeros_counted", 4)
                positives_counted = sems(s2, "positives_counted", 4)
                masked_done = sems(s2, "masked_done", 4)
                x0_high_done = sems(s2, "x0_high_done")
                x0_low_done = sems(s2, "x0_low_done")
                small = sem(s2, "small")
                length_done = sem(s2, "length_done")
                zero_sum_done = sem(s2, "zero_sum_done")
                by_c = lambda ap: ap.rearrange("p (r c) -> p c r", c=C)
                grouped = lambda ap: ap.rearrange("p (c r) -> p c r", c=C)

                with next_block() as block:
                    @block.sync
                    def _(sp):
                        start(sp, 0, 5)
                        def store(i, k, u):
                            n = 2 * k + u
                            dst = bias_scratch[bass.ds((2 * i + k) * P, P), :].rearrange("n (c r) -> n c r", c=C)
                            sp.wait_ge(masked_done[n], START + i + 1)
                            sp.dma_start(dst[:, :, u * P:(u + 1) * P], grouped(masked[n][:])).then_inc(
                                masked_stored[n], DMA)

                        def load_next(i, k, u):
                            sp.wait_ge(positives_counted[2 * k + u], START + i + 1)
                            load_half(sp, i + 1, k, u)

                        with sp.Fori(0, PAIRS - 1) as i:
                            for k in range(2):
                                for u in range(2):
                                    store(i, k, u)
                                    load_next(i, k, u)
                        for k in range(2):
                            for u in range(2):
                                store(PAIRS - 1, k, u)
                        for k in range(2):
                            for u in range(2):
                                sp.wait_ge(positives_counted[2 * k + u], START + PAIRS)
                                sp.dma_start(half_rows[k][u][:], adj[k * P:(k + 1) * P, u * HALF:(u + 1) * HALF]
                                             ).then_inc(half_in[k][u], DMA)
                        sp.wait_ge(zero_sum_done, START + 1)
                        sp.dma_start(zeros_scratch.rearrange("(t p) o -> p t o", p=P), zero_sum[:].rearrange(
                            "p (t o) -> p t o", o=1), allow_slow_non_contiguous=True).then_inc(zeros_stored, DMA)

                    @block.gpsimd
                    def _(pool):
                        start(pool, 1, 5)
                        def await_x0(i, k):
                            pool.wait_ge(x0_high_done[k], START + i + 1)

                        def low_x0(i, k):
                            t = 2 * i + k
                            pool.tensor_tensor(part_of(x0_parts, t, 1), tile_of(xa, t), plain(part_of(x0_parts, t, 0)),
                                               ALU.subtract).then_inc(x0_low_done[k], 1)

                        def pair(i, first):
                            for k in range(2):
                                for u in range(2):
                                    n = 2 * k + u
                                    pool.wait_ge(floor_done[n], START + i + 1)
                                    pool.wait_ge(zeros_counted[n], START + i + 1)
                                    if u == 1 and not first:
                                        await_x0(i - 1, k)
                                    pool.tensor_tensor(grouped(masked[n][:]), grouped(masked[n][:]),
                                                       by_c(half_rows[k][u][:]), ALU.add).then_inc(masked_done[n], 1)
                                if not first:
                                    low_x0(i - 1, k)

                        pair(0, True)
                        with pool.Fori(1, PAIRS) as i:
                            pair(i, False)
                        for k in range(2):
                            await_x0(PAIRS - 1, k)
                            low_x0(PAIRS - 1, k)

                    @block.tensor
                    def _(pe):
                        start(pe, 2, 5)
                        def awaited(i, k, g):
                            if g % 2 == 0:
                                pe.wait_ge(half_in[k][g // 2], START + DMA * (i + 1))
                        rows.run(pe, lambda k, at: adj_part(k, at, P), awaited)

                    @block.scalar
                    def _(act):
                        start(act, 3, 5)
                        act.activation(norm.deviation[0][:], eps_col[:], ACT.Sqrt)

                        def count_zeros(i, k, u):
                            n = 2 * k + u
                            act.wait_ge(floor_done[n], START + i + 1)
                            if k == 0:
                                act.wait_ge(zeros_counted[2 + u], START + i)
                            else:
                                act.wait_ge(zeros_counted[u], START + i + 1)
                            act.activation(zero_mark[u][:], masked[n][:], ACT.Copy, scale=1.0 / NEVER,
                                           accum_out=zeros[:, bass.ds(2 * i + k, 1), u:u + 1].rearrange(
                                               "p o u -> p (o u)")).then_inc(zeros_counted[n], 1)

                        def make_x0(i, k):
                            t = 2 * i + k
                            norm.apply(act, i, k, tile_of(xa, t))
                            act.wait_ge(norm.normed[k], START + i + 1)
                            act.activation(part_of(x0_parts, t, 0), tile_of(xa, t), ACT.Copy).then_inc(
                                x0_high_done[k], 1)

                        def tile(i, k, first=False):
                            rows.high(act, i, k, 0)
                            rows.high(act, i, k, 1)
                            if not first:
                                make_x0(i - 1, k)
                            rows.high(act, i, k, 2)
                            count_zeros(i, k, 0)
                            rows.high(act, i, k, 3)
                            if not (first and k == 0):
                                norm.root(act, i - 1 + k, 1 - k)
                            count_zeros(i, k, 1)

                        for k in range(2):
                            tile(0, k, first=True)
                        with act.Fori(1, PAIRS) as i:
                            for k in range(2):
                                tile(i, k)
                        act.wait_ge(small, START + 1)
                        act.activation(length[:], positive_sum[:], ACT.Sqrt).then_inc(length_done, 1)
                        make_x0(PAIRS - 1, 0)
                        norm.root(act, PAIRS - 1, 1)
                        make_x0(PAIRS - 1, 1)

                    @block.vector
                    def _(dve):
                        start(dve, 4, 5)
                        def count_positives(i, k, u):
                            t = 2 * i + k
                            dve.wait_ge(half_in[k][u], START + DMA * (i + 1))
                            dve.wait_ge(positives_counted[2 * (1 - k) + u], START + i + k)
                            dve.tensor_scalar(positive_mark[u][:], half_rows[k][u][:], 0.0, 0.0, ALU.is_gt,
                                              ALU.add, accum_out=positives[:, bass.ds(t, 1), u:u + 1].rearrange(
                                                  "p o u -> p (o u)")).then_inc(positives_counted[2 * k + u], 1)

                        def make_floor(i, k, u):
                            n = 2 * k + u
                            dve.wait_ge(masked_stored[n], START + DMA * i)
                            dve.wait_ge(half_in[k][u], START + DMA * (i + 1))
                            dve.tensor_scalar(grouped(masked[n][:]), by_c(half_rows[k][u][:]), 0.0, NEVER, ALU.is_equal, ALU.mult).then_inc(floor_done[n], 1)

                        def residual(i, k):
                            norm.residual(dve, i, k, rows, mix_col[:, 0:1], tile_of(xa, 2 * i + k))

                        def tile(i, k, first=False):
                            before = not (first and k == 0)
                            rows.low(dve, i, k, 0)
                            if not first:
                                norm.scale_and_shift(dve, i - 1, k)
                            make_floor(i, k, 0)
                            rows.low(dve, i, k, 1)
                            if before:
                                residual(i - 1 + k, 1 - k)
                            make_floor(i, k, 1)
                            if before:
                                norm.await_stats(dve, i - 1 + k, 1 - k)
                            rows.low(dve, i, k, 2)
                            if before:
                                norm.variance(dve, i - 1 + k, 1 - k)
                            count_positives(i, k, 0)
                            rows.low(dve, i, k, 3)
                            count_positives(i, k, 1)

                        for k in range(2):
                            tile(0, k, first=True)
                        with dve.Fori(1, PAIRS) as i:
                            for k in range(2):
                                tile(i, k)
                        norm.scale_and_shift(dve, PAIRS - 1, 0)
                        for n in range(4):
                            dve.wait_ge(positives_counted[n], START + PAIRS)
                        dve.tensor_tensor(positive_sum[:], positives[:, :, 0], positives[:, :, 1], ALU.add).then_inc(
                            small, 1)
                        for n in range(4):
                            dve.wait_ge(zeros_counted[n], START + PAIRS)
                        dve.tensor_tensor(zero_sum[:], zeros[:, :, 0], zeros[:, :, 1], ALU.add).then_inc(
                            zero_sum_done, 1)
                        dve.wait_ge(length_done, START + 1)
                        dve.tensor_scalar(length[:], length[:], NORM_EPS, None, ALU.max).then_inc(small, 1)
                        dve.wait_ge(small, START + 2)
                        dve.reciprocal(head[:], length[:]).then_inc(small, 1)
                        residual(PAIRS - 1, 1)
                        norm.await_stats(dve, PAIRS - 1, 1)
                        norm.variance(dve, PAIRS - 1, 1)
                        norm.scale_and_shift(dve, PAIRS - 1, 1)

            with ExitStack() as s3:
                norm = TileNorm(s3, "l1")
                rows = RowProducts(s3, "l1", x0_parts, norm.z_done)
                inc = [sb(s3, f"inc{g}", [P, BANK]) for g in range(GROUPS)]
                x1_tile = [sb(s3, f"x1_tile{k}", [P, D]) for k in range(2)]
                degree_part = [sb(s3, f"degree_part{k}", [P, GROUPS]) for k in range(2)]
                degree = [sb(s3, f"degree{k}", [P, 1]) for k in range(2)]
                inv_degree = [sb(s3, f"inv_degree{k}", [P, 1]) for k in range(2)]
                sum_mark = [s3.enter_context(nc.psum_tensor(f"sum_mark{b}", [P, BANK], F32)) for b in range(2)]
                head_part = sems(s3, "head_part", GROUPS)
                inc_done = sems(s3, "inc_done", GROUPS)
                inc_summed = sems(s3, "inc_summed", GROUPS)
                degree_done = sems(s3, "degree_done")
                inv_degree_done = sems(s3, "inv_degree_done")
                x1_stored = sems(s3, "x1_stored")

                with next_block() as block:
                    @block.sync
                    def _(sp):
                        start(sp, 0, 5)
                        def load_next(i, k):
                            for u in range(2):
                                for g in (2 * u, 2 * u + 1):
                                    sp.wait_ge(inc_done[g], START + 2 * i + k + 1)
                                load_half(sp, i + 1, k, u)

                        def store(i, k):
                            sp.wait_ge(norm.normed[k], START + i + 1)
                            sp.dma_start(x1_scratch[bass.ds((2 * i + k) * P, P), :], x1_tile[k][:]).then_inc(
                                x1_stored[k], DMA)

                        for k in range(2):
                            load_next(0, k)
                        with sp.Fori(1, PAIRS - 1) as i:
                            for k in range(2):
                                load_next(i, k)
                                store(i - 1, k)
                        for i in (PAIRS - 2, PAIRS - 1):
                            for k in range(2):
                                store(i, k)
                        for k in range(2):
                            sp.wait_ge(x1_stored[k], START + DMA * PAIRS)
                        for n in range(4):
                            sp.wait_ge(masked_stored[n], START + DMA * PAIRS)
                        sp.wait_ge(zeros_stored, START + DMA)

                    @block.gpsimd
                    def _(pool):
                        start(pool, 1, 5)
                        with pool.Fori(0, PAIRS) as i:
                            for k in range(2):
                                for g in range(GROUPS):
                                    pool.wait_ge(head_part[g], START + 2 * i + k + 1)
                                    pool.tensor_tensor(inc[g][:], inc[g][:], adj_part(k, g * BANK, BANK),
                                                       ALU.add).then_inc(inc_done[g], 1)

                    @block.tensor
                    def _(pe):
                        start(pe, 2, 5)
                        def awaited(i, k, g):
                            pe.wait_ge(inc_done[g], START + 2 * i + k + 1)
                        rows.run(pe, lambda k, at: inc[at // BANK][:, at % BANK:at % BANK + P], awaited)

                    @block.scalar
                    def _(act):
                        start(act, 3, 5)
                        def sum_inc(i, k, g):
                            act.wait_ge(inc_done[g], START + 2 * i + k + 1)
                            act.wait_ge(degree_done[k], START + i)
                            act.wait_ge(inc_summed[(g - 2) % GROUPS], START + 2 * i + k + (1 if g >= 2 else 0))
                            act.activation(sum_mark[g % 2][:], inc[g][:], ACT.Copy,
                                           accum_out=degree_part[k][:, g:g + 1]).then_inc(inc_summed[g], 1)

                        def tile(i, k, first=False):
                            for g in range(GROUPS):
                                rows.high(act, i, k, g)
                                if g == 1 and not first:
                                    act.wait_ge(x1_stored[k], START + DMA * (i - 1))
                                    norm.apply(act, i - 1, k, x1_tile[k][:])
                                sum_inc(i, k, g)
                                if g == 3 and not (first and k == 0):
                                    norm.root(act, i - 1 + k, 1 - k)

                        for k in range(2):
                            tile(0, k, first=True)
                        with act.Fori(1, PAIRS) as i:
                            for k in range(2):
                                tile(i, k)
                        act.wait_ge(x1_stored[0], START + DMA * (PAIRS - 1))
                        norm.apply(act, PAIRS - 1, 0, x1_tile[0][:])
                        norm.root(act, PAIRS - 1, 1)
                        act.wait_ge(x1_stored[1], START + DMA * (PAIRS - 1))
                        norm.apply(act, PAIRS - 1, 1, x1_tile[1][:])

                    @block.vector
                    def _(dve):
                        start(dve, 4, 5)
                        def mark_positives(i, k, g):
                            dve.wait_ge(half_in[k][g // 2], START + DMA * (PAIRS + i + 1))
                            dve.tensor_scalar(inc[g][:], adj_part(k, g * BANK, BANK), 0.0,
                                              head[:, bass.ds(2 * i + k, 1)], ALU.is_gt, ALU.mult).then_inc(
                                head_part[g], 1)

                        def inverse_degree(i, k):
                            for g in range(GROUPS):
                                dve.wait_ge(inc_summed[g], START + 2 * i + k + 1)
                            dve.tensor_reduce(degree[k][:], degree_part[k][:], AX_X, ALU.add).then_inc(
                                degree_done[k], 1)
                            dve.wait_ge(degree_done[k], START + i + 1)
                            dve.reciprocal(inv_degree[k][:], degree[k][:]).then_inc(inv_degree_done[k], 1)

                        def residual(i, k):
                            dve.wait_ge(inv_degree_done[k], START + i + 1)
                            norm.residual(dve, i, k, rows, inv_degree[k][:, 0:1], tile_of(xa, 2 * i + k))

                        def tile(i, k, first=False, more=True):
                            before = not (first and k == 0)
                            j, l = i - 1 + k, 1 - k
                            for g in range(GROUPS):
                                if g == 2 and before:
                                    norm.await_stats(dve, j, l)
                                rows.low(dve, i, k, g)
                                if g == 0 and not first:
                                    norm.scale_and_shift(dve, i - 1, k)
                                if g == 0 and before:
                                    inverse_degree(j, l)
                                if g == 1 and before:
                                    residual(j, l)
                                if g == 2 and before:
                                    norm.variance(dve, j, l)
                                if more:
                                    dve.wait_ge(inc_summed[g], START + 2 * i + k + 1)
                                    mark_positives(i + k, 1 - k, g)

                        for g in range(GROUPS):
                            mark_positives(0, 0, g)
                        for k in range(2):
                            tile(0, k, first=True)
                        with dve.Fori(1, PAIRS - 1) as i:
                            for k in range(2):
                                tile(i, k)
                        tile(PAIRS - 1, 0)
                        tile(PAIRS - 1, 1, more=False)
                        norm.scale_and_shift(dve, PAIRS - 1, 0)
                        inverse_degree(PAIRS - 1, 1)
                        residual(PAIRS - 1, 1)
                        norm.await_stats(dve, PAIRS - 1, 1)
                        norm.variance(dve, PAIRS - 1, 1)
                        norm.scale_and_shift(dve, PAIRS - 1, 1)
        clear_spent()

        late = ExitStack()
        whole.enter_context(late)
        total = sb(late, "total", [P, T, D])
        mean_var_all = sb(late, "mean_var_all", [P, T, 2])
        degree_all = sb(late, "degree_all", [P, 2 * T])
        with ExitStack() as s4:
            x1_head = sb(s4, "x1_head", [P, 2, D])
            xT_high = sb(s4, "xT_high", [P, K, R], F32R)
            xT_low = sb(s4, "xT_low", [P, K, R], F32R)
            wo_raw = sb(s4, "wo_raw", [P, K, D])
            wo_high = sb(s4, "wo_high", [P, K, D], F32R)
            wo_low = sb(s4, "wo_low", [P, K, D], F32R)
            wk_raw, wvt_raw = ([sb(s4, f"{w}_raw{k}", [P, K, D]) for k in range(2)] for w in ("wk", "wvt"))
            wk_high, wk_low, wvt_high, wvt_low, fold_high, fold_low = (
                [sb(s4, f"{w}{k}", [P, K, D], F32R) for k in range(2)]
                for w in ("wk_high", "wk_low", "wvt_high", "wvt_low", "fold_high", "fold_low"))
            wq_raw = sb(s4, "wq_raw", [P, K, D])
            wq_high = sb(s4, "wq_high", [P, K, D], F32R)
            wq_low = sb(s4, "wq_low", [P, K, D], F32R)
            qT_high = sb(s4, "qT_high", [P, K, R], F32R)
            qT_low = sb(s4, "qT_low", [P, K, R], F32R)
            kT_high = sb(s4, "kT_high", [P, K, N], F32R)
            kT_low = sb(s4, "kT_low", [P, K, N], F32R)
            vals = sb(s4, "vals", [P, T, 2, D], F32R)
            masked_in = [sb(s4, f"masked_in{b}", [P, N]) for b in range(2)]
            probs = [sb(s4, f"probs{b}", [P, N]) for b in range(2)]
            pT_high = sb(s4, "pT_high", [P, T, P], F32R)
            pT_low = sb(s4, "pT_low", [P, T, P], F32R)
            column_sum = sb(s4, "column_sum", [P, N])
            adj_piece = sb(s4, "adj_piece", [P, 2, R])
            piece_sum = sb(s4, "piece_sum", [P, R])
            ones_col = sb(s4, "ones_col", [P, 1])
            stats2 = [sb(s4, f"stats2_{b}", [P, 6]) for b in range(2)]
            mean_var2 = [sb(s4, f"mean_var2_{b}", [P, 2]) for b in range(2)]
            zero_count = sb(s4, "zero_count", [P, T])
            least = sb(s4, "least", [P, T])
            least_tmp = sb(s4, "least_tmp", [P, T])
            chunk_max = [sb(s4, f"chunk_max{b}", [P, GROUPS]) for b in range(2)]
            row_max = [sb(s4, f"row_max{b}", [P, 1]) for b in range(2)]
            neg_max = [sb(s4, f"neg_max{b}", [P, 1]) for b in range(2)]
            masked_exp = [sb(s4, f"masked_exp{b}", [P, 1]) for b in range(2)]
            chunk_sum = [sb(s4, f"chunk_sum{b}", [P, GROUPS]) for b in range(2)]
            row_total = [sb(s4, f"row_total{b}", [P, 1]) for b in range(2)]
            denom = [sb(s4, f"denom{b}", [P, 1]) for b in range(2)]
            inv_denom = [sb(s4, f"inv_denom{b}", [P, 1]) for b in range(2)]
            s_bank, t_bank, o_bank, m_bank = (
                [s4.enter_context(nc.psum_tensor(f"{n}_bank{b}", [P, BANK], F32)) for b in range(2)]
                for n in ("s", "t", "o", "m"))

            total_in = sem(s4, "total_in")
            count_in = sem(s4, "count_in")
            least_done = sem(s4, "least_done")
            x1_in = sem(s4, "x1_in")
            xT_full = sem(s4, "xT_full")
            xT_high_done = sem(s4, "xT_high_done")
            xT_low_done = sem(s4, "xT_low_done")
            wo_in = sem(s4, "wo_in")
            wo_high_done = sem(s4, "wo_high_done")
            wo_low_done = sem(s4, "wo_low_done")
            wk_in, wvt_in, wk_high_done, wk_low_done, wvt_high_done, wvt_low_done = (
                sems(s4, f"{n}_") for n in
                ("wk_in", "wvt_in", "wk_high_done", "wk_low_done", "wvt_high_done", "wvt_low_done"))
            fold_full, fold_high_done, fold_low_done = (
                sems(s4, f"{n}_") for n in ("fold_full", "fold_high_done", "fold_low_done"))
            k_full, k_high_done, k_low_done = (sems(s4, f"{n}_") for n in ("k_full", "k_high_done", "k_low_done"))
            v_full, v_high_done, v_low_done = (sems(s4, f"{n}_") for n in ("v_full", "v_high_done", "v_low_done"))
            wq_in = sem(s4, "wq_in")
            wq_high_done = sem(s4, "wq_high_done")
            wq_low_done = sem(s4, "wq_low_done")
            q_full = sem(s4, "q_full")
            q_high_done = sem(s4, "q_high_done")
            q_low_done = sem(s4, "q_low_done")
            bias_in = sems(s4, "bias_in")
            s_full = sems(s4, "s_full")
            s_done = sems(s4, "s_done")
            first_max_done = sem(s4, "first_max_done")
            max_done = sems(s4, "max_done")
            neg_done = sems(s4, "neg_done")
            masked_exp_done = sems(s4, "masked_exp_done")
            exp_done = sems(s4, "exp_done")
            t_full = sems(s4, "t_full")
            pT_high_done = sems(s4, "pT_high_done")
            pT_low_done = sems(s4, "pT_low_done")
            sum_done = sems(s4, "sum_done")
            denom_done = sems(s4, "denom_done")
            inv_done = sems(s4, "inv_done")
            o_full = sems(s4, "o_full")
            o_half = sems(s4, "o_half")
            o_done = sems(s4, "o_done")
            piece_in = sem(s4, "piece_in")
            column_sum_zeroed = sem(s4, "column_sum_zeroed")
            piece_paired = sem(s4, "piece_paired")
            piece_added = sem(s4, "piece_added")
            ones_done = sem(s4, "ones_done")
            degree_full = sem(s4, "degree_full")
            degree_out = sem(s4, "degree_out")
            stats2_done = sems(s4, "stats2_done")
            var2_done = sems(s4, "var2_done")
            var2_kept = sems(s4, "var2_kept")

            half_scale = 0.5 * float(D) ** -0.5
            PAIRS_C = C // 2
            halves = lambda bank: bank[:].rearrange("p (k n) -> p k n", k=K)

            def three_products(pe, dst, left, right, kk_range, cols, last_sem):
                for kk in kk_range:
                    for n, (a, b) in enumerate(((left[0], right[0]), (left[0], right[1]), (left[1], right[0]))):
                        mm = pe.matmul(dst, a[:, kk, cols], b[:, kk, :], start=(kk == 0 and n == 0),
                                       stop=(kk == K - 1 and n == 2))
                return mm

            with next_block() as block:
                @block.sync
                def _(sp):
                    start(sp, 0, 5)
                    sp.dma_start(total[:].rearrange("p (a c) d -> p a (c d)", a=2),
                                 x1_scratch.rearrange("(a r c) d -> r a (c d)", a=2, c=C)).then_inc(total_in, DMA)
                    sp.dma_start(zero_count[:].rearrange("p (a c) -> p a c", a=2),
                                 zeros_scratch.rearrange("(a r c) o -> r a (c o)", a=2, c=C)).then_inc(count_in, DMA)
                    bias_rows = bias_scratch.rearrange("(b r c) m -> b c r m", b=2, c=C)

                    def load_keys_weights(h, jj, k):
                        c, n = 2 * jj + k, PAIRS_C * h + jj
                        sp.wait_ge(wvt_low_done[k], START + n)
                        sp.dma_start(wvt_raw[k][:], wvt_scratch[bass.ds(c, 1)].rearrange("o p k n -> (o p) k n")
                                     ).then_inc(wvt_in[k], DMA)
                        sp.wait_ge(wk_low_done[k], START + n)
                        sp.dma_start(wk_raw[k][:], wk[:, bass.ds(c * D, D)].rearrange("(k p) n -> p k n", p=P)
                                     ).then_inc(wk_in[k], DMA)

                    def load_query_weights(c, use):
                        sp.wait_ge(wq_low_done, START + use)
                        sp.dma_start(wq_raw[:], wq[:, bass.ds(c * D, D)].rearrange("(k p) n -> p k n", p=P)
                                     ).then_inc(wq_in, DMA)

                    def load_masked(c, use):
                        for b in range(2):
                            sp.wait_ge(neg_done[b], START + use)
                            sp.dma_start(masked_in[b][:], bias_rows[b, bass.ds(c, 1)].rearrange("o r m -> (o r) m")
                                         ).then_inc(bias_in[b], DMA)

                    def load_piece(h, c, use):
                        sp.wait_ge(piece_paired, START + use)
                        sp.dma_start(adj_piece[:], adj[bass.ds(h * R, R), bass.ds(c * R, R)].rearrange(
                            "(a p) m -> p a m", p=P)).then_inc(piece_in, DMA)

                    def load_head(h):
                        sp.wait_ge(xT_full, START + h)
                        sp.dma_start(x1_head[:], x1_scratch[bass.ds(h * R, R), :].rearrange("(a p) d -> p a d", p=P)
                                     ).then_inc(x1_in, DMA)
                        sp.wait_ge(wo_low_done, START + h)
                        sp.dma_start(wo_raw[:], wout[bass.ds(h * D, D), :].rearrange("(k p) n -> p k n", p=P)
                                     ).then_inc(wo_in, DMA)
                        for k in range(2):
                            load_keys_weights(h, 0, k)
                        load_query_weights(0, h * C)
                        load_piece(h, 0, h * C)
                        load_masked(0, h * C)

                    def head(h, more):
                        with sp.Fori(1, PAIRS_C) as jj:
                            for k in range(2):
                                load_keys_weights(h, jj, k)
                        with sp.Fori(1, C) as c:
                            load_query_weights(c, h * C + c)
                            load_piece(h, c, h * C + c)
                            load_masked(c, h * C + c)
                        if more:
                            load_head(h + 1)

                    load_head(0)
                    with sp.Fori(0, H - 1) as h:
                        head(h, True)
                    head(H - 1, False)

                @block.tensor
                def _(pe):
                    start(pe, 1, 5)
                    def turn_x(h):
                        pe.wait_ge(x1_in, START + DMA * (h + 1))
                        for kk in range(K):
                            for a in range(2):
                                mm = pe.transpose(m_bank[0][:, kk * R + a * P:kk * R + (a + 1) * P],
                                                  x1_head[:, a, kk * P:(kk + 1) * P], ident[:])
                        mm.then_inc(xT_full, 1)

                    def fold_values(h, jj, k):
                        n = PAIRS_C * h + jj
                        pe.wait_ge(wvt_low_done[k], START + n + 1)
                        pe.wait_ge(fold_low_done[1 - k], START + n + k)
                        for a in range(2):
                            mm = three_products(pe, m_bank[0][:, a * D:(a + 1) * D], (wvt_high[k], wvt_low[k]),
                                                (wo_high, wo_low), range(K), slice(a * P, (a + 1) * P), None)
                        mm.then_inc(fold_full[k], 1)

                    def keys(h, jj, k):
                        n = PAIRS_C * h + jj
                        pe.wait_ge(wk_low_done[k], START + n + 1)
                        pe.wait_ge(k_low_done[1 - k], START + n + k)
                        if k == 1:
                            pe.wait_ge(q_low_done, START + h * C + 1)
                        for dh in range(K):
                            mm = three_products(pe, m_bank[1][:, dh * R:(dh + 1) * R], (wk_high[k], wk_low[k]),
                                                (xT_high, xT_low), range(K), slice(dh * P, (dh + 1) * P), None)
                        mm.then_inc(k_full[k], 1)

                    def values(h, jj, k):
                        n = PAIRS_C * h + jj
                        pe.wait_ge(fold_low_done[k], START + n + 1)
                        pe.wait_ge(v_low_done[k], START + n)
                        pe.wait_ge(o_done[k], START + h * C)
                        for a in range(2):
                            mm = three_products(pe, o_bank[k][:, a * D:(a + 1) * D], (xT_high, xT_low),
                                                (fold_high[k], fold_low[k]), range(K), slice(a * P, (a + 1) * P), None)
                        mm.then_inc(v_full[k], 1)

                    def queries(use):
                        pe.wait_ge(wq_low_done, START + use + 1)
                        for dh in range(K):
                            mm = three_products(pe, m_bank[1][:, dh * R:(dh + 1) * R], (wq_high, wq_low),
                                                (xT_high, xT_low), range(K), slice(dh * P, (dh + 1) * P), None)
                        mm.then_inc(q_full, 1)

                    def scores(b, use, j):
                        bank = j % 2
                        if j == 0:
                            pe.wait_ge(q_low_done, START + use + 1)
                        pe.wait_ge(s_done[bank], START + 2 * (2 * use + b) + j // 2)
                        for dh in range(K):
                            for n, (a, kT) in enumerate(((qT_high, kT_high), (qT_high, kT_low), (qT_low, kT_high))):
                                mm = pe.matmul(s_bank[bank][:], a[:, dh, b * P:(b + 1) * P],
                                               kT[:, dh, j * BANK:(j + 1) * BANK], start=(dh == 0 and n == 0),
                                               stop=(dh == K - 1 and n == 2))
                        mm.then_inc(s_full[bank], 1)

                    def turns(b, use, g):
                        pe.wait_ge(exp_done[b], START + GROUPS * use + g + 1)
                        pe.wait_ge(pT_low_done[g % 2], START + 2 * (2 * use + b) + g // 2)
                        for a in range(TPB):
                            at = (g * TPB + a) * P
                            mm = pe.transpose(t_bank[g % 2][:, a * P:(a + 1) * P], probs[b][:, at:at + P], ident[:])
                        mm.then_inc(t_full[g % 2], 1)

                    def weigh(h, b, use, g):
                        if g == 0:
                            pe.wait_ge(o_done[b], START + use)
                            pe.wait_ge(v_low_done[b], START + PAIRS_C * (h + 1))
                        if g == GROUPS - 1:
                            pe.wait_ge(v_low_done[1], START + PAIRS_C * (h + 1))
                        pe.wait_ge(pT_low_done[g % 2], START + 2 * (2 * use + b) + g // 2 + 1)
                        for t in range(g * TPB, (g + 1) * TPB):
                            pe.matmul(o_bank[b][:], pT_high[:, t, :], vals[:, t, :, :].rearrange("p s d -> p (s d)"),
                                      start=(t == 0), stop=False)
                            mm = pe.matmul(o_bank[b][:, 0:D], pT_low[:, t, :], vals[:, t, 0, :], start=False,
                                           stop=(t == T - 1))
                        if g == GROUPS - 1:
                            mm.then_inc(o_full[b], 1)

                    def first_of_head(h, amid=(lambda n: None)):
                        amid(0)
                        pe.wait_ge(xT_low_done, START + h + 1)
                        pe.wait_ge(wo_low_done, START + h + 1)
                        fold_values(h, 0, 0)
                        amid(1)
                        pe.wait_ge(q_low_done, START + h * C)
                        keys(h, 0, 0)
                        amid(2)
                        fold_values(h, 0, 1)
                        amid(3)
                        pe.wait_ge(k_low_done[0], START + PAIRS_C * h + 1)
                        queries(h * C)
                        amid(4)

                    def step(h, b, use, next_queries=False, next_head=False):
                        turns(b, use, 0)
                        turns(b, use, 1)
                        scores(1 - b, use + b, 0)
                        turns(b, use, 2)
                        scores(1 - b, use + b, 1)
                        turns(b, use, 3)
                        scores(1 - b, use + b, 2)
                        weigh(h, b, use, 0)
                        scores(1 - b, use + b, 3)
                        if next_queries:
                            queries(use + 1)
                        if next_head:
                            turn_x(h + 1)
                        for g in range(1, GROUPS):
                            weigh(h, b, use, g)

                    def last_step(h, use, next_head):
                        turn = lambda *groups: [turns(1, use, g) for g in groups]
                        weigh_all = lambda *groups: [weigh(h, 1, use, g) for g in groups]
                        parts = (lambda: turn(0, 1), lambda: turn(2), lambda: (turn(3), weigh_all(0)),
                                 lambda: weigh_all(1), lambda: weigh_all(2, 3))
                        if next_head:
                            first_of_head(h + 1, lambda n: parts[n]())
                        else:
                            parts[0]()
                            degrees()
                            for part in parts[1:]:
                                part()

                    def degrees():
                        permuted = column_sum[:].rearrange("p (a r c) -> p a c r", a=2, c=C)
                        pe.wait_ge(ones_done, START + 1)
                        pe.wait_ge(piece_added, START + H * C)
                        for t in range(T):
                            pe.matmul(m_bank[0][:, t:t + 1], permuted[:, t // C, t % C, :], ones_col[:],
                                      start=True, stop=True)
                        for t in range(T):
                            mm = pe.matmul(m_bank[0][:, T + t:T + t + 1], column_sum[:, t * P:(t + 1) * P],
                                           ones_col[:], start=True, stop=True)
                        mm.then_inc(degree_full, 1)

                    def head(h, more):
                        with pe.Fori(0, PAIRS_C - 1) as jj:
                            keys(h, jj, 1)
                            values(h, jj, 0)
                            fold_values(h, jj + 1, 0)
                            keys(h, jj + 1, 0)
                            values(h, jj, 1)
                            fold_values(h, jj + 1, 1)
                        for k in range(2):
                            pe.wait_ge(k_low_done[k], START + PAIRS_C * h + PAIRS_C - 1)
                        scores(0, h * C, 0)
                        keys(h, PAIRS_C - 1, 1)
                        scores(0, h * C, 1)
                        scores(0, h * C, 2)
                        for k in range(2):
                            pe.wait_ge(k_low_done[k], START + PAIRS_C * (h + 1))
                        scores(0, h * C, 3)
                        values(h, PAIRS_C - 1, 0)
                        values(h, PAIRS_C - 1, 1)
                        with pe.Fori(0, C - 1) as c:
                            step(h, 0, h * C + c, next_queries=True)
                            step(h, 1, h * C + c)
                        step(h, 0, h * C + C - 1, next_head=more)
                        last_step(h, h * C + C - 1, more)

                    turn_x(0)
                    first_of_head(0)
                    with pe.Fori(0, H - 1) as h:
                        head(h, True)
                    head(H - 1, False)

                @block.scalar
                def _(act):
                    start(act, 2, 5)
                    def split_x(h):
                        act.wait_ge(xT_full, START + h + 1)
                        act.activation(xT_high[:], halves(m_bank[0]), ACT.Copy).then_inc(xT_high_done, 1)

                    def split_out_weights(h):
                        act.wait_ge(wo_in, START + DMA * (h + 1))
                        act.activation(wo_high[:], wo_raw[:], ACT.Copy).then_inc(wo_high_done, 1)

                    def split_keys_weights(h, jj, k):
                        n = PAIRS_C * h + jj
                        act.wait_ge(fold_full[k], START + n)
                        act.wait_ge(wvt_in[k], START + DMA * (n + 1))
                        act.activation(wvt_high[k][:], wvt_raw[k][:], ACT.Copy).then_inc(wvt_high_done[k], 1)
                        act.wait_ge(k_full[k], START + n)
                        act.wait_ge(wk_in[k], START + DMA * (n + 1))
                        act.activation(wk_high[k][:], wk_raw[k][:], ACT.Copy).then_inc(wk_high_done[k], 1)

                    def fold_high_part(h, jj, k):
                        n = PAIRS_C * h + jj
                        act.wait_ge(fold_full[k], START + n + 1)
                        act.wait_ge(v_full[k], START + n)
                        act.activation(fold_high[k][:], halves(m_bank[0]), ACT.Copy).then_inc(fold_high_done[k], 1)

                    def keys_high_part(h, jj, k):
                        act.wait_ge(k_full[k], START + PAIRS_C * h + jj + 1)
                        act.activation(kT_high[:, :, bass.ds((2 * jj + k) * R, R)], halves(m_bank[1]),
                                       ACT.Copy).then_inc(k_high_done[k], 1)

                    def values_high_part(h, jj, k):
                        act.wait_ge(v_full[k], START + PAIRS_C * h + jj + 1)
                        act.activation(vals[:, bass.ds(2 * (2 * jj + k), 2), 0, :], halves(o_bank[k]),
                                       ACT.Copy).then_inc(v_high_done[k], 1)

                    def split_query_weights(use):
                        act.wait_ge(wq_in, START + DMA * (use + 1))
                        act.wait_ge(q_full, START + use)
                        act.activation(wq_high[:], wq_raw[:], ACT.Copy).then_inc(wq_high_done, 1)

                    def evacuate_queries(use):
                        act.wait_ge(q_full, START + use + 1)
                        act.activation(qT_high[:], halves(m_bank[1]), ACT.Copy, scale=half_scale).then_inc(
                            q_high_done, 1)

                    def exps(b, use, j):
                        if j == 0:
                            act.wait_ge(neg_done[b], START + use + 1)
                            act.wait_ge(inv_done[b], START + use)
                            act.activation(masked_exp[b][:], neg_max[b][:], ACT.Exp, bias=masked_col[:, 0:1]).then_inc(
                                masked_exp_done[b], 1)
                        part = probs[b][:, j * BANK:(j + 1) * BANK]
                        act.activation(part, part, ACT.Exp, bias=neg_max[b][:, 0:1], scale=2.0,
                                       accum_out=chunk_sum[b][:, j:j + 1]).then_inc(exp_done[b], 1)

                    def prob_high(b, use, g):
                        act.wait_ge(t_full[g % 2], START + 2 * (2 * use + b) + g // 2 + 1)
                        act.activation(pT_high[:, g * TPB:(g + 1) * TPB, :], t_bank[g % 2][:].rearrange(
                            "p (a n) -> p a n", a=TPB), ACT.Copy).then_inc(pT_high_done[g % 2], 1)

                    def step(h, b, use, next_queries=False, next_weights=False, next_x=False, next_products=False):
                        exps(b, use, 0)
                        exps(b, use, 1)
                        prob_high(b, use, 0)
                        if next_weights:
                            split_out_weights(h + 1)
                            split_keys_weights(h + 1, 0, 0)
                        exps(b, use, 2)
                        prob_high(b, use, 1)
                        exps(b, use, 3)
                        if next_products:
                            fold_high_part(h + 1, 0, 0)
                        prob_high(b, use, 2)
                        if next_queries:
                            split_query_weights(use + 1)
                        if next_products:
                            keys_high_part(h + 1, 0, 0)
                        prob_high(b, use, 3)
                        if next_queries:
                            evacuate_queries(use + 1)
                        if next_x:
                            split_x(h + 1)
                            split_keys_weights(h + 1, 0, 1)
                            split_query_weights(use + 1)
                        if next_products:
                            fold_high_part(h + 1, 0, 1)
                            evacuate_queries(use + 1)

                    def head(h, more):
                        with act.Fori(0, PAIRS_C - 1) as jj:
                            for k in range(2):
                                split_keys_weights(h, jj + 1, k)
                                keys_high_part(h, jj + k, 1 - k)
                                values_high_part(h, jj, k)
                                fold_high_part(h, jj + 1, k)
                        keys_high_part(h, PAIRS_C - 1, 1)
                        values_high_part(h, PAIRS_C - 1, 0)
                        with act.Fori(0, C - 1) as c:
                            step(h, 0, h * C + c, next_queries=True)
                            step(h, 1, h * C + c)
                        step(h, 0, h * C + C - 1, next_weights=more, next_x=more)
                        step(h, 1, h * C + C - 1, next_products=more)

                    act.activation(masked_exp[0][:], masked_col[:], ACT.Exp).then_inc(masked_exp_done[0], 1)
                    split_x(0)
                    split_out_weights(0)
                    split_keys_weights(0, 0, 0)
                    split_keys_weights(0, 0, 1)
                    split_query_weights(0)
                    fold_high_part(0, 0, 0)
                    keys_high_part(0, 0, 0)
                    fold_high_part(0, 0, 1)
                    evacuate_queries(0)
                    with act.Fori(0, H - 1) as h:
                        head(h, True)
                    head(H - 1, False)
                @block.gpsimd
                def _(pool):
                    start(pool, 4, 5)
                    def low(dst, source, high):
                        return pool.tensor_tensor(dst, source, plain(high), ALU.subtract)

                    def split_out_weights(h):
                        pool.wait_ge(wo_high_done, START + h + 1)
                        low(wo_low[:], wo_raw[:], wo_high[:]).then_inc(wo_low_done, 1)

                    def split_keys_weights(h, jj, k):
                        n = PAIRS_C * h + jj
                        pool.wait_ge(wvt_high_done[k], START + n + 1)
                        low(wvt_low[k][:], wvt_raw[k][:], wvt_high[k][:]).then_inc(wvt_low_done[k], 1)
                        pool.wait_ge(wk_high_done[k], START + n + 1)
                        low(wk_low[k][:], wk_raw[k][:], wk_high[k][:]).then_inc(wk_low_done[k], 1)

                    def split_query_weights(use):
                        pool.wait_ge(wq_high_done, START + use + 1)
                        low(wq_low[:], wq_raw[:], wq_high[:]).then_inc(wq_low_done, 1)

                    def split_first_weights(h):
                        split_out_weights(h)
                        split_keys_weights(h, 0, 0)
                        split_keys_weights(h, 0, 1)
                        query_weights_and_piece(0, h * C)

                    def pair_piece(use):
                        pool.wait_ge(piece_in, START + DMA * (use + 1))
                        pool.wait_ge(piece_added, START + use)
                        pool.tensor_tensor(piece_sum[:], adj_piece[:, 0, :], adj_piece[:, 1, :], ALU.add).then_inc(
                            piece_paired, 1)

                    def add_piece(c):
                        mine = column_sum[:, bass.ds(c * R, R)]
                        pool.tensor_tensor(mine, mine, piece_sum[:], ALU.add).then_inc(piece_added, 1)

                    def query_weights_and_piece(c, use):
                        pair_piece(use)
                        pool.wait_ge(piece_paired, START + use + 1)
                        split_query_weights(use)
                        add_piece(c)

                    def head(h, more):
                        with pool.Fori(1, PAIRS_C) as jj:
                            for k in range(2):
                                split_keys_weights(h, jj, k)
                        with pool.Fori(1, C) as c:
                            query_weights_and_piece(c, h * C + c)
                        if more:
                            split_first_weights(h + 1)

                    pool.memset(ones_col[:], 1.0).then_inc(ones_done, 1)
                    pool.memset(column_sum[:], 0.0).then_inc(column_sum_zeroed, 1)
                    pool.wait_ge(column_sum_zeroed, START + 1)
                    split_first_weights(0)
                    with pool.Fori(0, H - 1) as h:
                        head(h, True)
                    head(H - 1, False)

                @block.vector
                def _(dve):
                    start(dve, 3, 5)
                    def low(dst, source, high):
                        return dve.tensor_tensor(dst, source, plain(high), ALU.subtract)

                    def split_x(h):
                        dve.wait_ge(xT_high_done, START + h + 1)
                        low(xT_low[:], halves(m_bank[0]), xT_high[:]).then_inc(xT_low_done, 1)

                    def fold_low_part(h, jj, k):
                        dve.wait_ge(fold_high_done[k], START + PAIRS_C * h + jj + 1)
                        low(fold_low[k][:], halves(m_bank[0]), fold_high[k][:]).then_inc(fold_low_done[k], 1)

                    def keys_low_part(h, jj, k):
                        at = bass.ds((2 * jj + k) * R, R)
                        dve.wait_ge(k_high_done[k], START + PAIRS_C * h + jj + 1)
                        low(kT_low[:, :, at], halves(m_bank[1]), kT_high[:, :, at]).then_inc(k_low_done[k], 1)

                    def values_low_part(h, jj, k):
                        at = bass.ds(2 * (2 * jj + k), 2)
                        dve.wait_ge(v_high_done[k], START + PAIRS_C * h + jj + 1)
                        low(vals[:, at, 1, :], halves(o_bank[k]), vals[:, at, 0, :]).then_inc(v_low_done[k], 1)

                    def evacuate_queries(use):
                        dve.wait_ge(q_high_done, START + use + 1)
                        dve.scalar_tensor_tensor(out=qT_low[:], in0=halves(m_bank[1]), scalar=half_scale,
                                                 in1=plain(qT_high[:]), op0=ALU.mult, op1=ALU.subtract).then_inc(
                            q_low_done, 1)

                    def await_scores(b, use, j):
                        dve.wait_ge(s_full[j % 2], START + 2 * (2 * use + b) + j // 2 + 1)

                    def masked_scores(b, use, j):
                        at = slice(j * BANK, (j + 1) * BANK)
                        dve.tensor_tensor_reduce(probs[b][:, at], s_bank[j % 2][:], masked_in[b][:, at], 1.0, NEVER,
                                                 ALU.add, ALU.max, chunk_max[b][:, j:j + 1]).then_inc(s_done[j % 2], 1)

                    def masked_scores_alone(use, j):
                        at = slice(j * BANK, (j + 1) * BANK)
                        await_scores(0, use, j)
                        dve.tensor_tensor(probs[0][:, at], s_bank[j % 2][:], masked_in[0][:, at], ALU.add).then_inc(
                            s_done[j % 2], 1)
                        dve.wait_ge(s_done[j % 2], START + 2 * (2 * use) + j // 2 + 1)
                        await_scores(0, use, j + 1)
                        dve.tensor_reduce(chunk_max[0][:, j:j + 1], probs[0][:, at], AX_X, ALU.max).then_inc(
                            first_max_done, 1)

                    def row_maximum(b, use, c, first=None):
                        for bank in range(2):
                            dve.wait_ge(s_done[bank], START + 2 * (2 * use + b) + 2)
                        if first is not None:
                            dve.wait_ge(first_max_done, START + 2 * (first + 1))
                        dve.tensor_reduce(row_max[b][:], chunk_max[b][:], AX_X, ALU.max).then_inc(max_done[b], 1)
                        dve.wait_ge(max_done[b], START + use + 1)
                        dve.tensor_scalar(neg_max[b][:], row_max[b][:], least[:, bass.ds(b * C + c, 1)], -2.0,
                                          ALU.max, ALU.mult).then_inc(neg_done[b], 1)

                    def prob_low(b, use, g):
                        dve.wait_ge(pT_high_done[g % 2], START + 2 * (2 * use + b) + g // 2 + 1)
                        low(pT_low[:, g * TPB:(g + 1) * TPB, :], t_bank[g % 2][:].rearrange("p (a n) -> p a n", a=TPB),
                            pT_high[:, g * TPB:(g + 1) * TPB, :]).then_inc(pT_low_done[g % 2], 1)

                    def denominator(b, use, c, ready):
                        dve.wait_ge(exp_done[b], START + GROUPS * (use + 1))
                        dve.tensor_reduce(row_total[b][:], chunk_sum[b][:], AX_X, ALU.add).then_inc(sum_done[b], 1)
                        dve.wait_ge(sum_done[b], START + use + 1)
                        dve.scalar_tensor_tensor(out=denom[b][:], in0=masked_exp[b][:],
                                                 scalar=zero_count[:, bass.ds(b * C + c, 1)], in1=row_total[b][:],
                                                 op0=ALU.mult, op1=ALU.add).then_inc(denom_done[b], 1)
                        ready(3)
                        dve.wait_ge(denom_done[b], START + use + 1)
                        dve.reciprocal(inv_denom[b][:], denom[b][:]).then_inc(inv_done[b], 1)

                    def add_head(b, use, c):
                        dve.wait_ge(o_full[b], START + use + 1)
                        dve.wait_ge(inv_done[b], START + use + 1)
                        mine = total[:, bass.ds(b * C + c, 1), :].rearrange("p o d -> p (o d)")
                        dve.scalar_tensor_tensor(out=mine, in0=o_bank[b][:, 0:D], scalar=inv_denom[b][:, 0:1], in1=mine,
                                                 op0=ALU.mult, op1=ALU.add).then_inc(o_half[b], 1)
                        dve.wait_ge(o_half[b], START + use + 1)
                        dve.scalar_tensor_tensor(out=mine, in0=o_bank[b][:, D:2 * D], scalar=inv_denom[b][:, 0:1],
                                                 in1=mine, op0=ALU.mult, op1=ALU.add).then_inc(o_done[b], 1)

                    def await_total(b, use, c):
                        dve.wait_ge(o_done[b], START + use + 1)
                        dve.wait_ge(var2_done[b], START + c)

                    def statistics(b, c):
                        dve.bn_stats(stats2[b][:], total[:, bass.ds(b * C + c, 1), :].rearrange("p o d -> p (o d)")
                                     ).then_inc(stats2_done[b], 1)

                    def await_statistics(b, c):
                        dve.wait_ge(stats2_done[b], START + c + 1)
                        dve.wait_ge(var2_kept[b], START + c)

                    def variance(b):
                        dve.bn_aggr(mean_var2[b][:], stats2[b][:]).then_inc(var2_done[b], 1)

                    def keep_variance(b, c):
                        dve.wait_ge(var2_done[b], START + c + 1)
                        dve.tensor_copy(mean_var_all[:, bass.ds(b * C + c, 1), :].rearrange("p o d -> p (o d)"),
                                        mean_var2[b][:]).then_inc(var2_kept[b], 1)

                    def step(b, use, c, next_queries=False, next_head=None, finished=None):
                        ready = lambda j: await_scores(1 - b, use + b, j)
                        score = lambda j: masked_scores(1 - b, use + b, j)
                        prob_low(b, use, 0)
                        dve.wait_ge(bias_in[1 - b], START + DMA * (use + b + 1))
                        ready(0)
                        if finished is not None:
                            await_total(1 - b, use - 1 + b, finished)
                        prob_low(b, use, 1)
                        score(0)
                        if finished is not None:
                            statistics(1 - b, finished)
                            await_statistics(1 - b, finished)
                        ready(1)
                        prob_low(b, use, 2)
                        score(1)
                        if finished is not None:
                            variance(1 - b)
                        ready(2)
                        prob_low(b, use, 3)
                        score(2)
                        if finished is not None:
                            keep_variance(1 - b, finished)
                        denominator(b, use, c, ready)
                        score(3)
                        row_maximum(1 - b, use + b, c + b)
                        if next_queries:
                            evacuate_queries(use + 1)
                        if next_head is not None:
                            split_x(next_head)
                        add_head(b, use, c)

                    def last_step(use, c, next_head):
                        prob_low(1, use, 0)
                        prob_low(1, use, 1)
                        if next_head is not None:
                            fold_low_part(next_head, 0, 0)
                        prob_low(1, use, 2)
                        if next_head is not None:
                            keys_low_part(next_head, 0, 0)
                        prob_low(1, use, 3)
                        denominator(1, use, c, lambda j: None)
                        if next_head is not None:
                            fold_low_part(next_head, 0, 1)
                            evacuate_queries(use + 1)
                        add_head(1, use, c)

                    def head(h, next_head):
                        with dve.Fori(0, PAIRS_C - 1) as jj:
                            for k in range(2):
                                keys_low_part(h, jj + k, 1 - k)
                                values_low_part(h, jj, k)
                                if k == 0:
                                    fold_low_part(h, jj + 1, k)
                                else:
                                    fold_low_part(h, jj + 1, k)
                        use = h * C
                        dve.wait_ge(bias_in[0], START + DMA * (use + 1))
                        masked_scores_alone(use, 0)
                        masked_scores(0, use, 1)
                        keys_low_part(h, PAIRS_C - 1, 1)
                        masked_scores_alone(use, 2)
                        masked_scores(0, use, 3)
                        row_maximum(0, use, 0, h)
                        values_low_part(h, PAIRS_C - 1, 0)
                        dve.wait_ge(v_full[1], START + PAIRS_C * (h + 1))
                        dve.tensor_copy(vals[:, T - 2:T, 0, :], halves(o_bank[1])).then_inc(v_high_done[1], 1)
                        values_low_part(h, PAIRS_C - 1, 1)
                        if next_head is not None:
                            with dve.Fori(0, C - 1) as c:
                                step(0, h * C + c, c, next_queries=True)
                                step(1, h * C + c, c)
                            step(0, h * C + C - 1, C - 1, next_head=next_head)
                            last_step(h * C + C - 1, C - 1, next_head)
                        else:
                            step(0, h * C, 0, next_queries=True)
                            step(1, h * C, 0, finished=0)
                            with dve.Fori(1, C - 1) as c:
                                step(0, h * C + c, c, next_queries=True, finished=c - 1)
                                step(1, h * C + c, c, finished=c)
                            step(0, h * C + C - 1, C - 1, finished=C - 2)
                            last_step(h * C + C - 1, C - 1, None)
                            dve.wait_ge(degree_full, START + 1)
                            dve.tensor_copy(degree_all[:], m_bank[0][:, 0:2 * T]).then_inc(degree_out, 1)
                            for b in range(2):
                                await_total(b, h * C + C - 1, C - 1)
                                statistics(b, C - 1)
                            for b in range(2):
                                await_statistics(b, C - 1)
                                variance(b)
                            for b in range(2):
                                keep_variance(b, C - 1)

                    dve.wait_ge(count_in, START + DMA)
                    dve.tensor_scalar(least[:], zero_count[:], 0.0, 0.5 * MASKED, ALU.is_gt, ALU.mult).then_inc(least_done, 1)
                    dve.tensor_scalar(least_tmp[:], zero_count[:], 0.0, NEVER, ALU.is_equal, ALU.mult).then_inc(
                        least_done, 1)
                    dve.wait_ge(least_done, START + 2)
                    dve.tensor_tensor(least[:], least[:], least_tmp[:], ALU.add).then_inc(least_done, 1)
                    dve.wait_ge(least_done, START + 3)
                    dve.wait_ge(total_in, START + DMA)
                    split_x(0)
                    fold_low_part(0, 0, 0)
                    keys_low_part(0, 0, 0)
                    fold_low_part(0, 0, 1)
                    evacuate_queries(0)
                    with dve.Fori(0, H - 1) as h:
                        head(h, h + 1)
                    head(H - 1, None)

        clear_spent()

        PIECES = T // 2
        RING = 4
        with ExitStack() as s5:
            scaled = sb(s5, "scaled", [P, T, 2, D], F32R)
            xb = sb(s5, "xb", [P, T, D])
            bias_all = sb(s5, "bias_all", [P, D])
            root = sb(s5, "root", [P, 2 * T])
            dis = sb(s5, "dis", [P, 2 * T])
            dev_all, inv_all, shift_all = (sb(s5, f"{n}_all", [P, T]) for n in ("dev", "inv", "shift"))
            pieces = [sb(s5, f"pieces{n}", [P, 2, BANK]) for n in range(RING)]
            piece_high, piece_low = ([sb(s5, f"piece_{n}{b}", [P, 2, BANK], F32R) for b in range(2)]
                                     for n in ("high", "low"))
            z, stats, mean_var, dev, inv, shift = (
                sb(s5, f"{n}3", [P, TPB, w])
                for n, w in (("z", D), ("stats", 6), ("mean_var", 2), ("dev", 1), ("inv", 1), ("shift", 1)))
            banks = s5.enter_context(nc.psum_tensor("banks", [P, 2, TPB, BANK], F32))
            proj = Projection(s5, "p3", [banks[:, 1, k, :] for k in range(2)],
                              [banks[:, 1, 2 + k, :] for k in range(2)], w3, 1)
            xb_in, bias_in, root_done, dis_done, dev_all_done, inv_all_done, shift_all_done, \
                x2_stored, biased = (sem(s5, f"{n}3") for n in (
                    "xb_in", "bias_in", "root_done", "dis_done", "dev_all_done",
                    "inv_all_done", "shift_all_done", "x2_stored", "biased"))
            x2_done = sems(s5, "x2_done")
            pieces_in = sems(s5, "pieces_in", RING)
            high_done, low_done, used = (sems(s5, f"piece_{n}") for n in ("high_done", "low_done", "used"))
            z_done, stats_done, var_done, dev_done, inv_done, shift_done, normed, out_stored = (
                sem(s5, f"{n}3") for n in ("z_done", "stats_done", "var_done", "dev_done", "inv_done", "shift_done",
                                           "normed", "out_stored"))
            splits = lambda q, p: q * (PIECES // 2) + p // 2

            with next_block() as block:
                @block.sync
                def _(sp):
                    start(sp, 0, 5)
                    proj.load_weight(sp)
                    sp.dma_start(bias_all[:], bias.partition_broadcast(P)).then_inc(bias_in, DMA)
                    adj_tiles = adj.rearrange("(a r c) n -> a r c n", a=2, c=C)

                    def load_piece(q, p):
                        a, c = 2 * p // C, 2 * p % C
                        sp.dma_start(pieces[p % RING][:], adj_tiles[a, :, c:c + 2, bass.ds(q * BANK, BANK)]).then_inc(
                            pieces_in[p % RING], DMA)

                    def reload_piece(q, p):
                        sp.wait_ge(low_done[p % 2], START + splits(q, p) - RING // 2 + 1)
                        load_piece(q, p)

                    for p in range(RING):
                        load_piece(0, p)
                    for k in range(2):
                        sp.wait_ge(x2_done[k], START + PAIRS)
                    sp.dma_start(x2_scratch.rearrange("(a r c) d -> r a (c d)", a=2, c=C),
                                 total[:].rearrange("p (a c) d -> p a (c d)", a=2)).then_inc(x2_stored, DMA)
                    sp.wait_ge(x2_stored, START + DMA)
                    sp.dma_start(xb[:], x2_scratch.rearrange("(t p) d -> p t d", p=P)).then_inc(xb_in, DMA)
                    with sp.Fori(0, GROUPS - 1) as q:
                        for p in range(RING, PIECES):
                            reload_piece(q, p)
                        for p in range(RING):
                            reload_piece(q + 1, p)
                    for p in range(RING, PIECES):
                        reload_piece(GROUPS - 1, p)

                @block.gpsimd
                def _(pool):
                    start(pool, 1, 5)
                    pool.wait_ge(xb_in, START + DMA)
                    pool.wait_ge(bias_in, START + DMA)
                    for t in range(T):
                        pool.tensor_tensor(xb[:, t, :], xb[:, t, :], bias_all[:], ALU.add).then_inc(biased, 1)

                @block.tensor
                def _(pe):
                    start(pe, 2, 5)
                    def turn(i, k):
                        pe.wait_ge(x2_done[k], START + i + 1)
                        proj.transposes(pe, i, k, total[:, 2 * i + k, :])

                    turn(0, 0)
                    turn(0, 1)
                    pe.wait_ge(proj.w_low_done, START + 1)
                    proj.products(pe, 0, 0)
                    for i in range(1, PAIRS):
                        for k in range(2):
                            turn(i, k)
                            proj.products(pe, i - 1 + k, 1 - k)
                    proj.products(pe, PAIRS - 1, 1)
                    for k in range(2):
                        pe.wait_ge(proj.y_read[k], START + PAIRS)
                    with pe.Fori(0, GROUPS) as q:
                        for p in range(PIECES):
                            if p == 0:
                                pe.wait_ge(z_done, START + TPB * q)
                            pe.wait_ge(low_done[p % 2], START + splits(q, p) + 1)
                            for a in range(TPB):
                                for e in range(2):
                                    for n, (left, part) in enumerate(((piece_high, 0), (piece_high, 1),
                                                                      (piece_low, 0))):
                                        mm = pe.matmul(
                                            banks[:, bass.ds(q % 2, 1), a, 0:D].rearrange("p o d -> p (o d)"),
                                            left[p % 2][:, e, a * P:(a + 1) * P], scaled[:, 2 * p + e, part, :],
                                            start=(p == 0 and e == 0 and n == 0),
                                            stop=(p == PIECES - 1 and e == 1 and n == 2))
                            mm.then_inc(used[p % 2], 1)

                @block.scalar
                def _(act):
                    start(act, 3, 5)
                    act.activation(dev_all[:], mean_var_all[:, :, 1], ACT.Sqrt, bias=eps_col[:, 0:1]).then_inc(
                        dev_all_done, 1)
                    act.activation(root[:], degree_all[:], ACT.Sqrt).then_inc(root_done, 1)
                    proj.split_weight_high(act)

                    def scaled_high(i, k):
                        proj.y_high(act, i, k, part_of(scaled, 2 * i + k, 0), dis[:, bass.ds(2 * i + k, 1)])

                    def apply_norm(i):
                        t = 2 * i + 1
                        mine = total[:, bass.ds(t, 1), :].rearrange("p o d -> p (o d)")
                        act.activation(mine, mine, ACT.Identity, bias=shift_all[:, bass.ds(t, 1)],
                                       scale=inv_all[:, bass.ds(t, 1)]).then_inc(x2_done[1], 1)

                    act.wait_ge(shift_all_done, START + 1)
                    apply_norm(0)
                    proj.high(act, 0, 0)
                    apply_norm(1)
                    proj.high(act, 0, 1)
                    act.wait_ge(dis_done, START + 1)
                    scaled_high(0, 0)
                    with act.Fori(1, PAIRS - 1) as i:
                        proj.high(act, i, 0)
                        apply_norm(i + 1)
                        scaled_high(i - 1, 1)
                        proj.high(act, i, 1)
                        scaled_high(i, 0)
                    for k in range(2):
                        proj.high(act, PAIRS - 1, k)
                        scaled_high(PAIRS - 2 + k, 1 - k)
                    scaled_high(PAIRS - 1, 1)

                    def high_part(q, p):
                        act.wait_ge(pieces_in[p % RING], START + DMA * (q * (PIECES // RING) + p // RING + 1))
                        act.wait_ge(used[p % 2], START + splits(q, p))
                        act.activation(piece_high[p % 2][:], pieces[p % RING][:], ACT.Copy).then_inc(
                            high_done[p % 2], 1)

                    def norm_root(q):
                        act.wait_ge(var_done, START + TPB * (q + 1))
                        act.activation(dev[:, :, 0], mean_var[:, :, 1], ACT.Sqrt, bias=eps_col[:, 0:1]).then_inc(
                            dev_done, 1)

                    def norm_apply(q):
                        act.wait_ge(shift_done, START + q + 1)
                        for a in range(TPB):
                            act.activation(z[:, a, :], z[:, a, :], ACT.Identity, bias=shift[:, a, :],
                                           scale=inv[:, a, :]).then_inc(normed, 1)
                        act.wait_ge(normed, START + TPB * (q + 1))
                        act.dma_start(out[bass.ds(q * BANK, BANK), :].rearrange("(a p) d -> p a d", p=P),
                                      z[:]).then_inc(out_stored, DMA)

                    for p in range(PIECES):
                        high_part(0, p)
                    with act.Fori(1, GROUPS) as q:
                        for p in range(PIECES):
                            high_part(q, p)
                            if p == TPB:
                                norm_root(q - 1)
                            if p == TPB + 2:
                                norm_apply(q - 1)
                    norm_root(GROUPS - 1)
                    norm_apply(GROUPS - 1)
                    act.wait_ge(out_stored, START + DMA * GROUPS)

                @block.vector
                def _(dve):
                    start(dve, 4, 5)
                    dve.sem_inc(z_done, TPB)
                    dve.wait_ge(dev_all_done, START + 1)
                    dve.reciprocal(inv_all[:], dev_all[:]).then_inc(inv_all_done, 1)
                    dve.wait_ge(inv_all_done, START + 1)
                    dve.scalar_tensor_tensor(out=shift_all[:], in0=mean_var_all[:, :, 0], scalar=-1.0, in1=inv_all[:],
                                             op0=ALU.mult, op1=ALU.mult).then_inc(shift_all_done, 1)
                    dve.wait_ge(shift_all_done, START + 1)

                    def apply_norm(i):
                        t = 2 * i
                        mine = total[:, bass.ds(t, 1), :].rearrange("p o d -> p (o d)")
                        dve.tensor_scalar(mine, mine, inv_all[:, bass.ds(t, 1)], shift_all[:, bass.ds(t, 1)], ALU.mult,
                                          ALU.add).then_inc(x2_done[0], 1)

                    def scaled_low(i, k):
                        t = 2 * i + k
                        proj.y_low(dve, i, k, part_of(scaled, t, 1), part_of(scaled, t, 0), dis[:, bass.ds(t, 1)])

                    apply_norm(0)
                    apply_norm(1)
                    dve.wait_ge(root_done, START + 1)
                    dve.reciprocal(dis[:], root[:]).then_inc(dis_done, 1)
                    proj.split_weight_low(dve)
                    proj.low(dve, 0, 0)
                    proj.low(dve, 0, 1)
                    dve.wait_ge(dis_done, START + 1)
                    scaled_low(0, 0)
                    with dve.Fori(1, PAIRS - 1) as i:
                        proj.low(dve, i, 0)
                        scaled_low(i - 1, 1)
                        proj.low(dve, i, 1)
                        apply_norm(i + 1)
                        scaled_low(i, 0)
                    for k in range(2):
                        proj.low(dve, PAIRS - 1, k)
                        scaled_low(PAIRS - 2 + k, 1 - k)
                    scaled_low(PAIRS - 1, 1)

                    def low_part(q, p):
                        dve.wait_ge(high_done[p % 2], START + splits(q, p) + 1)
                        dve.tensor_tensor(piece_low[p % 2][:], pieces[p % RING][:], plain(piece_high[p % 2][:]),
                                          ALU.subtract).then_inc(low_done[p % 2], 1)

                    def residual(q, a):
                        t = TPB * q + a
                        if a == 0:
                            dve.wait_ge(used[1], START + splits(q, PIECES))
                            dve.wait_ge(biased, START + TPB * (q + 1))
                            dve.wait_ge(out_stored, START + DMA * q)
                        dve.scalar_tensor_tensor(
                            out=z[:, a, :], in0=banks[:, bass.ds(q % 2, 1), a, 0:D].rearrange("p o d -> p (o d)"),
                            scalar=dis[:, bass.ds(T + t, 1)], in1=xb[:, bass.ds(t, 1), :].rearrange("p o d -> p (o d)"),
                            op0=ALU.mult, op1=ALU.add).then_inc(z_done, 1)
                        dve.wait_ge(z_done, START + TPB * (q + 1) + a + 1)
                        dve.bn_stats(stats[:, a, :], z[:, a, :]).then_inc(stats_done, 1)

                    def variance(a):
                        dve.bn_aggr(mean_var[:, a, :], stats[:, a, :]).then_inc(var_done, 1)

                    def scale_and_shift(q):
                        dve.wait_ge(dev_done, START + q + 1)
                        dve.reciprocal(inv[:, :, 0], dev[:, :, 0]).then_inc(inv_done, 1)
                        dve.wait_ge(inv_done, START + q + 1)
                        dve.scalar_tensor_tensor(out=shift[:, :, 0], in0=mean_var[:, :, 0], scalar=-1.0,
                                                 in1=inv[:, :, 0], op0=ALU.mult, op1=ALU.mult).then_inc(shift_done, 1)

                    for p in range(PIECES):
                        low_part(0, p)
                    with dve.Fori(1, GROUPS) as q:
                        for p in range(PIECES):
                            if 0 < p <= TPB:
                                dve.wait_ge(stats_done, START + TPB * (q - 1) + p)
                            low_part(q, p)
                            if 0 < p <= TPB:
                                variance(p - 1)
                            if p < TPB:
                                residual(q - 1, p)
                            if p == TPB + 1:
                                scale_and_shift(q - 1)
                    last = GROUPS - 1
                    for a in range(TPB):
                        residual(last, a)
                        if a > 0:
                            dve.wait_ge(stats_done, START + TPB * last + a)
                            variance(a - 1)
                    dve.wait_ge(stats_done, START + TPB * GROUPS)
                    variance(TPB - 1)
                    scale_and_shift(last)


_INS = ['x', 'adj', 'L0_gnn_t', 'L0_gnn_weight', 'L2_gnn_Wq', 'L2_gnn_Wk', 'L2_gnn_Wv', 'L2_gnn_Wout',
        'L3_gnn_weight', 'L3_gnn_bias']
_OUTS = [((2048, 256), 'float32')]


def kernel(**inputs):
    import numpy as _np
    import concourse.bacc as _bacc
    from concourse import mybir as _mybir
    from concourse.bass_utils import run_bass_kernel_spmd as _run

    nc = _bacc.Bacc("TRN2", target_bir_lowering=False, num_devices=1)
    arrays, args = {}, []
    for name in _INS:
        a = _np.ascontiguousarray(inputs[name])
        arrays[f"in_{name}_dram"] = a
        args.append(nc.dram_tensor(f"in_{name}_dram", a.shape, _mybir.dt.from_np(a.dtype), kind="ExternalInput").ap())
    for i, (shape, dtype) in enumerate(_OUTS):
        dt = _mybir.dt.from_np(_np.dtype(dtype))
        args.append(nc.dram_tensor(f"out_{i}_dram", shape, dt, kind="ExternalOutput").ap())
    graph_layers(nc, *args)
    r = _run(nc, [arrays], core_ids=[0])
    got = tuple(r.results[0][f"out_{i}_dram"] for i in range(len(_OUTS)))
    return got[0]
```

```python
from contextlib import ExitStack

import concourse.bass as bass
from concourse import mybir

ALU = mybir.AluOpType
ACT = mybir.ActivationFunctionType
AX_X = mybir.AxisListType.X
F32 = mybir.dt.float32
F32R = mybir.dt.float32r
BF16 = mybir.dt.bfloat16

P = 128
BANK = 512
LN_EPS = 1e-5
NORM_EPS = 1e-12
MASKED = -1.0e6
NEVER = -2.0 ** 100
DMA = 16
START = 1


def plain(ap):
    return ap.bitcast(F32)


def graph_layers(nc, x, adj, mix, w0, wq, wk, wv, wout, w3, bias, out):
    N, D = x.shape
    T = N // P
    K = D // P
    H = wq.shape[1] // D
    C = H
    R = N // H
    PAIRS = T // 2
    HALF = N // 2
    GROUPS = N // BANK
    TPB = BANK // P
    assert K == 2 and R == 2 * P and C * R == N and C == PAIRS and 2 * D == BANK

    bias_scratch = nc.dram_tensor("bias_scratch", (N, N), F32, kind="Internal").ap()
    wvt_scratch = nc.dram_tensor("wvt_scratch", (C, P, K, D), F32, kind="Internal").ap()
    x1_scratch = nc.dram_tensor("x1_scratch", (N, D), F32, kind="Internal").ap()
    x2_scratch = nc.dram_tensor("x2_scratch", (N, D), F32, kind="Internal").ap()
    dis_scratch = nc.dram_tensor("dis_scratch", (N, 1), F32, kind="Internal").ap()
    zeros_scratch = nc.dram_tensor("zeros_scratch", (N, 1), F32, kind="Internal").ap()

    whole = ExitStack()

    def sb(scope, name, shape, dtype=F32):
        return scope.enter_context(nc.sbuf_tensor(name, shape, dtype))

    spent, fresh, of_block = [], [], []

    def sem(scope, name, started=True, lasting=False):
        made = scope.enter_context(nc.semaphore(name))
        if not lasting:
            spent.append(made)
        if started:
            fresh.append(made)
        return made

    def next_block():
        of_block[:] = fresh
        fresh.clear()
        return nc.Block()

    def start(engine, n, of):
        for s in of_block[n::of]:
            engine.sem_inc(s, START)

    def clear_spent():
        numbers = sorted(s.num for s in spent)
        with nc.Block() as block:
            @block.gpsimd
            def _(pool):
                start = numbers[0]
                for n, after in zip(numbers, numbers[1:] + [None]):
                    if after != n + 1:
                        pool.sem_clear(range(start, n + 1))
                        start = after
        spent.clear()

    def sems(scope, name, n=2):
        return [sem(scope, f"{name}{i}") for i in range(n)]

    with whole:
        ident = sb(whole, "ident", [P, P])
        eps_col = sb(whole, "eps_col", [P, 1])
        masked_col = sb(whole, "masked_col", [P, 1])
        x1_tile = [sb(whole, f"x1_tile{k}", [P, D]) for k in range(2)]
        x1_stored = [sem(whole, f"x1_stored{k}", lasting=True) for k in range(2)]

        class Projection:
            def __init__(self, scope, tag, xT_bank, y_bank, w_dram, y_reads):
                self.xT_bank, self.y_bank, self.w_dram = xT_bank, y_bank, w_dram
                self.y_reads = y_reads
                self.w = sb(scope, f"{tag}_w", [P, K, D])
                self.w_high = sb(scope, f"{tag}_w_high", [P, K, D], F32R)
                self.w_low = sb(scope, f"{tag}_w_low", [P, K, D], F32R)
                self.xT_high = [sb(scope, f"{tag}_xT_high{k}", [P, K, P], F32R) for k in range(2)]
                self.xT_low = [sb(scope, f"{tag}_xT_low{k}", [P, K, P], F32R) for k in range(2)]
                self.w_in = sem(scope, f"{tag}_w_in")
                self.w_high_done = sem(scope, f"{tag}_w_high_done")
                self.w_low_done = sem(scope, f"{tag}_w_low_done")
                self.xT_full = sems(scope, f"{tag}_xT_full")
                self.high_done = sems(scope, f"{tag}_high_done")
                self.low_done = sems(scope, f"{tag}_low_done")
                self.y_full = sems(scope, f"{tag}_y_full")
                self.y_high_done = sems(scope, f"{tag}_y_high_done")
                self.y_read = sems(scope, f"{tag}_y_read")

            def load_weight(self, sp):
                sp.dma_start(self.w[:], self.w_dram.rearrange("(k p) n -> p k n", p=P)).then_inc(self.w_in, DMA)

            def split_weight_high(self, act):
                act.wait_ge(self.w_in, START + DMA)
                act.activation(self.w_high[:], self.w[:], ACT.Copy).then_inc(self.w_high_done, 1)

            def split_weight_low(self, dve):
                dve.wait_ge(self.w_high_done, START + 1)
                dve.tensor_tensor(self.w_low[:], self.w[:], plain(self.w_high[:]), ALU.subtract).then_inc(
                    self.w_low_done, 1)

            def transposes(self, pe, i, k, tile):
                pe.wait_ge(self.low_done[k], START + i)
                for kk in range(K):
                    mm = pe.transpose(self.xT_bank[k][:, kk * P:(kk + 1) * P], tile[:, kk * P:(kk + 1) * P], ident[:])
                mm.then_inc(self.xT_full[k], 1)

            def turned(self, k):
                return self.xT_bank[k][:, 0:D].rearrange("p (k n) -> p k n", k=K)

            def high(self, act, i, k):
                act.wait_ge(self.xT_full[k], START + i + 1)
                act.wait_ge(self.y_full[k], START + i)
                act.activation(self.xT_high[k][:], self.turned(k), ACT.Copy).then_inc(self.high_done[k], 1)

            def low(self, dve, i, k):
                dve.wait_ge(self.high_done[k], START + i + 1)
                dve.tensor_tensor(self.xT_low[k][:], self.turned(k), plain(self.xT_high[k][:]),
                                  ALU.subtract).then_inc(self.low_done[k], 1)

            def products(self, pe, i, k):
                pe.wait_ge(self.low_done[k], START + i + 1)
                pe.wait_ge(self.y_read[k], START + self.y_reads * i)
                for kk in range(K):
                    for n, (a, b) in enumerate(((self.xT_high[k], self.w_high), (self.xT_high[k], self.w_low),
                                                (self.xT_low[k], self.w_high))):
                        mm = pe.matmul(self.y_bank[k][:, 0:D], a[:, kk, :], b[:, kk, :], start=(kk == 0 and n == 0),
                                       stop=(kk == K - 1 and n == 2))
                mm.then_inc(self.y_full[k], 1)

            def y_high(self, act, i, k, dst, scale=1.0):
                act.wait_ge(self.y_full[k], START + i + 1)
                act.activation(dst, self.y_bank[k][:, 0:D], ACT.Copy, scale=scale).then_inc(self.y_high_done[k], 1)

            def y_low(self, dve, i, k, dst, high, scale=1.0):
                dve.wait_ge(self.y_high_done[k], START + i + 1)
                dve.scalar_tensor_tensor(out=dst, in0=self.y_bank[k][:, 0:D], scalar=scale, in1=plain(high),
                                         op0=ALU.mult, op1=ALU.subtract).then_inc(self.y_read[k], 1)

        def part_of(right, t, part):
            return right[:, bass.ds(t, 1), part, :].rearrange("p o d -> p (o d)")

        AHEAD = GROUPS - 1

        class TurnBuffers:
            def __init__(self, scope):
                self.high_part = [sb(scope, f"rows_high{g}", [P, TPB, P], F32R) for g in range(GROUPS)]
                self.low_part = [sb(scope, f"rows_low{g}", [P, TPB, P], F32R) for g in range(GROUPS)]
                self.turn_bank = [scope.enter_context(nc.psum_tensor(f"turn_bank{g}", [P, BANK], F32))
                                  for g in range(GROUPS)]
                self.o_bank = [scope.enter_context(nc.psum_tensor(f"rows_o_bank{k}", [P, BANK], F32)) for k in range(2)]
                self.turned = sems(scope, "turned", GROUPS)
                self.high_done = sems(scope, "high_done", GROUPS)
                self.low_done = sems(scope, "low_done", GROUPS)

        class RowProducts:
            def __init__(self, scope, tag, buffers, tiles_before, right, o_read, wide):
                self.tiles_before, self.right, self.o_read, self.wide = tiles_before, right, o_read, wide
                self.high_part, self.low_part = buffers.high_part, buffers.low_part
                self.turn_bank, self.o_bank = buffers.turn_bank, buffers.o_bank
                self.turned, self.high_done, self.low_done = buffers.turned, buffers.high_done, buffers.low_done
                self.o_full = sems(scope, f"{tag}_o_full")

            def uses(self, i, k):
                return self.tiles_before + 2 * i + k

            def turns(self, pe, i, k, g, cols):
                pe.wait_ge(self.low_done[g], START + self.uses(i, k))
                for a in range(TPB):
                    mm = pe.transpose(self.turn_bank[g][:, a * P:(a + 1) * P], cols(a), ident[:])
                mm.then_inc(self.turned[g], 1)

            def bank(self, g):
                return self.turn_bank[g][:].rearrange("p (a n) -> p a n", a=TPB)

            def high(self, act, i, k, g):
                act.wait_ge(self.turned[g], START + self.uses(i, k) + 1)
                act.activation(self.high_part[g][:], self.bank(g), ACT.Copy).then_inc(self.high_done[g], 1)

            def low(self, dve, i, k, g):
                dve.wait_ge(self.high_done[g], START + self.uses(i, k) + 1)
                dve.tensor_tensor(self.low_part[g][:], self.bank(g), plain(self.high_part[g][:]),
                                  ALU.subtract).then_inc(self.low_done[g], 1)

            def weigh(self, pe, i, k, g):
                pe.wait_ge(self.low_done[g], START + self.uses(i, k) + 1)
                if g == 0:
                    pe.wait_ge(self.o_read[k], START + i)
                for a in range(TPB):
                    m = g * TPB + a
                    if self.wide:
                        pe.matmul(self.o_bank[k][:], self.high_part[g][:, a, :],
                                  self.right[:, m, :, :].rearrange("p s d -> p (s d)"), start=(m == 0), stop=False)
                    else:
                        for part in range(2):
                            pe.matmul(self.o_bank[k][:, 0:D], self.high_part[g][:, a, :], self.right[:, m, part, :],
                                      start=(m == 0 and part == 0), stop=False)
                    mm = pe.matmul(self.o_bank[k][:, 0:D], self.low_part[g][:, a, :], self.right[:, m, 0, :],
                                   start=False, stop=(m == T - 1))
                if g == GROUPS - 1:
                    mm.then_inc(self.o_full[k], 1)

            def run(self, pe, cols, awaited, before_weigh=None):
                def turns(i, k, g):
                    awaited(i, k, g)
                    self.turns(pe, i, k, g, lambda a: cols(k, (g * TPB + a) * P))

                def tile(i, k, more, start_of=None):
                    for g in range(GROUPS):
                        if start_of is not None:
                            start_of(g)
                        self.weigh(pe, i, k, g)
                        if g + AHEAD < GROUPS:
                            turns(i, k, g + AHEAD)
                        elif more:
                            turns(i + k, 1 - k, g + AHEAD - GROUPS)

                for g in range(AHEAD):
                    turns(0, 0, g)
                tile(0, 0, True, before_weigh)
                tile(0, 1, True)
                with pe.Fori(1, PAIRS - 1) as i:
                    tile(i, 0, True)
                    tile(i, 1, True)
                tile(PAIRS - 1, 0, True)
                tile(PAIRS - 1, 1, False)

        class TileNorm:
            def __init__(self, scope, tag):
                self.z = [sb(scope, f"{tag}_z{k}", [P, D]) for k in range(2)]
                self.stats, self.mean_var, self.deviation, self.inv_dev, self.shift = (
                    [sb(scope, f"{tag}_{n}{k}", [P, w]) for k in range(2)]
                    for n, w in (("stats", 6), ("mean_var", 2), ("deviation", 1), ("inv_dev", 1), ("shift", 1)))
                self.half_done, self.z_done, self.stats_done, self.var_done, self.dev_done, self.inv_done, self.shift_done, \
                    self.normed = (sems(scope, f"{tag}_{n}") for n in (
                        "half_done", "z_done", "stats_done", "var_done", "dev_done", "inv_done", "shift_done", "normed"))

            def residual(self, dve, i, k, products, scale, x):
                dve.wait_ge(products.o_full[k], START + i + 1)
                dve.wait_ge(self.normed[k], START + i)
                if products.wide:
                    dve.scalar_tensor_tensor(out=self.z[k][:], in0=products.o_bank[k][:, D:2 * D], scalar=scale,
                                             in1=x, op0=ALU.mult, op1=ALU.add).then_inc(self.half_done[k], 1)
                    dve.wait_ge(self.half_done[k], START + i + 1)
                    x = self.z[k][:]
                dve.scalar_tensor_tensor(out=self.z[k][:], in0=products.o_bank[k][:, 0:D], scalar=scale, in1=x,
                                         op0=ALU.mult, op1=ALU.add).then_inc(self.z_done[k], 1)
                dve.wait_ge(self.z_done[k], START + i + 1)
                dve.bn_stats(self.stats[k][:], self.z[k][:]).then_inc(self.stats_done[k], 1)

            def await_stats(self, dve, i, k):
                dve.wait_ge(self.stats_done[k], START + i + 1)

            def variance(self, dve, i, k):
                dve.bn_aggr(self.mean_var[k][:], self.stats[k][:]).then_inc(self.var_done[k], 1)

            def root(self, act, i, k):
                act.wait_ge(self.var_done[k], START + i + 1)
                act.activation(self.deviation[k][:], self.mean_var[k][:, 1:2], ACT.Sqrt, bias=eps_col[:, 0:1]
                               ).then_inc(self.dev_done[k], 1)

            def scale_and_shift(self, dve, i, k):
                dve.wait_ge(self.dev_done[k], START + i + 1)
                dve.reciprocal(self.inv_dev[k][:], self.deviation[k][:]).then_inc(self.inv_done[k], 1)
                dve.wait_ge(self.inv_done[k], START + i + 1)
                dve.scalar_tensor_tensor(out=self.shift[k][:], in0=self.mean_var[k][:, 0:1], scalar=-1.0,
                                         in1=self.inv_dev[k][:], op0=ALU.mult, op1=ALU.mult).then_inc(
                    self.shift_done[k], 1)

            def apply(self, act, i, k, dst):
                act.wait_ge(self.shift_done[k], START + i + 1)
                act.activation(dst, self.z[k][:], ACT.Identity, bias=self.shift[k][:, 0:1],
                               scale=self.inv_dev[k][:, 0:1]).then_inc(self.normed[k], 1)

        front = ExitStack()
        with front:
            half_rows = [[sb(front, f"half_rows{k}{u}", [P, HALF]) for u in range(2)] for k in range(2)]
            xa = sb(front, "xa", [P, T, D])
            support, x0_parts = (sb(front, n, [P, T, 2, D], F32R) for n in ("support", "x0_parts"))
            positives = sb(front, "positives", [P, T, 2])
            head = sb(front, "head", [P, T])
            masked = [sb(front, f"masked{n}", [P, HALF]) for n in range(4)]
            zero_sum = sb(front, "zero_sum", [P, T])
            masked_stored = sems(front, "masked_stored", 4)
            wvt = [sb(front, f"wvt{k}", [P, K, D]) for k in range(2)]
            wvt_stored = sems(front, "wvt_stored")
            zeros_stored = sem(front, "zeros_stored")
            mix_col = sb(front, "mix_col", [P, 1])
            one_less_mix = sb(front, "one_less_mix", [P, 1])
            half_in = [sems(front, f"half_in{k}_") for k in range(2)]
            tile_of = lambda array, t: array[:, bass.ds(t, 1), :].rearrange("p o d -> p (o d)")
            adj_part = lambda k, at, n: half_rows[k][at // HALF][:, at % HALF:at % HALF + n]

            def load_half(sp, i, k, u):
                sp.dma_start(half_rows[k][u][:], adj[bass.ds((2 * i + k) * P, P), u * HALF:(u + 1) * HALF]).then_inc(
                    half_in[k][u], DMA)

            with ExitStack() as s1:
                wv_rows = [sb(s1, f"wv_rows{k}", [P, K, D]) for k in range(2)]
                xT_bank, y_bank, wvt_bank = (
                    [s1.enter_context(nc.psum_tensor(f"{n}_bank{k}", [P, BANK], F32)) for k in range(2)]
                    for n in ("xT", "y", "wvt"))
                proj = Projection(s1, "sup", xT_bank, y_bank, w0, 2)
                ident_zeroed = sem(s1, "ident_zeroed")
                consts_done = sem(s1, "consts_done")
                mix_in = sem(s1, "mix_in")
                mix_done = sem(s1, "mix_done")
                xa_in = sems(s1, "xa_in", GROUPS)
                wv_in = sems(s1, "wv_in")
                wvt_full = sems(s1, "wvt_full")
                wvt_ready = sems(s1, "wvt_ready")

                with next_block() as block:
                    @block.sync
                    def _(sp):
                        start(sp, 0, 5)
                        proj.load_weight(sp)
                        sp.dma_start(mix_col[:], mix.rearrange("(a b) -> a b", a=1).broadcast_to([P, 1])).then_inc(
                            mix_in, DMA)
                        for g in range(GROUPS):
                            tiles = slice(g * TPB, (g + 1) * TPB)
                            sp.dma_start(xa[:, tiles, :], x[g * BANK:(g + 1) * BANK, :].rearrange(
                                "(t p) d -> p t d", p=P)).then_inc(xa_in[g], DMA)
                        def load_wv(i, k):
                            sp.wait_ge(wvt_full[k], START + i)
                            sp.dma_start(wv_rows[k][:], wv[:, bass.ds((2 * i + k) * D, D)].rearrange(
                                "(k p) d -> p k d", p=P)).then_inc(wv_in[k], DMA)
                        for k in range(2):
                            load_wv(0, k)
                        for k in range(2):
                            for u in range(2):
                                load_half(sp, 0, k, u)
                        with sp.Fori(1, C // 2) as i:
                            for k in range(2):
                                load_wv(i, k)

                    @block.gpsimd
                    def _(pool):
                        start(pool, 1, 5)
                        pool.memset(ident[:], 0.0).then_inc(ident_zeroed, 1)
                        pool.memset(eps_col[:], LN_EPS).then_inc(consts_done, 1)
                        pool.memset(masked_col[:], MASKED).then_inc(consts_done, 1)
                        pool.wait_ge(ident_zeroed, START + 1)
                        pool.affine_select(out=ident[:], in_=ident[:], compare_op=ALU.not_equal, fill=1.0, base=0,
                                           pattern=[[-1, P]], channel_multiplier=1).then_inc(consts_done, 1)

                    @block.tensor
                    def _(pe):
                        start(pe, 2, 5)
                        def turn_values(i, k):
                            pe.wait_ge(wv_in[k], START + DMA * (i + 1))
                            pe.wait_ge(wvt_ready[k], START + i)
                            for dk in range(K):
                                for kk in range(K):
                                    mm = pe.transpose(wvt_bank[k][:, dk * D + kk * P:dk * D + (kk + 1) * P],
                                                      wv_rows[k][:, kk, dk * P:(dk + 1) * P], ident[:])
                            mm.then_inc(wvt_full[k], 1)

                        pe.wait_ge(consts_done, START + 3)
                        pe.wait_ge(xa_in[0], START + DMA)
                        proj.transposes(pe, 0, 0, xa[:, 0, :])
                        proj.transposes(pe, 0, 1, xa[:, 1, :])
                        pe.wait_ge(proj.w_low_done, START + 1)
                        for i in range(PAIRS):
                            for k in range(2):
                                proj.products(pe, i, k)
                                if i + 1 < PAIRS:
                                    if (2 * i + 2 + k) % TPB == 0:
                                        pe.wait_ge(xa_in[(2 * i + 2 + k) // TPB], START + DMA)
                                    proj.transposes(pe, i + 1, k, xa[:, 2 * i + 2 + k, :])
                                if k == 0:
                                    turn_values(i // 2, i % 2)

                    @block.scalar
                    def _(act):
                        start(act, 3, 5)
                        act.wait_ge(consts_done, START + 3)
                        proj.split_weight_high(act)
                        proj.high(act, 0, 0)
                        proj.high(act, 0, 1)
                        def keep_values(i, k):
                            act.wait_ge(wvt_full[k], START + i + 1)
                            act.wait_ge(wvt_stored[k], START + DMA * i)
                            act.activation(wvt[k][:], wvt_bank[k][:].rearrange("p (k d) -> p k d", k=K),
                                           ACT.Copy).then_inc(wvt_ready[k], 1)

                        def store_values(i, k):
                            act.wait_ge(wvt_ready[k], START + i + 1)
                            act.dma_start(wvt_scratch[bass.ds(2 * i + k, 1)].rearrange("o p k d -> (o p) k d"),
                                          wvt[k][:]).then_inc(wvt_stored[k], DMA)

                        for i in range(PAIRS):
                            for k in range(2):
                                proj.y_high(act, i, k, support[:, 2 * i + k, 0, :])
                                if i + 1 < PAIRS:
                                    proj.high(act, i + 1, k)
                            keep_values(i // 2, i % 2)
                            store_values(i // 2, i % 2)

                    @block.vector
                    def _(dve):
                        start(dve, 4, 5)
                        proj.split_weight_low(dve)
                        proj.low(dve, 0, 0)
                        proj.low(dve, 0, 1)
                        dve.wait_ge(mix_in, START + DMA)
                        dve.tensor_scalar(one_less_mix[:], mix_col[:], -1.0, 1.0, ALU.mult, ALU.add).then_inc(
                            mix_done, 1)

                        def add_support(i, k):
                            mine = tile_of(xa, 2 * i + k)
                            dve.scalar_tensor_tensor(out=mine, in0=y_bank[k][:, 0:D], scalar=one_less_mix[:, 0:1],
                                                     in1=mine, op0=ALU.mult, op1=ALU.add).then_inc(proj.y_read[k], 1)

                        def low_support(i, k):
                            t = 2 * i + k
                            proj.y_low(dve, i, k, part_of(support, t, 1), part_of(support, t, 0))

                        dve.wait_ge(mix_done, START + 1)
                        with dve.Fori(0, PAIRS - 1) as i:
                            for k in range(2):
                                low_support(i, k)
                                proj.low(dve, i + 1, k)
                                add_support(i, k)
                        for k in range(2):
                            low_support(PAIRS - 1, k)
                            add_support(PAIRS - 1, k)

            with ExitStack() as s2:
                norm0 = TileNorm(s2, "l0")
                turn_buffers = TurnBuffers(s2)
                rows0 = RowProducts(s2, "l0", turn_buffers, 0, support, norm0.z_done, False)
                zeros = sb(s2, "zeros", [P, T, 2])
                positive_sum = sb(s2, "positive_sum", [P, T])
                length = sb(s2, "length", [P, T])
                positive_mark, zero_mark = (
                    [sb(s2, f"{n}_mark{u}", [P, HALF], BF16) for u in range(2)]
                    for n in ("positive", "zero"))
                floor_done = sems(s2, "floor_done", 4)
                zeros_counted = sems(s2, "zeros_counted", 4)
                positives_counted = sems(s2, "positives_counted", 4)
                masked_done = sems(s2, "masked_done", 4)
                x0_high_done = sems(s2, "x0_high_done")
                x0_low_done = sems(s2, "x0_low_done")
                small = sem(s2, "small")
                length_done = sem(s2, "length_done")
                zero_sum_done = sem(s2, "zero_sum_done")
                by_c = lambda ap: ap.rearrange("p (r c) -> p c r", c=C)
                grouped = lambda ap: ap.rearrange("p (c r) -> p c r", c=C)

                norm1 = TileNorm(s2, "l1")
                rows1 = RowProducts(s2, "l1", turn_buffers, T, x0_parts, norm1.z_done, True)
                inc = [sb(s2, f"inc{g}", [P, BANK]) for g in range(GROUPS)]
                degree_part = [sb(s2, f"degree_part{k}", [P, GROUPS]) for k in range(2)]
                degree = [sb(s2, f"degree{k}", [P, 1]) for k in range(2)]
                inv_degree = [sb(s2, f"inv_degree{k}", [P, 1]) for k in range(2)]
                sum_mark = [sb(s2, f"sum_mark{b}", [P, BANK], BF16) for b in range(2)]
                head_part = sems(s2, "head_part", GROUPS)
                inc_done = sems(s2, "inc_done", GROUPS)
                inc_summed = sems(s2, "inc_summed", GROUPS)
                degree_done = sems(s2, "degree_done")
                inv_degree_done = sems(s2, "inv_degree_done")

                with next_block() as block:
                    @block.sync
                    def _(sp):
                        start(sp, 0, 5)
                        def layer0():
                            def store(i, k, u):
                                n = 2 * k + u
                                dst = bias_scratch[bass.ds((2 * i + k) * P, P), :].rearrange("n (c r) -> n c r", c=C)
                                sp.wait_ge(masked_done[n], START + i + 1)
                                sp.dma_start(dst[:, :, u * P:(u + 1) * P], grouped(masked[n][:])).then_inc(
                                    masked_stored[n], DMA)

                            def load_next(i, k, u):
                                sp.wait_ge(positives_counted[2 * k + u], START + i + 1)
                                load_half(sp, i + 1, k, u)

                            with sp.Fori(0, PAIRS - 1) as i:
                                for k in range(2):
                                    for u in range(2):
                                        store(i, k, u)
                                        load_next(i, k, u)
                            for k in range(2):
                                for u in range(2):
                                    store(PAIRS - 1, k, u)
                                    sp.wait_ge(positives_counted[2 * k + u], START + PAIRS)
                                    sp.dma_start(half_rows[k][u][:], adj[k * P:(k + 1) * P, u * HALF:(u + 1) * HALF]
                                                 ).then_inc(half_in[k][u], DMA)
                            sp.wait_ge(zero_sum_done, START + 1)
                            sp.dma_start(zeros_scratch.rearrange("(t p) o -> p t o", p=P), zero_sum[:].rearrange(
                                "p (t o) -> p t o", o=1), allow_slow_non_contiguous=True).then_inc(zeros_stored, DMA)

                        def layer1():
                            def load_next(i, k):
                                for u in range(2):
                                    for g in (2 * u, 2 * u + 1):
                                        sp.wait_ge(inc_done[g], START + 2 * i + k + 1)
                                    load_half(sp, i + 1, k, u)

                            def store(i, k):
                                sp.wait_ge(norm1.normed[k], START + i + 1)
                                sp.dma_start(x1_scratch[bass.ds((2 * i + k) * P, P), :], x1_tile[k][:]).then_inc(
                                    x1_stored[k], DMA)

                            for k in range(2):
                                load_next(0, k)
                            with sp.Fori(1, PAIRS - 1) as i:
                                for k in range(2):
                                    load_next(i, k)
                                    store(i - 1, k)
                            for i in (PAIRS - 2, PAIRS - 1):
                                for k in range(2):
                                    store(i, k)
                            for n in range(4):
                                sp.wait_ge(masked_stored[n], START + DMA * PAIRS)
                            for k in range(2):
                                sp.wait_ge(wvt_stored[k], START + DMA * (C // 2))
                            sp.wait_ge(zeros_stored, START + DMA)

                        layer0()
                        layer1()

                    @block.gpsimd
                    def _(pool):
                        start(pool, 1, 5)
                        def layer0():
                            def await_x0(i, k):
                                pool.wait_ge(x0_high_done[k], START + i + 1)

                            def low_x0(i, k):
                                t = 2 * i + k
                                pool.tensor_tensor(part_of(x0_parts, t, 1), tile_of(xa, t), plain(part_of(x0_parts, t, 0)),
                                                   ALU.subtract).then_inc(x0_low_done[k], 1)

                            def pair(i, first):
                                for k in range(2):
                                    for u in range(2):
                                        n = 2 * k + u
                                        pool.wait_ge(floor_done[n], START + i + 1)
                                        pool.wait_ge(zeros_counted[n], START + i + 1)
                                        if u == 1 and not first:
                                            await_x0(i - 1, k)
                                        pool.tensor_tensor(grouped(masked[n][:]), grouped(masked[n][:]),
                                                           by_c(half_rows[k][u][:]), ALU.add).then_inc(masked_done[n], 1)
                                    if not first:
                                        low_x0(i - 1, k)

                            pair(0, True)
                            with pool.Fori(1, PAIRS) as i:
                                pair(i, False)
                            await_x0(PAIRS - 1, 0)
                            low_x0(PAIRS - 1, 0)
                            add_adjacency(0, 0, 0)
                            add_adjacency(0, 0, 1)
                            await_x0(PAIRS - 1, 1)
                            low_x0(PAIRS - 1, 1)

                        def add_adjacency(i, k, g):
                            pool.wait_ge(head_part[g], START + 2 * i + k + 1)
                            pool.tensor_tensor(inc[g][:], inc[g][:], adj_part(k, g * BANK, BANK),
                                               ALU.add).then_inc(inc_done[g], 1)

                        def layer1():
                            for g in range(2, GROUPS):
                                add_adjacency(0, 0, g)
                            for g in range(GROUPS):
                                add_adjacency(0, 1, g)
                            with pool.Fori(1, PAIRS) as i:
                                for k in range(2):
                                    for g in range(GROUPS):
                                        add_adjacency(i, k, g)

                        layer0()
                        layer1()

                    @block.tensor
                    def _(pe):
                        start(pe, 2, 5)
                        def layer0():
                            def awaited(i, k, g):
                                if g % 2 == 0:
                                    pe.wait_ge(half_in[k][g // 2], START + DMA * (i + 1))
                            rows0.run(pe, lambda k, at: adj_part(k, at, P), awaited)

                        def layer1():
                            def awaited(i, k, g):
                                pe.wait_ge(inc_done[g], START + 2 * i + k + 1)
                            def x0_there(g):
                                if g == 0:
                                    pe.wait_ge(norm0.z_done[0], START + PAIRS)
                                if g == GROUPS - 1:
                                    pe.wait_ge(norm0.z_done[1], START + PAIRS)
                                for k in range(2):
                                    pe.wait_ge(x0_low_done[k], START + (g + 1) * TPB // 2)
                            rows1.run(pe, lambda k, at: inc[at // BANK][:, at % BANK:at % BANK + P], awaited, x0_there)

                        layer0()
                        layer1()

                    @block.scalar
                    def _(act):
                        start(act, 3, 5)
                        def layer0():
                            act.activation(norm0.deviation[0][:], eps_col[:], ACT.Sqrt)

                            def count_zeros(i, k, u):
                                n = 2 * k + u
                                act.wait_ge(floor_done[n], START + i + 1)
                                if k == 0:
                                    act.wait_ge(zeros_counted[2 + u], START + i)
                                else:
                                    act.wait_ge(zeros_counted[u], START + i + 1)
                                act.activation(zero_mark[u][:], masked[n][:], ACT.Copy, scale=1.0 / NEVER,
                                               accum_out=zeros[:, bass.ds(2 * i + k, 1), u:u + 1].rearrange(
                                                   "p o u -> p (o u)")).then_inc(zeros_counted[n], 1)

                            def make_x0(i, k):
                                t = 2 * i + k
                                norm0.apply(act, i, k, tile_of(xa, t))
                                act.wait_ge(norm0.normed[k], START + i + 1)
                                act.activation(part_of(x0_parts, t, 0), tile_of(xa, t), ACT.Copy).then_inc(
                                    x0_high_done[k], 1)

                            def tile(i, k, first=False):
                                rows0.high(act, i, k, 0)
                                rows0.high(act, i, k, 1)
                                if not first:
                                    make_x0(i - 1, k)
                                rows0.high(act, i, k, 2)
                                count_zeros(i, k, 0)
                                rows0.high(act, i, k, 3)
                                if not (first and k == 0):
                                    norm0.root(act, i - 1 + k, 1 - k)
                                count_zeros(i, k, 1)

                            for k in range(2):
                                tile(0, k, first=True)
                            with act.Fori(1, PAIRS) as i:
                                for k in range(2):
                                    tile(i, k)
                            act.wait_ge(small, START + 1)
                            act.activation(length[:], positive_sum[:], ACT.Sqrt).then_inc(length_done, 1)
                            make_x0(PAIRS - 1, 0)
                            rows1.high(act, 0, 0, 0)
                            norm0.root(act, PAIRS - 1, 1)
                            make_x0(PAIRS - 1, 1)

                        def layer1():
                            def sum_inc(i, k, g):
                                act.wait_ge(inc_done[g], START + 2 * i + k + 1)
                                act.wait_ge(degree_done[k], START + i)
                                act.wait_ge(inc_summed[(g - 2) % GROUPS], START + 2 * i + k + (1 if g >= 2 else 0))
                                act.activation(sum_mark[g % 2][:], inc[g][:], ACT.Copy,
                                               accum_out=degree_part[k][:, g:g + 1]).then_inc(inc_summed[g], 1)

                            def tile(i, k, first=False):
                                for g in range(GROUPS):
                                    if not (first and k == 0 and g == 0):
                                        rows1.high(act, i, k, g)
                                    if g == 1 and not first:
                                        act.wait_ge(x1_stored[k], START + DMA * (i - 1))
                                        norm1.apply(act, i - 1, k, x1_tile[k][:])
                                    sum_inc(i, k, g)
                                    if g == 3 and not (first and k == 0):
                                        norm1.root(act, i - 1 + k, 1 - k)

                            for k in range(2):
                                tile(0, k, first=True)
                            with act.Fori(1, PAIRS) as i:
                                for k in range(2):
                                    tile(i, k)
                            act.wait_ge(x1_stored[0], START + DMA * (PAIRS - 1))
                            norm1.apply(act, PAIRS - 1, 0, x1_tile[0][:])
                            norm1.root(act, PAIRS - 1, 1)
                            act.wait_ge(x1_stored[1], START + DMA * (PAIRS - 1))
                            norm1.apply(act, PAIRS - 1, 1, x1_tile[1][:])

                        layer0()
                        layer1()

                    @block.vector
                    def _(dve):
                        start(dve, 4, 5)
                        def layer0():
                            def count_positives(i, k, u):
                                t = 2 * i + k
                                dve.wait_ge(half_in[k][u], START + DMA * (i + 1))
                                dve.wait_ge(positives_counted[2 * (1 - k) + u], START + i + k)
                                dve.tensor_scalar(positive_mark[u][:], half_rows[k][u][:], 0.0, 0.0, ALU.is_gt,
                                                  ALU.add, accum_out=positives[:, bass.ds(t, 1), u:u + 1].rearrange(
                                                      "p o u -> p (o u)")).then_inc(positives_counted[2 * k + u], 1)

                            def make_floor(i, k, u):
                                n = 2 * k + u
                                dve.wait_ge(masked_stored[n], START + DMA * i)
                                dve.wait_ge(half_in[k][u], START + DMA * (i + 1))
                                dve.tensor_scalar(grouped(masked[n][:]), by_c(half_rows[k][u][:]), 0.0, NEVER, ALU.is_equal, ALU.mult).then_inc(floor_done[n], 1)

                            def residual(i, k):
                                norm0.residual(dve, i, k, rows0, mix_col[:, 0:1], tile_of(xa, 2 * i + k))

                            def tile(i, k, first=False):
                                before = not (first and k == 0)
                                rows0.low(dve, i, k, 0)
                                if not first:
                                    norm0.scale_and_shift(dve, i - 1, k)
                                make_floor(i, k, 0)
                                rows0.low(dve, i, k, 1)
                                if before:
                                    residual(i - 1 + k, 1 - k)
                                make_floor(i, k, 1)
                                if before:
                                    norm0.await_stats(dve, i - 1 + k, 1 - k)
                                rows0.low(dve, i, k, 2)
                                if before:
                                    norm0.variance(dve, i - 1 + k, 1 - k)
                                count_positives(i, k, 0)
                                rows0.low(dve, i, k, 3)
                                count_positives(i, k, 1)

                            for k in range(2):
                                tile(0, k, first=True)
                            with dve.Fori(1, PAIRS) as i:
                                for k in range(2):
                                    tile(i, k)
                            norm0.scale_and_shift(dve, PAIRS - 1, 0)
                            for n in range(4):
                                dve.wait_ge(positives_counted[n], START + PAIRS)
                            dve.tensor_tensor(positive_sum[:], positives[:, :, 0], positives[:, :, 1], ALU.add).then_inc(
                                small, 1)
                            for n in range(4):
                                dve.wait_ge(zeros_counted[n], START + PAIRS)
                            dve.tensor_tensor(zero_sum[:], zeros[:, :, 0], zeros[:, :, 1], ALU.add).then_inc(
                                zero_sum_done, 1)
                            dve.wait_ge(length_done, START + 1)
                            dve.tensor_scalar(length[:], length[:], NORM_EPS, None, ALU.max).then_inc(small, 1)
                            dve.wait_ge(small, START + 2)
                            dve.reciprocal(head[:], length[:]).then_inc(small, 1)

                        def layer1():
                            def mark_positives(i, k, g):
                                dve.wait_ge(half_in[k][g // 2], START + DMA * (PAIRS + i + 1))
                                dve.tensor_scalar(inc[g][:], adj_part(k, g * BANK, BANK), 0.0,
                                                  head[:, bass.ds(2 * i + k, 1)], ALU.is_gt, ALU.mult).then_inc(
                                    head_part[g], 1)

                            def inverse_degree(i, k):
                                for g in range(GROUPS):
                                    dve.wait_ge(inc_summed[g], START + 2 * i + k + 1)
                                dve.tensor_reduce(degree[k][:], degree_part[k][:], AX_X, ALU.add).then_inc(
                                    degree_done[k], 1)
                                dve.wait_ge(degree_done[k], START + i + 1)
                                dve.reciprocal(inv_degree[k][:], degree[k][:]).then_inc(inv_degree_done[k], 1)

                            def residual(i, k):
                                dve.wait_ge(inv_degree_done[k], START + i + 1)
                                norm1.residual(dve, i, k, rows1, inv_degree[k][:, 0:1], tile_of(xa, 2 * i + k))

                            def tile(i, k, first=False, more=True):
                                before = not (first and k == 0)
                                j, l = i - 1 + k, 1 - k
                                for g in range(GROUPS):
                                    if g == 2 and before:
                                        norm1.await_stats(dve, j, l)
                                    if not (first and k == 0 and g == 0):
                                        rows1.low(dve, i, k, g)
                                    if g == 0 and not first:
                                        norm1.scale_and_shift(dve, i - 1, k)
                                    if g == 0 and before:
                                        inverse_degree(j, l)
                                    if g == 1 and before:
                                        residual(j, l)
                                    if g == 2 and before:
                                        norm1.variance(dve, j, l)
                                    if more:
                                        dve.wait_ge(inc_summed[g], START + 2 * i + k + 1)
                                        mark_positives(i + k, 1 - k, g)

                            dve.wait_ge(small, START + 3)
                            for g in range(GROUPS):
                                mark_positives(0, 0, g)
                            norm0.residual(dve, PAIRS - 1, 1, rows0, mix_col[:, 0:1], xa[:, T - 1, :])
                            norm0.await_stats(dve, PAIRS - 1, 1)
                            norm0.variance(dve, PAIRS - 1, 1)
                            rows1.low(dve, 0, 0, 0)
                            norm0.scale_and_shift(dve, PAIRS - 1, 1)
                            for k in range(2):
                                dve.wait_ge(norm0.normed[k], START + PAIRS)
                            for k in range(2):
                                tile(0, k, first=True)
                            with dve.Fori(1, PAIRS - 1) as i:
                                for k in range(2):
                                    tile(i, k)
                            tile(PAIRS - 1, 0)
                            tile(PAIRS - 1, 1, more=False)
                            norm1.scale_and_shift(dve, PAIRS - 1, 0)
                            inverse_degree(PAIRS - 1, 1)
                            residual(PAIRS - 1, 1)
                            norm1.await_stats(dve, PAIRS - 1, 1)
                            norm1.variance(dve, PAIRS - 1, 1)
                            norm1.scale_and_shift(dve, PAIRS - 1, 1)

                        layer0()
                        layer1()
        clear_spent()

        late = ExitStack()
        whole.enter_context(late)
        total = sb(late, "total", [P, T, D])
        mean_var_all = sb(late, "mean_var_all", [P, T, 2])
        degree = sb(late, "degree", [P, T])
        with ExitStack() as s4:
            x1_head = sb(s4, "x1_head", [P, 2, D])
            xT_high = sb(s4, "xT_high", [P, K, R], F32R)
            xT_low = sb(s4, "xT_low", [P, K, R], F32R)
            wo_raw = sb(s4, "wo_raw", [P, K, D])
            wo_high = sb(s4, "wo_high", [P, K, D], F32R)
            wo_low = sb(s4, "wo_low", [P, K, D], F32R)
            wk_raw, wvt_raw = ([sb(s4, f"{w}_raw{k}", [P, K, D]) for k in range(2)] for w in ("wk", "wvt"))
            wk_high, wk_low, wvt_high, wvt_low, fold_high, fold_low = (
                [sb(s4, f"{w}{k}", [P, K, D], F32R) for k in range(2)]
                for w in ("wk_high", "wk_low", "wvt_high", "wvt_low", "fold_high", "fold_low"))
            wq_raw = sb(s4, "wq_raw", [P, K, D])
            wq_high = sb(s4, "wq_high", [P, K, D], F32R)
            wq_low = sb(s4, "wq_low", [P, K, D], F32R)
            qT_high = sb(s4, "qT_high", [P, K, R], F32R)
            qT_low = sb(s4, "qT_low", [P, K, R], F32R)
            kT_high = sb(s4, "kT_high", [P, K, N], F32R)
            kT_low = sb(s4, "kT_low", [P, K, N], F32R)
            vals = sb(s4, "vals", [P, T, 2, D], F32R)
            masked_in = [sb(s4, f"masked_in{b}", [P, N]) for b in range(2)]
            probs = [sb(s4, f"probs{b}", [P, N]) for b in range(2)]
            pT_high = sb(s4, "pT_high", [P, T, P], F32R)
            pT_low = sb(s4, "pT_low", [P, T, P], F32R)
            column_sum = sb(s4, "column_sum", [P, N])
            adj_piece = sb(s4, "adj_piece", [P, 2, R])
            piece_sum = sb(s4, "piece_sum", [P, R])
            stats2 = [sb(s4, f"stats2_{b}", [P, 6]) for b in range(2)]
            mean_var2 = [sb(s4, f"mean_var2_{b}", [P, 2]) for b in range(2)]
            zero_count = sb(s4, "zero_count", [P, T])
            least = sb(s4, "least", [P, T])
            least_tmp = sb(s4, "least_tmp", [P, T])
            chunk_max = [sb(s4, f"chunk_max{b}", [P, GROUPS]) for b in range(2)]
            early_max = sb(s4, "early_max", [P, 1])
            row_max = [sb(s4, f"row_max{b}", [P, 1]) for b in range(2)]
            neg_max = [sb(s4, f"neg_max{b}", [P, 1]) for b in range(2)]
            masked_exp = [sb(s4, f"masked_exp{b}", [P, 1]) for b in range(2)]
            chunk_sum = [sb(s4, f"chunk_sum{b}", [P, GROUPS]) for b in range(2)]
            row_total = [sb(s4, f"row_total{b}", [P, 1]) for b in range(2)]
            denom = [sb(s4, f"denom{b}", [P, 1]) for b in range(2)]
            inv_denom = [sb(s4, f"inv_denom{b}", [P, 1]) for b in range(2)]
            s_bank, t_bank, o_bank, m_bank = (
                [s4.enter_context(nc.psum_tensor(f"{n}_bank{b}", [P, BANK], F32)) for b in range(2)]
                for n in ("s", "t", "o", "m"))

            total_in = sem(s4, "total_in")
            count_in = sem(s4, "count_in")
            least_done = sem(s4, "least_done")
            x1_in = sem(s4, "x1_in")
            xT_full = sem(s4, "xT_full")
            xT_high_done = sem(s4, "xT_high_done")
            xT_low_done = sem(s4, "xT_low_done")
            wo_in = sem(s4, "wo_in")
            wo_high_done = sem(s4, "wo_high_done")
            wo_low_done = sem(s4, "wo_low_done")
            wk_in, wvt_in, wk_high_done, wk_low_done, wvt_high_done, wvt_low_done = (
                sems(s4, f"{n}_") for n in
                ("wk_in", "wvt_in", "wk_high_done", "wk_low_done", "wvt_high_done", "wvt_low_done"))
            fold_full, fold_high_done, fold_low_done = (
                sems(s4, f"{n}_") for n in ("fold_full", "fold_high_done", "fold_low_done"))
            k_full, k_high_done, k_low_done = (sems(s4, f"{n}_") for n in ("k_full", "k_high_done", "k_low_done"))
            v_full, v_high_done, v_low_done = (sems(s4, f"{n}_") for n in ("v_full", "v_high_done", "v_low_done"))
            wq_in = sem(s4, "wq_in")
            wq_high_done = sem(s4, "wq_high_done")
            wq_low_done = sem(s4, "wq_low_done")
            q_full = sem(s4, "q_full")
            q_high_done = sem(s4, "q_high_done")
            q_low_done = sem(s4, "q_low_done")
            bias_in = sems(s4, "bias_in")
            s_full = sems(s4, "s_full")
            s_done = sems(s4, "s_done")
            first_max_done = sem(s4, "first_max_done")
            early_max_done = sem(s4, "early_max_done")
            max_done = sems(s4, "max_done")
            neg_done = sems(s4, "neg_done")
            masked_exp_done = sems(s4, "masked_exp_done")
            exp_done = sems(s4, "exp_done")
            t_full = sems(s4, "t_full")
            pT_high_done = sems(s4, "pT_high_done")
            pT_low_done = sems(s4, "pT_low_done")
            sum_done = sems(s4, "sum_done")
            denom_done = sems(s4, "denom_done")
            inv_done = sems(s4, "inv_done")
            o_full = sems(s4, "o_full")
            o_half = sems(s4, "o_half")
            o_done = sems(s4, "o_done")
            piece_in = sem(s4, "piece_in")
            column_sum_zeroed = sem(s4, "column_sum_zeroed")
            piece_paired = sem(s4, "piece_paired")
            piece_added = sem(s4, "piece_added")
            sums_turned = sem(s4, "sums_turned")
            degree_done = sem(s4, "degree_done")
            stats2_done = sems(s4, "stats2_done")
            var2_done = sems(s4, "var2_done")
            var2_kept = sems(s4, "var2_kept")

            half_scale = 0.5 * float(D) ** -0.5
            PAIRS_C = C // 2
            halves = lambda bank: bank[:].rearrange("p (k n) -> p k n", k=K)

            def three_products(pe, dst, left, right, cols):
                for kk in range(K):
                    for n, (a, b) in enumerate(((left[0], right[0]), (left[0], right[1]), (left[1], right[0]))):
                        mm = pe.matmul(dst, a[:, kk, cols], b[:, kk, :], start=(kk == 0 and n == 0),
                                       stop=(kk == K - 1 and n == 2))
                return mm

            with next_block() as block:
                @block.sync
                def _(sp):
                    start(sp, 0, 5)
                    bias_rows = bias_scratch.rearrange("(b r c) m -> b c r m", b=2, c=C)

                    def load_keys_weights(h, jj, k):
                        c, n = 2 * jj + k, PAIRS_C * h + jj
                        sp.wait_ge(wvt_low_done[k], START + n)
                        sp.dma_start(wvt_raw[k][:], wvt_scratch[bass.ds(c, 1)].rearrange("o p k n -> (o p) k n")
                                     ).then_inc(wvt_in[k], DMA)
                        sp.wait_ge(wk_low_done[k], START + n)
                        sp.dma_start(wk_raw[k][:], wk[:, bass.ds(c * D, D)].rearrange("(k p) n -> p k n", p=P)
                                     ).then_inc(wk_in[k], DMA)

                    def load_query_weights(c, use):
                        sp.wait_ge(wq_low_done, START + use)
                        sp.dma_start(wq_raw[:], wq[:, bass.ds(c * D, D)].rearrange("(k p) n -> p k n", p=P)
                                     ).then_inc(wq_in, DMA)

                    def load_masked(c, use):
                        for b in range(2):
                            sp.wait_ge(neg_done[b], START + use)
                            sp.dma_start(masked_in[b][:], bias_rows[b, bass.ds(c, 1)].rearrange("o r m -> (o r) m")
                                         ).then_inc(bias_in[b], DMA)

                    def load_piece(h, c, use):
                        sp.wait_ge(piece_paired, START + use)
                        sp.dma_start(adj_piece[:], adj[bass.ds(h * R, R), bass.ds(c * R, R)].rearrange(
                            "(a p) m -> p a m", p=P)).then_inc(piece_in, DMA)

                    def load_head(h):
                        sp.wait_ge(wo_low_done, START + h)
                        sp.dma_start(wo_raw[:], wout[bass.ds(h * D, D), :].rearrange("(k p) n -> p k n", p=P)
                                     ).then_inc(wo_in, DMA)
                        sp.wait_ge(xT_full, START + h)
                        sp.dma_start(x1_head[:], x1_scratch[bass.ds(h * R, R), :].rearrange("(a p) d -> p a d", p=P)
                                     ).then_inc(x1_in, DMA)
                        for k in range(2):
                            load_keys_weights(h, 0, k)
                        load_query_weights(0, h * C)
                        load_piece(h, 0, h * C)
                        load_masked(0, h * C)

                    def head(h, more):
                        with sp.Fori(1, PAIRS_C) as jj:
                            for k in range(2):
                                load_keys_weights(h, jj, k)
                        with sp.Fori(1, C) as c:
                            load_query_weights(c, h * C + c)
                            load_piece(h, c, h * C + c)
                            load_masked(c, h * C + c)
                        if more:
                            load_head(h + 1)

                    sp.dma_start(zero_count[:].rearrange("p (a c) -> p a c", a=2),
                                 zeros_scratch.rearrange("(a r c) o -> r a (c o)", a=2, c=C)).then_inc(count_in, DMA)
                    for k in range(2):
                        sp.wait_ge(x1_stored[k], START + DMA * PAIRS // 2)
                    load_head(0)
                    for k in range(2):
                        sp.wait_ge(x1_stored[k], START + DMA * PAIRS)
                    sp.dma_start(total[:].rearrange("p (a c) d -> p a (c d)", a=2),
                                 x1_scratch.rearrange("(a r c) d -> r a (c d)", a=2, c=C)).then_inc(total_in, DMA)
                    with sp.Fori(0, H - 1) as h:
                        head(h, True)
                    head(H - 1, False)

                @block.tensor
                def _(pe):
                    start(pe, 1, 5)
                    def turn_x(h):
                        pe.wait_ge(x1_in, START + DMA * (h + 1))
                        for kk in range(K):
                            for a in range(2):
                                mm = pe.transpose(m_bank[0][:, kk * R + a * P:kk * R + (a + 1) * P],
                                                  x1_head[:, a, kk * P:(kk + 1) * P], ident[:])
                        mm.then_inc(xT_full, 1)

                    def fold_values(h, jj, k):
                        n = PAIRS_C * h + jj
                        pe.wait_ge(wvt_low_done[k], START + n + 1)
                        pe.wait_ge(fold_low_done[1 - k], START + n + k)
                        for a in range(2):
                            mm = three_products(pe, m_bank[0][:, a * D:(a + 1) * D], (wvt_high[k], wvt_low[k]),
                                                (wo_high, wo_low), slice(a * P, (a + 1) * P))
                        mm.then_inc(fold_full[k], 1)

                    def keys(h, jj, k):
                        n = PAIRS_C * h + jj
                        pe.wait_ge(wk_low_done[k], START + n + 1)
                        pe.wait_ge(k_low_done[1 - k], START + n + k)
                        if k == 1:
                            pe.wait_ge(q_low_done, START + h * C + 1)
                        for dh in range(K):
                            mm = three_products(pe, m_bank[1][:, dh * R:(dh + 1) * R], (wk_high[k], wk_low[k]),
                                                (xT_high, xT_low), slice(dh * P, (dh + 1) * P))
                        mm.then_inc(k_full[k], 1)

                    def values(h, jj, k):
                        n = PAIRS_C * h + jj
                        pe.wait_ge(fold_low_done[k], START + n + 1)
                        pe.wait_ge(v_low_done[k], START + n)
                        pe.wait_ge(o_done[k], START + h * C)
                        for a in range(2):
                            mm = three_products(pe, o_bank[k][:, a * D:(a + 1) * D], (xT_high, xT_low),
                                                (fold_high[k], fold_low[k]), slice(a * P, (a + 1) * P))
                        mm.then_inc(v_full[k], 1)

                    def queries(use):
                        pe.wait_ge(wq_low_done, START + use + 1)
                        for dh in range(K):
                            mm = three_products(pe, m_bank[1][:, dh * R:(dh + 1) * R], (wq_high, wq_low),
                                                (xT_high, xT_low), slice(dh * P, (dh + 1) * P))
                        mm.then_inc(q_full, 1)

                    def scores(b, use, j):
                        bank = j % 2
                        if j == 0:
                            pe.wait_ge(q_low_done, START + use + 1)
                        pe.wait_ge(s_done[bank], START + 2 * (2 * use + b) + j // 2)
                        for dh in range(K):
                            for n, (a, kT) in enumerate(((qT_high, kT_high), (qT_high, kT_low), (qT_low, kT_high))):
                                mm = pe.matmul(s_bank[bank][:], a[:, dh, b * P:(b + 1) * P],
                                               kT[:, dh, j * BANK:(j + 1) * BANK], start=(dh == 0 and n == 0),
                                               stop=(dh == K - 1 and n == 2))
                        mm.then_inc(s_full[bank], 1)

                    def turns(b, use, g):
                        pe.wait_ge(exp_done[b], START + GROUPS * use + g + 1)
                        pe.wait_ge(pT_low_done[g % 2], START + 2 * (2 * use + b) + g // 2)
                        for a in range(TPB):
                            at = (g * TPB + a) * P
                            mm = pe.transpose(t_bank[g % 2][:, a * P:(a + 1) * P], probs[b][:, at:at + P], ident[:])
                        mm.then_inc(t_full[g % 2], 1)

                    def weigh(h, b, use, g):
                        if g == 0:
                            pe.wait_ge(o_done[b], START + use)
                            pe.wait_ge(v_low_done[b], START + PAIRS_C * (h + 1))
                        if g == GROUPS - 1:
                            pe.wait_ge(v_low_done[1], START + PAIRS_C * (h + 1))
                        pe.wait_ge(pT_low_done[g % 2], START + 2 * (2 * use + b) + g // 2 + 1)
                        for t in range(g * TPB, (g + 1) * TPB):
                            pe.matmul(o_bank[b][:], pT_high[:, t, :], vals[:, t, :, :].rearrange("p s d -> p (s d)"),
                                      start=(t == 0), stop=False)
                            mm = pe.matmul(o_bank[b][:, 0:D], pT_low[:, t, :], vals[:, t, 0, :], start=False,
                                           stop=(t == T - 1))
                        if g == GROUPS - 1:
                            mm.then_inc(o_full[b], 1)

                    def first_of_head(h, amid=(lambda n: None)):
                        amid(0)
                        pe.wait_ge(xT_low_done, START + h + 1)
                        pe.wait_ge(wo_low_done, START + h + 1)
                        fold_values(h, 0, 0)
                        amid(1)
                        pe.wait_ge(q_low_done, START + h * C)
                        keys(h, 0, 0)
                        amid(2)
                        fold_values(h, 0, 1)
                        amid(3)
                        pe.wait_ge(k_low_done[0], START + PAIRS_C * h + 1)
                        queries(h * C)
                        amid(4)

                    def step(h, b, use, next_queries=False, next_head=False):
                        turns(b, use, 0)
                        turns(b, use, 1)
                        scores(1 - b, use + b, 0)
                        turns(b, use, 2)
                        scores(1 - b, use + b, 1)
                        turns(b, use, 3)
                        scores(1 - b, use + b, 2)
                        weigh(h, b, use, 0)
                        scores(1 - b, use + b, 3)
                        if next_queries:
                            queries(use + 1)
                        if next_head:
                            turn_x(h + 1)
                        for g in range(1, GROUPS):
                            weigh(h, b, use, g)

                    def last_step(h, use, next_head):
                        turn = lambda *groups: [turns(1, use, g) for g in groups]
                        weigh_all = lambda *groups: [weigh(h, 1, use, g) for g in groups]
                        parts = (lambda: turn(0, 1), lambda: turn(2), lambda: (turn(3), weigh_all(0)),
                                 lambda: weigh_all(1), lambda: weigh_all(2, 3))
                        if next_head:
                            first_of_head(h + 1, lambda n: parts[n]())
                        else:
                            parts[0]()
                            turn_column_sums()
                            for part in parts[1:]:
                                part()

                    def turn_column_sums():
                        permuted = column_sum[:].rearrange("p (a r c) -> p a c r", a=2, c=C)
                        pe.wait_ge(piece_added, START + H * C)
                        for g in range(GROUPS):
                            bank = m_bank[g % 2]
                            if g >= 2:
                                pe.wait_ge(degree_done, START + g - 1)
                            for t in range(g * TPB, (g + 1) * TPB):
                                mm = pe.transpose(bank[:, t % TPB * P:(t % TPB + 1) * P],
                                                  permuted[:, t // C, t % C, :], ident[:])
                            mm.then_inc(sums_turned, 1)

                    def head(h, more):
                        with pe.Fori(0, PAIRS_C - 1) as jj:
                            keys(h, jj, 1)
                            values(h, jj, 0)
                            fold_values(h, jj + 1, 0)
                            keys(h, jj + 1, 0)
                            values(h, jj, 1)
                            fold_values(h, jj + 1, 1)
                        for k in range(2):
                            pe.wait_ge(k_low_done[k], START + PAIRS_C * h + PAIRS_C - 1)
                        scores(0, h * C, 0)
                        keys(h, PAIRS_C - 1, 1)
                        scores(0, h * C, 1)
                        scores(0, h * C, 2)
                        for k in range(2):
                            pe.wait_ge(k_low_done[k], START + PAIRS_C * (h + 1))
                        scores(0, h * C, 3)
                        values(h, PAIRS_C - 1, 0)
                        values(h, PAIRS_C - 1, 1)
                        with pe.Fori(0, C - 1) as c:
                            step(h, 0, h * C + c, next_queries=True)
                            step(h, 1, h * C + c)
                        step(h, 0, h * C + C - 1, next_head=more)
                        last_step(h, h * C + C - 1, more)

                    turn_x(0)
                    first_of_head(0)
                    with pe.Fori(0, H - 1) as h:
                        head(h, True)
                    head(H - 1, False)

                @block.scalar
                def _(act):
                    start(act, 2, 5)
                    def split_x(h):
                        act.wait_ge(xT_full, START + h + 1)
                        act.activation(xT_high[:], halves(m_bank[0]), ACT.Copy).then_inc(xT_high_done, 1)

                    def split_out_weights(h):
                        act.wait_ge(wo_in, START + DMA * (h + 1))
                        act.activation(wo_high[:], wo_raw[:], ACT.Copy).then_inc(wo_high_done, 1)

                    def split_keys_weights(h, jj, k):
                        n = PAIRS_C * h + jj
                        act.wait_ge(fold_full[k], START + n)
                        act.wait_ge(wvt_in[k], START + DMA * (n + 1))
                        act.activation(wvt_high[k][:], wvt_raw[k][:], ACT.Copy).then_inc(wvt_high_done[k], 1)
                        act.wait_ge(k_full[k], START + n)
                        act.wait_ge(wk_in[k], START + DMA * (n + 1))
                        act.activation(wk_high[k][:], wk_raw[k][:], ACT.Copy).then_inc(wk_high_done[k], 1)

                    def fold_high_part(h, jj, k):
                        n = PAIRS_C * h + jj
                        act.wait_ge(fold_full[k], START + n + 1)
                        act.wait_ge(v_full[k], START + n)
                        act.activation(fold_high[k][:], halves(m_bank[0]), ACT.Copy).then_inc(fold_high_done[k], 1)

                    def keys_high_part(h, jj, k):
                        act.wait_ge(k_full[k], START + PAIRS_C * h + jj + 1)
                        act.activation(kT_high[:, :, bass.ds((2 * jj + k) * R, R)], halves(m_bank[1]),
                                       ACT.Copy).then_inc(k_high_done[k], 1)

                    def values_high_part(h, jj, k):
                        act.wait_ge(v_full[k], START + PAIRS_C * h + jj + 1)
                        act.activation(vals[:, bass.ds(2 * (2 * jj + k), 2), 0, :], halves(o_bank[k]),
                                       ACT.Copy).then_inc(v_high_done[k], 1)

                    def split_query_weights(use):
                        act.wait_ge(wq_in, START + DMA * (use + 1))
                        act.wait_ge(q_full, START + use)
                        act.activation(wq_high[:], wq_raw[:], ACT.Copy).then_inc(wq_high_done, 1)

                    def evacuate_queries(use):
                        act.wait_ge(q_full, START + use + 1)
                        act.activation(qT_high[:], halves(m_bank[1]), ACT.Copy, scale=half_scale).then_inc(
                            q_high_done, 1)

                    def exps(b, use, j):
                        if j == 0:
                            act.wait_ge(neg_done[b], START + use + 1)
                            act.wait_ge(inv_done[b], START + use)
                            act.activation(masked_exp[b][:], neg_max[b][:], ACT.Exp, bias=masked_col[:, 0:1]).then_inc(
                                masked_exp_done[b], 1)
                        part = probs[b][:, j * BANK:(j + 1) * BANK]
                        act.activation(part, part, ACT.Exp, bias=neg_max[b][:, 0:1], scale=2.0,
                                       accum_out=chunk_sum[b][:, j:j + 1]).then_inc(exp_done[b], 1)

                    def prob_high(b, use, g):
                        act.wait_ge(t_full[g % 2], START + 2 * (2 * use + b) + g // 2 + 1)
                        act.activation(pT_high[:, g * TPB:(g + 1) * TPB, :], t_bank[g % 2][:].rearrange(
                            "p (a n) -> p a n", a=TPB), ACT.Copy).then_inc(pT_high_done[g % 2], 1)

                    def step(h, b, use, next_queries=False, next_weights=False, next_x=False, next_products=False):
                        exps(b, use, 0)
                        exps(b, use, 1)
                        prob_high(b, use, 0)
                        exps(b, use, 2)
                        prob_high(b, use, 1)
                        exps(b, use, 3)
                        if next_products:
                            fold_high_part(h + 1, 0, 0)
                        prob_high(b, use, 2)
                        if next_queries:
                            split_query_weights(use + 1)
                        if next_products:
                            keys_high_part(h + 1, 0, 0)
                        if next_weights:
                            split_out_weights(h + 1)
                        prob_high(b, use, 3)
                        if next_queries:
                            evacuate_queries(use + 1)
                        if next_weights:
                            split_keys_weights(h + 1, 0, 0)
                        if next_x:
                            split_x(h + 1)
                            split_keys_weights(h + 1, 0, 1)
                            split_query_weights(use + 1)
                        if next_products:
                            fold_high_part(h + 1, 0, 1)
                            evacuate_queries(use + 1)

                    def head(h, more):
                        with act.Fori(0, PAIRS_C - 1) as jj:
                            for k in range(2):
                                split_keys_weights(h, jj + 1, k)
                                keys_high_part(h, jj + k, 1 - k)
                                values_high_part(h, jj, k)
                                fold_high_part(h, jj + 1, k)
                        keys_high_part(h, PAIRS_C - 1, 1)
                        values_high_part(h, PAIRS_C - 1, 0)
                        with act.Fori(0, C - 1) as c:
                            step(h, 0, h * C + c, next_queries=True)
                            step(h, 1, h * C + c)
                        step(h, 0, h * C + C - 1, next_weights=more, next_x=more)
                        step(h, 1, h * C + C - 1, next_products=more)

                    act.activation(masked_exp[0][:], masked_col[:], ACT.Exp).then_inc(masked_exp_done[0], 1)
                    split_out_weights(0)
                    split_x(0)
                    split_keys_weights(0, 0, 0)
                    split_keys_weights(0, 0, 1)
                    split_query_weights(0)
                    fold_high_part(0, 0, 0)
                    keys_high_part(0, 0, 0)
                    fold_high_part(0, 0, 1)
                    evacuate_queries(0)
                    with act.Fori(0, H - 1) as h:
                        head(h, True)
                    head(H - 1, False)
                @block.gpsimd
                def _(pool):
                    start(pool, 4, 5)
                    def low(dst, source, high):
                        return pool.tensor_tensor(dst, source, plain(high), ALU.subtract)

                    def split_out_weights(h):
                        pool.wait_ge(wo_high_done, START + h + 1)
                        low(wo_low[:], wo_raw[:], wo_high[:]).then_inc(wo_low_done, 1)

                    def split_keys_weights(h, jj, k):
                        n = PAIRS_C * h + jj
                        pool.wait_ge(wvt_high_done[k], START + n + 1)
                        low(wvt_low[k][:], wvt_raw[k][:], wvt_high[k][:]).then_inc(wvt_low_done[k], 1)
                        pool.wait_ge(wk_high_done[k], START + n + 1)
                        low(wk_low[k][:], wk_raw[k][:], wk_high[k][:]).then_inc(wk_low_done[k], 1)

                    def split_query_weights(use):
                        pool.wait_ge(wq_high_done, START + use + 1)
                        low(wq_low[:], wq_raw[:], wq_high[:]).then_inc(wq_low_done, 1)

                    def split_first_weights(h):
                        split_out_weights(h)
                        split_keys_weights(h, 0, 0)
                        split_keys_weights(h, 0, 1)
                        query_weights_and_piece(0, h * C)

                    def pair_piece(use):
                        pool.wait_ge(column_sum_zeroed, START + 1)
                        pool.wait_ge(piece_in, START + DMA * (use + 1))
                        pool.wait_ge(piece_added, START + use)
                        pool.tensor_tensor(piece_sum[:], adj_piece[:, 0, :], adj_piece[:, 1, :], ALU.add).then_inc(
                            piece_paired, 1)

                    def add_piece(c):
                        mine = column_sum[:, bass.ds(c * R, R)]
                        pool.tensor_tensor(mine, mine, piece_sum[:], ALU.add).then_inc(piece_added, 1)

                    def query_weights_and_piece(c, use):
                        pair_piece(use)
                        pool.wait_ge(piece_paired, START + use + 1)
                        split_query_weights(use)
                        add_piece(c)

                    def head(h, more):
                        with pool.Fori(1, PAIRS_C) as jj:
                            for k in range(2):
                                split_keys_weights(h, jj, k)
                        with pool.Fori(1, C) as c:
                            query_weights_and_piece(c, h * C + c)
                        if more:
                            split_first_weights(h + 1)

                    split_first_weights(0)
                    with pool.Fori(0, H - 1) as h:
                        head(h, True)
                    head(H - 1, False)

                @block.vector
                def _(dve):
                    start(dve, 3, 5)
                    def low(dst, source, high):
                        return dve.tensor_tensor(dst, source, plain(high), ALU.subtract)

                    def split_x(h):
                        dve.wait_ge(xT_high_done, START + h + 1)
                        low(xT_low[:], halves(m_bank[0]), xT_high[:]).then_inc(xT_low_done, 1)

                    def fold_low_part(h, jj, k):
                        dve.wait_ge(fold_high_done[k], START + PAIRS_C * h + jj + 1)
                        low(fold_low[k][:], halves(m_bank[0]), fold_high[k][:]).then_inc(fold_low_done[k], 1)

                    def keys_low_part(h, jj, k):
                        at = bass.ds((2 * jj + k) * R, R)
                        dve.wait_ge(k_high_done[k], START + PAIRS_C * h + jj + 1)
                        low(kT_low[:, :, at], halves(m_bank[1]), kT_high[:, :, at]).then_inc(k_low_done[k], 1)

                    def values_low_part(h, jj, k):
                        at = bass.ds(2 * (2 * jj + k), 2)
                        dve.wait_ge(v_high_done[k], START + PAIRS_C * h + jj + 1)
                        low(vals[:, at, 1, :], halves(o_bank[k]), vals[:, at, 0, :]).then_inc(v_low_done[k], 1)

                    def evacuate_queries(use):
                        dve.wait_ge(q_high_done, START + use + 1)
                        dve.scalar_tensor_tensor(out=qT_low[:], in0=halves(m_bank[1]), scalar=half_scale,
                                                 in1=plain(qT_high[:]), op0=ALU.mult, op1=ALU.subtract).then_inc(
                            q_low_done, 1)

                    def await_scores(b, use, j):
                        dve.wait_ge(s_full[j % 2], START + 2 * (2 * use + b) + j // 2 + 1)

                    def masked_scores(b, use, j):
                        at = slice(j * BANK, (j + 1) * BANK)
                        dve.tensor_tensor_reduce(probs[b][:, at], s_bank[j % 2][:], masked_in[b][:, at], 1.0, NEVER,
                                                 ALU.add, ALU.max, chunk_max[b][:, j:j + 1]).then_inc(s_done[j % 2], 1)

                    def masked_scores_alone(use, j, await_next):
                        at = slice(j * BANK, (j + 1) * BANK)
                        await_scores(0, use, j)
                        dve.tensor_tensor(probs[0][:, at], s_bank[j % 2][:], masked_in[0][:, at], ALU.add).then_inc(
                            s_done[j % 2], 1)
                        dve.wait_ge(s_done[j % 2], START + 2 * (2 * use) + j // 2 + 1)
                        if await_next:
                            await_scores(0, use, j + 1)
                        dve.tensor_reduce(chunk_max[0][:, j:j + 1], probs[0][:, at], AX_X, ALU.max).then_inc(
                            first_max_done, 1)

                    def early_maximum(use, first):
                        dve.wait_ge(s_done[0], START + 2 * (2 * use) + 2)
                        dve.wait_ge(s_done[1], START + 2 * (2 * use) + 1)
                        dve.wait_ge(first_max_done, START + 2 * (first + 1))
                        await_scores(0, use, GROUPS - 1)
                        dve.tensor_reduce(early_max[:], chunk_max[0][:, 0:GROUPS - 1], AX_X, ALU.max).then_inc(
                            early_max_done, 1)

                    def row_maximum(b, use, c, first=None):
                        for bank in range(2):
                            dve.wait_ge(s_done[bank], START + 2 * (2 * use + b) + 2)
                        if first is not None:
                            dve.wait_ge(early_max_done, START + first + 1)
                            dve.tensor_tensor(row_max[b][:], early_max[:], chunk_max[b][:, GROUPS - 1:GROUPS],
                                              ALU.max).then_inc(max_done[b], 1)
                        else:
                            dve.tensor_reduce(row_max[b][:], chunk_max[b][:], AX_X, ALU.max).then_inc(max_done[b], 1)
                        dve.wait_ge(max_done[b], START + use + 1)
                        dve.tensor_scalar(neg_max[b][:], row_max[b][:], least[:, bass.ds(b * C + c, 1)], -2.0,
                                          ALU.max, ALU.mult).then_inc(neg_done[b], 1)

                    def prob_low(b, use, g):
                        dve.wait_ge(pT_high_done[g % 2], START + 2 * (2 * use + b) + g // 2 + 1)
                        low(pT_low[:, g * TPB:(g + 1) * TPB, :], t_bank[g % 2][:].rearrange("p (a n) -> p a n", a=TPB),
                            pT_high[:, g * TPB:(g + 1) * TPB, :]).then_inc(pT_low_done[g % 2], 1)

                    def denominator(b, use, c, ready):
                        dve.wait_ge(exp_done[b], START + GROUPS * (use + 1))
                        dve.tensor_reduce(row_total[b][:], chunk_sum[b][:], AX_X, ALU.add).then_inc(sum_done[b], 1)
                        dve.wait_ge(sum_done[b], START + use + 1)
                        dve.scalar_tensor_tensor(out=denom[b][:], in0=masked_exp[b][:],
                                                 scalar=zero_count[:, bass.ds(b * C + c, 1)], in1=row_total[b][:],
                                                 op0=ALU.mult, op1=ALU.add).then_inc(denom_done[b], 1)
                        ready(3)
                        dve.wait_ge(denom_done[b], START + use + 1)
                        dve.reciprocal(inv_denom[b][:], denom[b][:]).then_inc(inv_done[b], 1)

                    def add_head(b, use, c):
                        dve.wait_ge(o_full[b], START + use + 1)
                        dve.wait_ge(inv_done[b], START + use + 1)
                        mine = total[:, bass.ds(b * C + c, 1), :].rearrange("p o d -> p (o d)")
                        dve.scalar_tensor_tensor(out=mine, in0=o_bank[b][:, 0:D], scalar=inv_denom[b][:, 0:1], in1=mine,
                                                 op0=ALU.mult, op1=ALU.add).then_inc(o_half[b], 1)
                        dve.wait_ge(o_half[b], START + use + 1)
                        dve.scalar_tensor_tensor(out=mine, in0=o_bank[b][:, D:2 * D], scalar=inv_denom[b][:, 0:1],
                                                 in1=mine, op0=ALU.mult, op1=ALU.add).then_inc(o_done[b], 1)

                    def await_total(b, use, c):
                        dve.wait_ge(o_done[b], START + use + 1)
                        dve.wait_ge(var2_done[b], START + c)

                    def statistics(b, c):
                        dve.bn_stats(stats2[b][:], total[:, bass.ds(b * C + c, 1), :].rearrange("p o d -> p (o d)")
                                     ).then_inc(stats2_done[b], 1)

                    def await_statistics(b, c):
                        dve.wait_ge(stats2_done[b], START + c + 1)
                        dve.wait_ge(var2_kept[b], START + c)

                    def variance(b):
                        dve.bn_aggr(mean_var2[b][:], stats2[b][:]).then_inc(var2_done[b], 1)

                    def keep_variance(b, c):
                        dve.wait_ge(var2_done[b], START + c + 1)
                        dve.tensor_copy(mean_var_all[:, bass.ds(b * C + c, 1), :].rearrange("p o d -> p (o d)"),
                                        mean_var2[b][:]).then_inc(var2_kept[b], 1)

                    def step(b, use, c, next_queries=False, next_head=None, finished=None):
                        ready = lambda j: await_scores(1 - b, use + b, j)
                        score = lambda j: masked_scores(1 - b, use + b, j)
                        prob_low(b, use, 0)
                        dve.wait_ge(bias_in[1 - b], START + DMA * (use + b + 1))
                        ready(0)
                        if finished is not None:
                            await_total(1 - b, use - 1 + b, finished)
                        prob_low(b, use, 1)
                        score(0)
                        if finished is not None:
                            statistics(1 - b, finished)
                            await_statistics(1 - b, finished)
                        ready(1)
                        prob_low(b, use, 2)
                        score(1)
                        if finished is not None:
                            variance(1 - b)
                        ready(2)
                        prob_low(b, use, 3)
                        score(2)
                        if finished is not None:
                            keep_variance(1 - b, finished)
                        denominator(b, use, c, ready)
                        score(3)
                        row_maximum(1 - b, use + b, c + b)
                        if next_queries:
                            evacuate_queries(use + 1)
                        if next_head is not None:
                            split_x(next_head)
                        add_head(b, use, c)

                    def add_column_sums(g):
                        dve.wait_ge(sums_turned, START + g + 1)
                        dve.tensor_reduce(degree[:, g * TPB:(g + 1) * TPB], m_bank[g % 2][:].rearrange(
                            "p (t n) -> p t n", t=TPB), AX_X, ALU.add).then_inc(degree_done, 1)

                    def last_step(use, c, next_head):
                        prob_low(1, use, 0)
                        prob_low(1, use, 1)
                        if next_head is None:
                            for g in range(GROUPS):
                                add_column_sums(g)
                        if next_head is not None:
                            fold_low_part(next_head, 0, 0)
                        prob_low(1, use, 2)
                        if next_head is not None:
                            keys_low_part(next_head, 0, 0)
                        prob_low(1, use, 3)
                        denominator(1, use, c, lambda j: None)
                        if next_head is not None:
                            fold_low_part(next_head, 0, 1)
                            evacuate_queries(use + 1)
                        add_head(1, use, c)

                    def head(h, next_head):
                        with dve.Fori(0, PAIRS_C - 1) as jj:
                            for k in range(2):
                                keys_low_part(h, jj + k, 1 - k)
                                values_low_part(h, jj, k)
                                fold_low_part(h, jj + 1, k)
                        use = h * C
                        dve.wait_ge(bias_in[0], START + DMA * (use + 1))
                        masked_scores_alone(use, 0, True)
                        masked_scores(0, use, 1)
                        keys_low_part(h, PAIRS_C - 1, 1)
                        masked_scores_alone(use, 2, False)
                        early_maximum(use, h)
                        masked_scores(0, use, 3)
                        row_maximum(0, use, 0, h)
                        values_low_part(h, PAIRS_C - 1, 0)
                        dve.wait_ge(v_full[1], START + PAIRS_C * (h + 1))
                        dve.tensor_copy(vals[:, T - 2:T, 0, :], halves(o_bank[1])).then_inc(v_high_done[1], 1)
                        values_low_part(h, PAIRS_C - 1, 1)
                        if next_head is not None:
                            with dve.Fori(0, C - 1) as c:
                                step(0, h * C + c, c, next_queries=True)
                                step(1, h * C + c, c)
                            step(0, h * C + C - 1, C - 1, next_head=next_head)
                            last_step(h * C + C - 1, C - 1, next_head)
                        else:
                            step(0, h * C, 0, next_queries=True)
                            step(1, h * C, 0, finished=0)
                            with dve.Fori(1, C - 1) as c:
                                step(0, h * C + c, c, next_queries=True, finished=c - 1)
                                step(1, h * C + c, c, finished=c)
                            step(0, h * C + C - 1, C - 1, finished=C - 2)
                            last_step(h * C + C - 1, C - 1, None)
                            for b in range(2):
                                await_total(b, h * C + C - 1, C - 1)
                                statistics(b, C - 1)
                            for b in range(2):
                                await_statistics(b, C - 1)
                                variance(b)
                            for b in range(2):
                                keep_variance(b, C - 1)

                    dve.memset(column_sum[:], 0.0).then_inc(column_sum_zeroed, 1)
                    split_x(0)
                    fold_low_part(0, 0, 0)
                    keys_low_part(0, 0, 0)
                    fold_low_part(0, 0, 1)
                    evacuate_queries(0)
                    dve.wait_ge(count_in, START + DMA)
                    dve.tensor_scalar(least[:], zero_count[:], 0.0, 0.5 * MASKED, ALU.is_gt, ALU.mult).then_inc(least_done, 1)
                    dve.tensor_scalar(least_tmp[:], zero_count[:], 0.0, NEVER, ALU.is_equal, ALU.mult).then_inc(
                        least_done, 1)
                    dve.wait_ge(least_done, START + 2)
                    dve.tensor_tensor(least[:], least[:], least_tmp[:], ALU.add).then_inc(least_done, 1)
                    dve.wait_ge(least_done, START + 3)
                    dve.wait_ge(total_in, START + DMA)
                    with dve.Fori(0, H - 1) as h:
                        head(h, h + 1)
                    head(H - 1, None)

        clear_spent()

        PIECES = T // 2
        RING = 4
        TILE_AT = (0, 1, 3, 4)
        with ExitStack() as s5:
            scaled = sb(s5, "scaled", [P, T, 2, D], F32R)
            xb = sb(s5, "xb", [P, T, D])
            bias_all = sb(s5, "bias_all", [P, D])
            root = sb(s5, "root", [P, T])
            dis = sb(s5, "dis", [P, T])
            dis_plain = sb(s5, "dis_plain", [P, T])
            dev_all, inv_all, shift_all = (sb(s5, f"{n}_all", [P, T]) for n in ("dev", "inv", "shift"))
            pieces = [sb(s5, f"pieces{n}", [P, 2, BANK]) for n in range(RING)]
            piece_high, piece_low = ([sb(s5, f"piece_{n}{b}", [P, 2, BANK], F32R) for b in range(RING)]
                                     for n in ("high", "low"))
            z, stats, mean_var, dev, inv, shift = (
                sb(s5, f"{n}3", [P, TPB, w])
                for n, w in (("z", D), ("stats", 6), ("mean_var", 2), ("dev", 1), ("inv", 1), ("shift", 1)))
            banks = s5.enter_context(nc.psum_tensor("banks", [P, 2, TPB, BANK], F32))
            proj = Projection(s5, "p3", [banks[:, 1, k, :] for k in range(2)],
                              [banks[:, 1, 2 + k, :] for k in range(2)], w3, 1)
            xb_in, bias_in, root_done, dis_done, dis_stored, dis_in, dev_all_done, inv_all_done, shift_all_done, \
                x2_stored, biased = (sem(s5, f"{n}3") for n in (
                    "xb_in", "bias_in", "root_done", "dis_done", "dis_stored", "dis_in", "dev_all_done",
                    "inv_all_done", "shift_all_done", "x2_stored", "biased"))
            tile_full = sem(s5, "tile_full")
            last_normed = sem(s5, "last_normed")
            x2_done = [sem(s5, f"x2_done{k}", started=False) for k in range(2)]
            pieces_in = sems(s5, "pieces_in", RING)
            high_done, low_done, used = (sems(s5, f"piece_{n}", RING) for n in ("high_done", "low_done", "used"))
            half_done, z_done, stats_done, var_done, dev_done, inv_done, shift_done, normed, out_stored = (
                sem(s5, f"{n}3") for n in ("half_done", "z_done", "stats_done", "var_done", "dev_done", "inv_done", "shift_done",
                                           "normed", "out_stored"))
            splits = lambda q, p: q * (PIECES // RING) + p // RING

            out_halves = out[(GROUPS - 1) * BANK:, :].rearrange("(h a p) d -> h p a d", h=2, p=P)

            with next_block() as block:
                @block.sync
                def _(sp):
                    start(sp, 0, 5)
                    proj.load_weight(sp)
                    sp.dma_start(bias_all[:], bias.partition_broadcast(P)).then_inc(bias_in, DMA)
                    adj_tiles = adj.rearrange("(a r c) n -> a r c n", a=2, c=C)

                    def load_piece(q, p):
                        a, c = 2 * p // C, 2 * p % C
                        sp.dma_start(pieces[p % RING][:], adj_tiles[a, :, c:c + 2, bass.ds(q * BANK, BANK)]).then_inc(
                            pieces_in[p % RING], DMA)

                    def reload_piece(q, p):
                        sp.wait_ge(low_done[p % RING], START + splits(q, p))
                        load_piece(q, p)

                    for p in range(RING):
                        load_piece(0, p)
                    sp.wait_ge(dis_done, START + 1)
                    sp.dma_start(dis_scratch.rearrange("(a r c) o -> r a (c o)", a=2, c=C),
                                 dis[:].rearrange("p (a c) -> p a c", a=2)).then_inc(dis_stored, DMA)
                    for k in range(2):
                        sp.wait_ge(x2_done[k], START + PAIRS)
                    sp.dma_start(x2_scratch.rearrange("(a r c) d -> r a (c d)", a=2, c=C),
                                 total[:].rearrange("p (a c) d -> p a (c d)", a=2)).then_inc(x2_stored, DMA)
                    for p in range(RING, PIECES):
                        reload_piece(0, p)
                    sp.wait_ge(x2_stored, START + DMA)
                    sp.dma_start(xb[:], x2_scratch.rearrange("(t p) d -> p t d", p=P)).then_inc(xb_in, DMA)
                    sp.wait_ge(dis_stored, START + DMA)
                    sp.dma_start(dis_plain[:].rearrange("p (t o) -> p t o", o=1), dis_scratch.rearrange(
                        "(t p) o -> p t o", p=P), allow_slow_non_contiguous=True).then_inc(dis_in, DMA)
                    with sp.Fori(1, GROUPS) as q:
                        for p in range(PIECES):
                            reload_piece(q, p)
                    sp.wait_ge(last_normed, START + TPB // 2)
                    sp.dma_start(out_halves[1], z[:, TPB // 2:, :]).then_inc(out_stored, DMA)

                @block.gpsimd
                def _(pool):
                    start(pool, 1, 5)
                    pool.wait_ge(xb_in, START + DMA)
                    pool.wait_ge(bias_in, START + DMA)
                    for t in range(T):
                        pool.tensor_tensor(xb[:, t, :], xb[:, t, :], bias_all[:], ALU.add).then_inc(biased, 1)

                @block.tensor
                def _(pe):
                    start(pe, 2, 5)
                    def turn(i, k):
                        pe.wait_ge(x2_done[k], START + i + 1)
                        proj.transposes(pe, i, k, total[:, 2 * i + k, :])

                    turn(0, 0)
                    turn(0, 1)
                    pe.wait_ge(proj.w_low_done, START + 1)
                    for i in range(PAIRS):
                        for k in range(2):
                            proj.products(pe, i, k)
                            if i + 1 < PAIRS:
                                turn(i + 1, k)
                    for k in range(2):
                        pe.wait_ge(proj.y_read[k], START + PAIRS)
                    with pe.Fori(0, GROUPS) as q:
                        for p in range(PIECES):
                            if p == 0:
                                pe.wait_ge(z_done, START + TPB * q)
                            pe.wait_ge(low_done[p % RING], START + splits(q, p) + 1)
                            for a in range(TPB):
                                bank = banks[:, bass.ds(q % 2, 1), a, :].rearrange("p o d -> p (o d)")
                                for e in range(2):
                                    cols = slice(a * P, (a + 1) * P)
                                    pe.matmul(bank, piece_high[p % RING][:, e, cols],
                                              scaled[:, 2 * p + e, :, :].rearrange("p s d -> p (s d)"),
                                              start=(p == 0 and e == 0), stop=False)
                                    mm = pe.matmul(bank[:, 0:D], piece_low[p % RING][:, e, cols],
                                                   scaled[:, 2 * p + e, 0, :], start=False,
                                                   stop=(p == PIECES - 1 and e == 1))
                                if p == PIECES - 1 and a < TPB - 1:
                                    mm.then_inc(tile_full, 1)
                            mm.then_inc(used[p % RING], 1)

                @block.scalar
                def _(act):
                    start(act, 3, 5)
                    act.sem_inc(x2_done[1], START)
                    act.activation(dev_all[:], mean_var_all[:, :, 1], ACT.Sqrt, bias=eps_col[:, 0:1]).then_inc(
                        dev_all_done, 1)
                    act.activation(root[:], degree[:], ACT.Sqrt).then_inc(root_done, 1)
                    proj.split_weight_high(act)

                    def scaled_high(i, k):
                        proj.y_high(act, i, k, part_of(scaled, 2 * i + k, 0), dis[:, bass.ds(2 * i + k, 1)])

                    def apply_norm(i):
                        t = 2 * i + 1
                        mine = total[:, bass.ds(t, 1), :].rearrange("p o d -> p (o d)")
                        act.activation(mine, mine, ACT.Identity, bias=shift_all[:, bass.ds(t, 1)],
                                       scale=inv_all[:, bass.ds(t, 1)]).then_inc(x2_done[1], 1)

                    act.wait_ge(shift_all_done, START + 1)
                    apply_norm(0)
                    proj.high(act, 0, 0)
                    apply_norm(1)
                    proj.high(act, 0, 1)
                    act.wait_ge(dis_done, START + 1)
                    apply_norm(2)
                    with act.Fori(0, PAIRS - 3) as i:
                        scaled_high(i, 0)
                        proj.high(act, i + 1, 0)
                        scaled_high(i, 1)
                        proj.high(act, i + 1, 1)
                        apply_norm(i + 3)
                    def high_part(q, p):
                        act.wait_ge(pieces_in[p % RING], START + DMA * (q * (PIECES // RING) + p // RING + 1))
                        act.wait_ge(used[p % RING], START + splits(q, p))
                        act.activation(piece_high[p % RING][:], pieces[p % RING][:], ACT.Copy).then_inc(
                            high_done[p % RING], 1)

                    def norm_root(q):
                        act.wait_ge(var_done, START + TPB * (q + 1))
                        act.activation(dev[:, :, 0], mean_var[:, :, 1], ACT.Sqrt, bias=eps_col[:, 0:1]).then_inc(
                            dev_done, 1)

                    def norm_apply(q):
                        act.wait_ge(shift_done, START + q + 1)
                        for a in range(TPB):
                            act.activation(z[:, a, :], z[:, a, :], ACT.Identity, bias=shift[:, a, :],
                                           scale=inv[:, a, :]).then_inc(normed, 1)
                        act.wait_ge(normed, START + TPB * (q + 1))
                        act.dma_start(out[bass.ds(q * BANK, BANK), :].rearrange("(a p) d -> p a d", p=P),
                                      z[:]).then_inc(out_stored, DMA)

                    for i in range(PAIRS - 3, PAIRS):
                        for k in range(2):
                            scaled_high(i, k)
                            if i + 1 < PAIRS:
                                proj.high(act, i + 1, k)
                        if i < PAIRS - 1:
                            high_part(0, i - (PAIRS - 3))
                    for p in range(2, PIECES):
                        high_part(0, p)
                    with act.Fori(1, GROUPS) as q:
                        for p in range(PIECES):
                            high_part(q, p)
                            if p == PIECES - 2:
                                norm_root(q - 1)
                            if p == PIECES - 1:
                                norm_apply(q - 1)
                    norm_root(GROUPS - 1)
                    act.wait_ge(shift_done, START + GROUPS)
                    for a in range(TPB // 2):
                        act.activation(z[:, a, :], z[:, a, :], ACT.Identity, bias=shift[:, a, :],
                                       scale=inv[:, a, :]).then_inc(normed, 1)
                    act.wait_ge(normed, START + TPB * (GROUPS - 1) + TPB // 2)
                    act.dma_start(out_halves[0], z[:, 0:TPB // 2, :]).then_inc(out_stored, DMA)
                    act.wait_ge(out_stored, START + DMA * (GROUPS + 1))

                @block.vector
                def _(dve):
                    start(dve, 4, 5)
                    dve.sem_inc(x2_done[0], START)
                    dve.sem_inc(z_done, TPB)
                    dve.wait_ge(dev_all_done, START + 1)
                    dve.reciprocal(inv_all[:], dev_all[:]).then_inc(inv_all_done, 1)
                    dve.wait_ge(inv_all_done, START + 1)
                    dve.scalar_tensor_tensor(out=shift_all[:], in0=mean_var_all[:, :, 0], scalar=-1.0, in1=inv_all[:],
                                             op0=ALU.mult, op1=ALU.mult).then_inc(shift_all_done, 1)
                    dve.wait_ge(shift_all_done, START + 1)

                    def apply_norm(i):
                        t = 2 * i
                        mine = total[:, bass.ds(t, 1), :].rearrange("p o d -> p (o d)")
                        dve.tensor_scalar(mine, mine, inv_all[:, bass.ds(t, 1)], shift_all[:, bass.ds(t, 1)], ALU.mult,
                                          ALU.add).then_inc(x2_done[0], 1)

                    def scaled_low(i, k):
                        t = 2 * i + k
                        proj.y_low(dve, i, k, part_of(scaled, t, 1), part_of(scaled, t, 0), dis[:, bass.ds(t, 1)])

                    apply_norm(0)
                    apply_norm(1)
                    dve.wait_ge(root_done, START + 1)
                    dve.reciprocal(dis[:], root[:]).then_inc(dis_done, 1)
                    proj.split_weight_low(dve)
                    proj.low(dve, 0, 0)
                    proj.low(dve, 0, 1)
                    dve.wait_ge(dis_done, START + 1)
                    apply_norm(2)
                    with dve.Fori(0, PAIRS - 3) as i:
                        scaled_low(i, 0)
                        proj.low(dve, i + 1, 0)
                        scaled_low(i, 1)
                        proj.low(dve, i + 1, 1)
                        apply_norm(i + 3)
                    def low_part(q, p):
                        dve.wait_ge(high_done[p % RING], START + splits(q, p) + 1)
                        dve.tensor_tensor(piece_low[p % RING][:], pieces[p % RING][:], plain(piece_high[p % RING][:]),
                                          ALU.subtract).then_inc(low_done[p % RING], 1)

                    def residual(q, a):
                        t = TPB * q + a
                        if a < TPB - 1:
                            dve.wait_ge(tile_full, START + (TPB - 1) * q + a + 1)
                        else:
                            dve.wait_ge(used[RING - 1], START + splits(q, PIECES))
                        if a == 0:
                            dve.wait_ge(biased, START + TPB * (q + 1))
                            dve.wait_ge(dis_in, START + DMA)
                            dve.wait_ge(out_stored, START + DMA * q)
                        bank = banks[:, bass.ds(q % 2, 1), a, :].rearrange("p o d -> p (o d)")
                        dve.scalar_tensor_tensor(out=z[:, a, :], in0=bank[:, D:2 * D],
                                                 scalar=dis_plain[:, bass.ds(t, 1)],
                                                 in1=xb[:, bass.ds(t, 1), :].rearrange("p o d -> p (o d)"),
                                                 op0=ALU.mult, op1=ALU.add).then_inc(half_done, 1)
                        dve.wait_ge(half_done, START + t + 1)
                        dve.scalar_tensor_tensor(out=z[:, a, :], in0=bank[:, 0:D], scalar=dis_plain[:, bass.ds(t, 1)],
                                                 in1=z[:, a, :], op0=ALU.mult, op1=ALU.add).then_inc(z_done, 1)
                        dve.wait_ge(z_done, START + TPB * (q + 1) + a + 1)
                        dve.bn_stats(stats[:, a, :], z[:, a, :]).then_inc(stats_done, 1)

                    def variance(a):
                        dve.bn_aggr(mean_var[:, a, :], stats[:, a, :]).then_inc(var_done, 1)

                    def scale_and_shift(q):
                        dve.wait_ge(dev_done, START + q + 1)
                        dve.reciprocal(inv[:, :, 0], dev[:, :, 0]).then_inc(inv_done, 1)
                        dve.wait_ge(inv_done, START + q + 1)
                        dve.scalar_tensor_tensor(out=shift[:, :, 0], in0=mean_var[:, :, 0], scalar=-1.0,
                                                 in1=inv[:, :, 0], op0=ALU.mult, op1=ALU.mult).then_inc(shift_done, 1)

                    for i in range(PAIRS - 3, PAIRS):
                        for k in range(2):
                            scaled_low(i, k)
                            if i + 1 < PAIRS:
                                proj.low(dve, i + 1, k)
                        if i < PAIRS - 1:
                            low_part(0, i - (PAIRS - 3))
                    for p in range(2, PIECES):
                        low_part(0, p)
                    with dve.Fori(1, GROUPS) as q:
                        for p in range(PIECES):
                            if p - 1 in TILE_AT:
                                dve.wait_ge(stats_done, START + TPB * (q - 1) + TILE_AT.index(p - 1) + 1)
                            low_part(q, p)
                            if p - 1 in TILE_AT:
                                variance(TILE_AT.index(p - 1))
                            if p in TILE_AT:
                                residual(q - 1, TILE_AT.index(p))
                            if p == PIECES - 2:
                                scale_and_shift(q - 1)
                    last = GROUPS - 1
                    for a in range(TPB):
                        residual(last, a)
                        if a > 0:
                            dve.wait_ge(stats_done, START + TPB * last + a)
                            variance(a - 1)
                    dve.wait_ge(stats_done, START + TPB * GROUPS)
                    variance(TPB - 1)
                    scale_and_shift(last)
                    dve.wait_ge(shift_done, START + GROUPS)
                    for a in range(TPB // 2, TPB):
                        dve.tensor_scalar(z[:, a, :], z[:, a, :], inv[:, a, :], shift[:, a, :], ALU.mult,
                                          ALU.add).then_inc(last_normed, 1)


_INS = ['x', 'adj', 'L0_gnn_t', 'L0_gnn_weight', 'L2_gnn_Wq', 'L2_gnn_Wk', 'L2_gnn_Wv', 'L2_gnn_Wout',
        'L3_gnn_weight', 'L3_gnn_bias']
_OUTS = [((2048, 256), 'float32')]


def kernel(**inputs):
    import numpy as _np
    import concourse.bacc as _bacc
    from concourse import mybir as _mybir
    from concourse.bass_utils import run_bass_kernel_spmd as _run

    nc = _bacc.Bacc("TRN2", target_bir_lowering=False, num_devices=1)
    arrays, args = {}, []
    for name in _INS:
        a = _np.ascontiguousarray(inputs[name])
        arrays[f"in_{name}_dram"] = a
        args.append(nc.dram_tensor(f"in_{name}_dram", a.shape, _mybir.dt.from_np(a.dtype), kind="ExternalInput").ap())
    for i, (shape, dtype) in enumerate(_OUTS):
        dt = _mybir.dt.from_np(_np.dtype(dtype))
        args.append(nc.dram_tensor(f"out_{i}_dram", shape, dt, kind="ExternalOutput").ap())
    graph_layers(nc, *args)
    r = _run(nc, [arrays], core_ids=[0])
    got = tuple(r.results[0][f"out_{i}_dram"] for i in range(len(_OUTS)))
    return got[0]
```
